# Optimizing a Trainium2 kernel written in Bass

```python
import numpy as np
import jax
import jax.numpy as jnp

def _softmax(x, axis=-1):
    return jax.nn.softmax(x, axis=axis)

def _gelu(x):
    return jax.nn.gelu(x, approximate=True)

def _silu(x):
    return jax.nn.silu(x)

def _sigmoid(x):
    return jax.nn.sigmoid(x)

def _layernorm(x, axis=-1, eps=1e-05):
    m = jnp.mean(x, axis=axis, keepdims=True)
    v = jnp.var(x, axis=axis, keepdims=True)
    return (x - m) / jnp.sqrt(v + eps)

def _scatter_add(tgt, idx, src, axis=0):
    return tgt.at[idx].add(src)

def _segment_sum(src, seg, n):
    return jax.ops.segment_sum(src, seg, n)
kernel_name = 'mk_recurrent_d2_jaxref_r8_5f2796'

def setup_inputs(seed: int=0):
    np.random.seed(seed)
    _w = jnp.asarray

    def _L0_attn_setup():
        import jax, jax.numpy as jnp
        import numpy as np
        B, T, DIM = (8, 512, 128)
        HEADS = 16
        WS = [10, 20]
        SHIFTS = [5, 10]
        DIM_IN = DIM // 2
        DIM_BR = DIM_IN // 2
        H_BR = HEADS // 2
        EPS = 1e-06

        def rmsnorm(x, w):
            return x * jax.lax.rsqrt(jnp.mean(x * x, axis=-1, keepdims=True) + EPS) * w

        def _branch(x, window, shift, qkv_w, qkv_b, pw, pb, rpb, heads):
            Bx, Tn, C = x.shape
            pad = -Tn % window
            xp = jnp.pad(x, ((0, 0), (0, pad), (0, 0)))
            Tp = Tn + pad
            nW = Tp // window
            hd = C // heads
            scale = hd ** (-0.5)
            if shift > 0:
                xp = jnp.roll(xp, -shift, axis=1)
                m = np.zeros(Tp, np.float32)
                m[Tp - window:Tp - shift] = 1.0
                m[Tp - shift:] = 2.0
                mw = m.reshape(nW, window)
                amask = jnp.asarray(np.where(mw[:, :, None] != mw[:, None, :], -100.0, 0.0).astype(np.float32))
            else:
                amask = None
            xw = xp.reshape(Bx, nW, window, C)
            qkv = (xw @ qkv_w + qkv_b).reshape(Bx, nW, window, 3, heads, hd)
            q, k, v = (qkv[:, :, :, 0], qkv[:, :, :, 1], qkv[:, :, :, 2])
            attn = jnp.einsum('bnqhd,bnkhd->bnhqk', q * scale, k)
            coords = np.arange(window)
            ridx = coords[:, None] - coords[None, :] + window - 1
            bias = jnp.transpose(rpb[ridx], (2, 0, 1))
            attn = attn + bias[None, None]
            if amask is not None:
                attn = attn + amask[None, :, None]
            attn = jax.nn.softmax(attn, axis=-1)
            out = jnp.einsum('bnhqk,bnkhd->bnqhd', attn, v).reshape(Bx, nW, window, C)
            out = out @ pw + pb
            out = out.reshape(Bx, Tp, C)
            if shift > 0:
                out = jnp.roll(out, shift, axis=1)
            return out[:, :Tn]
        key = jax.random.key(seed)
        ks = jax.random.split(key, 12)
        w = lambda k, s: (jax.random.normal(k, s) * 0.02).astype(jnp.float32)
        z = lambda n: jnp.zeros((n,), jnp.float32)
        return {'x': jax.random.normal(ks[0], (B, T, DIM), jnp.float32), 'down_w': w(ks[1], (DIM, DIM_IN)), 'down_b': z(DIM_IN), 'up_w': w(ks[2], (DIM_IN, DIM)), 'up_b': z(DIM), 'norm1_w': jnp.ones((DIM_IN,), jnp.float32), 'norm2_w': jnp.ones((DIM,), jnp.float32), 'qkv1_w': w(ks[3], (DIM_BR, 3 * DIM_BR)), 'qkv1_b': z(3 * DIM_BR), 'proj1_w': w(ks[4], (DIM_BR, DIM_BR)), 'proj1_b': z(DIM_BR), 'rpb1': w(ks[5], (2 * WS[0] - 1, H_BR)), 'qkv2_w': w(ks[6], (DIM_BR, 3 * DIM_BR)), 'qkv2_b': z(3 * DIM_BR), 'proj2_w': w(ks[7], (DIM_BR, DIM_BR)), 'proj2_b': z(DIM_BR), 'rpb2': w(ks[8], (2 * WS[1] - 1, H_BR)), 'ffn_w1': w(ks[9], (DIM, 2 * DIM)), 'ffn_b1': z(2 * DIM), 'ffn_w2': w(ks[10], (2 * DIM, DIM)), 'ffn_b2': z(DIM)}
    _L0_attn_in = _L0_attn_setup()

    def _L0_ffn_setup():
        import jax, jax.numpy as jnp
        import numpy as np
        E = 8
        TOP_K = 2
        ROUTE_SCALE = 1.0
        ALPHA = 1.702
        LIMIT = 7.0
        D = 128
        F = 128
        B, S = (2, 128)

        def swiglu(h):
            g = jnp.minimum(h[..., ::2], LIMIT)
            l = jnp.clip(h[..., 1::2], -LIMIT, LIMIT)
            return g * jax.nn.sigmoid(ALPHA * g) * (l + 1.0)
        if __name__ == '__main__':
            out = reference(**setup_inputs())
            print(out.shape, out.dtype)
        key = jax.random.key(seed)
        ks = jax.random.split(key, 16)
        sd = 1.0 / np.sqrt(D)
        sf = 1.0 / np.sqrt(F)
        return {'x': jax.random.normal(ks[0], (B, S, D), jnp.float32), 'gate_w': jax.random.normal(ks[1], (E, D), jnp.float32) * sd, 'gate_b': jax.random.normal(ks[2], (E,), jnp.float32) * 0.01, 'w1': jax.random.normal(ks[3], (E, 2 * F, D), jnp.float32) * sd, 'b1': jax.random.normal(ks[4], (E, 2 * F), jnp.float32) * 0.01, 'w3': jax.random.normal(ks[5], (E, 2 * F, D), jnp.float32) * sd, 'b3': jax.random.normal(ks[6], (E, 2 * F), jnp.float32) * 0.01, 'w2': jax.random.normal(ks[7], (E, D, F), jnp.float32) * sf, 'b2': jax.random.normal(ks[8], (E, D), jnp.float32) * 0.01, 'sw1': jax.random.normal(ks[9], (2 * F, D), jnp.float32) * sd, 'sb1': jax.random.normal(ks[10], (2 * F,), jnp.float32) * 0.01, 'sw3': jax.random.normal(ks[11], (2 * F, D), jnp.float32) * sd, 'sb3': jax.random.normal(ks[12], (2 * F,), jnp.float32) * 0.01, 'sw2': jax.random.normal(ks[13], (D, F), jnp.float32) * sf, 'sb2': jax.random.normal(ks[14], (D,), jnp.float32) * 0.01}
    _L0_ffn_in = _L0_ffn_setup()

    def _L1_attn_setup():
        import math
        import jax, jax.numpy as jnp
        import numpy as np
        B, S, DIM, HEADS = (1, 256, 128, 16)
        HEAD_DIM = DIM // HEADS
        key = jax.random.key(seed)
        ks = jax.random.split(key, 6)
        scale = DIM ** (-0.5)
        x = jax.random.normal(ks[0], (B, S, DIM), jnp.float32)
        wq = jax.random.normal(ks[1], (DIM, DIM), jnp.float32) * scale
        wk = jax.random.normal(ks[2], (DIM, DIM), jnp.float32) * scale
        wv = jax.random.normal(ks[3], (DIM, DIM), jnp.float32) * scale
        wo = jax.random.normal(ks[4], (DIM, DIM), jnp.float32) * scale
        pope_bias = -jax.random.uniform(ks[5], (HEADS, HEAD_DIM), jnp.float32) * 3.0
        return {'x': x, 'wq': wq, 'wk': wk, 'wv': wv, 'wo': wo, 'pope_bias': pope_bias}
    _L1_attn_in = _L1_attn_setup()

    def _L1_ffn_setup():
        import jax, jax.numpy as jnp
        import numpy as np
        HIDDEN = 128
        FFN = 352
        N_EXPERTS = 8
        TOP_K = 2
        EPS = 1e-05
        B, S = (2, 256)

        def _rms_norm(x, weight, eps):
            var = jnp.mean(jnp.square(x), axis=-1, keepdims=True)
            return x * jax.lax.rsqrt(var + eps) * weight
        key = jax.random.key(seed)
        ks = jax.random.split(key, 5)
        scale = 0.02
        return {'hidden_states': jax.random.normal(ks[0], (B, S, HIDDEN), dtype=jnp.float32), 'ln_weight': jnp.ones((HIDDEN,), dtype=jnp.float32), 'router_w': jax.random.normal(ks[1], (HIDDEN, N_EXPERTS), dtype=jnp.float32) * scale, 'w1': jax.random.normal(ks[2], (N_EXPERTS, HIDDEN, FFN), dtype=jnp.float32) * scale, 'w3': jax.random.normal(ks[3], (N_EXPERTS, HIDDEN, FFN), dtype=jnp.float32) * scale, 'w2': jax.random.normal(ks[4], (N_EXPERTS, FFN, HIDDEN), dtype=jnp.float32) * scale}
    _L1_ffn_in = _L1_ffn_setup()
    _d = {'L0_attn_x': _L0_attn_in['x'], 'L0_attn_down_w': _L0_attn_in['down_w'], 'L0_attn_down_b': _L0_attn_in['down_b'], 'L0_attn_up_w': _L0_attn_in['up_w'], 'L0_attn_up_b': _L0_attn_in['up_b'], 'L0_attn_norm1_w': _L0_attn_in['norm1_w'], 'L0_attn_norm2_w': _L0_attn_in['norm2_w'], 'L0_attn_qkv1_w': _L0_attn_in['qkv1_w'], 'L0_attn_qkv1_b': _L0_attn_in['qkv1_b'], 'L0_attn_proj1_w': _L0_attn_in['proj1_w'], 'L0_attn_proj1_b': _L0_attn_in['proj1_b'], 'L0_attn_rpb1': _L0_attn_in['rpb1'], 'L0_attn_qkv2_w': _L0_attn_in['qkv2_w'], 'L0_attn_qkv2_b': _L0_attn_in['qkv2_b'], 'L0_attn_proj2_w': _L0_attn_in['proj2_w'], 'L0_attn_proj2_b': _L0_attn_in['proj2_b'], 'L0_attn_rpb2': _L0_attn_in['rpb2'], 'L0_attn_ffn_w1': _L0_attn_in['ffn_w1'], 'L0_attn_ffn_b1': _L0_attn_in['ffn_b1'], 'L0_attn_ffn_w2': _L0_attn_in['ffn_w2'], 'L0_attn_ffn_b2': _L0_attn_in['ffn_b2'], 'L0_ffn_gate_w': _L0_ffn_in['gate_w'], 'L0_ffn_gate_b': _L0_ffn_in['gate_b'], 'L0_ffn_w1': _L0_ffn_in['w1'], 'L0_ffn_b1': _L0_ffn_in['b1'], 'L0_ffn_w3': _L0_ffn_in['w3'], 'L0_ffn_b3': _L0_ffn_in['b3'], 'L0_ffn_w2': _L0_ffn_in['w2'], 'L0_ffn_b2': _L0_ffn_in['b2'], 'L0_ffn_sw1': _L0_ffn_in['sw1'], 'L0_ffn_sb1': _L0_ffn_in['sb1'], 'L0_ffn_sw3': _L0_ffn_in['sw3'], 'L0_ffn_sb3': _L0_ffn_in['sb3'], 'L0_ffn_sw2': _L0_ffn_in['sw2'], 'L0_ffn_sb2': _L0_ffn_in['sb2'], 'L1_attn_wq': _L1_attn_in['wq'], 'L1_attn_wk': _L1_attn_in['wk'], 'L1_attn_wv': _L1_attn_in['wv'], 'L1_attn_wo': _L1_attn_in['wo'], 'L1_attn_pope_bias': _L1_attn_in['pope_bias'], 'L1_ffn_ln_weight': _L1_ffn_in['ln_weight'], 'L1_ffn_router_w': _L1_ffn_in['router_w'], 'L1_ffn_w1': _L1_ffn_in['w1'], 'L1_ffn_w3': _L1_ffn_in['w3'], 'L1_ffn_w2': _L1_ffn_in['w2']}
    _x0 = _d['L0_attn_x']
    _d['L0_attn_x'] = jax.random.normal(jax.random.fold_in(jax.random.key(seed), 1), (8, 512, 128), dtype=_x0.dtype)
    del _x0
    return _d

def reference(L0_attn_x, L0_attn_down_w, L0_attn_down_b, L0_attn_up_w, L0_attn_up_b, L0_attn_norm1_w, L0_attn_norm2_w, L0_attn_qkv1_w, L0_attn_qkv1_b, L0_attn_proj1_w, L0_attn_proj1_b, L0_attn_rpb1, L0_attn_qkv2_w, L0_attn_qkv2_b, L0_attn_proj2_w, L0_attn_proj2_b, L0_attn_rpb2, L0_attn_ffn_w1, L0_attn_ffn_b1, L0_attn_ffn_w2, L0_attn_ffn_b2, L0_ffn_gate_w, L0_ffn_gate_b, L0_ffn_w1, L0_ffn_b1, L0_ffn_w3, L0_ffn_b3, L0_ffn_w2, L0_ffn_b2, L0_ffn_sw1, L0_ffn_sb1, L0_ffn_sw3, L0_ffn_sb3, L0_ffn_sw2, L0_ffn_sb2, L1_attn_wq, L1_attn_wk, L1_attn_wv, L1_attn_wo, L1_attn_pope_bias, L1_ffn_ln_weight, L1_ffn_router_w, L1_ffn_w1, L1_ffn_w3, L1_ffn_w2):

    def _L0_attn_ref(x, down_w, down_b, up_w, up_b, norm1_w, norm2_w, qkv1_w, qkv1_b, proj1_w, proj1_b, rpb1, qkv2_w, qkv2_b, proj2_w, proj2_b, rpb2, ffn_w1, ffn_b1, ffn_w2, ffn_b2):
        import jax, jax.numpy as jnp
        import numpy as np
        B, T, DIM = (8, 512, 128)
        HEADS = 16
        WS = [10, 20]
        SHIFTS = [5, 10]
        DIM_IN = DIM // 2
        DIM_BR = DIM_IN // 2
        H_BR = HEADS // 2
        EPS = 1e-06

        def rmsnorm(x, w):
            return x * jax.lax.rsqrt(jnp.mean(x * x, axis=-1, keepdims=True) + EPS) * w

        def _branch(x, window, shift, qkv_w, qkv_b, pw, pb, rpb, heads):
            Bx, Tn, C = x.shape
            pad = -Tn % window
            xp = jnp.pad(x, ((0, 0), (0, pad), (0, 0)))
            Tp = Tn + pad
            nW = Tp // window
            hd = C // heads
            scale = hd ** (-0.5)
            if shift > 0:
                xp = jnp.roll(xp, -shift, axis=1)
                m = np.zeros(Tp, np.float32)
                m[Tp - window:Tp - shift] = 1.0
                m[Tp - shift:] = 2.0
                mw = m.reshape(nW, window)
                amask = jnp.asarray(np.where(mw[:, :, None] != mw[:, None, :], -100.0, 0.0).astype(np.float32))
            else:
                amask = None
            xw = xp.reshape(Bx, nW, window, C)
            qkv = (xw @ qkv_w + qkv_b).reshape(Bx, nW, window, 3, heads, hd)
            q, k, v = (qkv[:, :, :, 0], qkv[:, :, :, 1], qkv[:, :, :, 2])
            attn = jnp.einsum('bnqhd,bnkhd->bnhqk', q * scale, k)
            coords = np.arange(window)
            ridx = coords[:, None] - coords[None, :] + window - 1
            bias = jnp.transpose(rpb[ridx], (2, 0, 1))
            attn = attn + bias[None, None]
            if amask is not None:
                attn = attn + amask[None, :, None]
            attn = jax.nn.softmax(attn, axis=-1)
            out = jnp.einsum('bnhqk,bnkhd->bnqhd', attn, v).reshape(Bx, nW, window, C)
            out = out @ pw + pb
            out = out.reshape(Bx, Tp, C)
            if shift > 0:
                out = jnp.roll(out, shift, axis=1)
            return out[:, :Tn]
        residual = x
        xi = rmsnorm(x @ down_w + down_b, norm1_w)
        x1, x2 = (xi[..., :DIM_BR], xi[..., DIM_BR:])
        o1 = _branch(x1, WS[0], SHIFTS[0], qkv1_w, qkv1_b, proj1_w, proj1_b, rpb1, H_BR)
        o2 = _branch(x2, WS[1], SHIFTS[1], qkv2_w, qkv2_b, proj2_w, proj2_b, rpb2, H_BR)
        xc = jnp.concatenate([o1, o2], axis=-1) @ up_w + up_b
        x = residual + xc
        h = rmsnorm(x, norm2_w)
        ffn = jax.nn.gelu(h @ ffn_w1 + ffn_b1, approximate=False) @ ffn_w2 + ffn_b2
        return x + ffn

    def _L0_ffn_ref(x, gate_w, gate_b, w1, b1, w3, b3, w2, b2, sw1, sb1, sw3, sb3, sw2, sb2):
        import jax, jax.numpy as jnp
        import numpy as np
        E = 8
        TOP_K = 2
        ROUTE_SCALE = 1.0
        ALPHA = 1.702
        LIMIT = 7.0
        D = 128
        F = 128
        B, S = (2, 128)

        def swiglu(h):
            g = jnp.minimum(h[..., ::2], LIMIT)
            l = jnp.clip(h[..., 1::2], -LIMIT, LIMIT)
            return g * jax.nn.sigmoid(ALPHA * g) * (l + 1.0)
        if __name__ == '__main__':
            out = reference(**setup_inputs())
            print(out.shape, out.dtype)
        inp_shape = x.shape
        xt = x.reshape(-1, D)
        logits = xt @ gate_w.T
        scores = jax.nn.softmax(logits.astype(jnp.float32), axis=-1)
        biased = scores + gate_b.astype(jnp.float32)
        idx = jax.lax.top_k(biased, TOP_K)[1]
        weights = (jnp.take_along_axis(scores, idx, axis=-1) * ROUTE_SCALE).astype(x.dtype)
        cw = jnp.sum(jax.nn.one_hot(idx, E, dtype=x.dtype) * weights[..., None], axis=1)
        h1 = jnp.einsum('td,efd->etf', xt, w1) + b1[:, None, :]
        h3 = jnp.einsum('td,efd->etf', xt, w3) + b3[:, None, :]
        a = swiglu(h1 * h3)
        y = jnp.einsum('etf,edf->etd', a, w2) + b2[:, None, :]
        routed = jnp.einsum('te,etd->td', cw, y)
        sh = swiglu((xt @ sw1.T + sb1) * (xt @ sw3.T + sb3))
        shared = sh @ sw2.T + sb2
        return (routed + shared).reshape(inp_shape)

    def _L1_attn_ref(x, wq, wk, wv, wo, pope_bias):
        import math
        import jax, jax.numpy as jnp
        import numpy as np
        B, S, DIM, HEADS = (1, 256, 128, 16)
        HEAD_DIM = DIM // HEADS
        B_, S_, C = x.shape
        H = HEADS
        D = C // H
        q = jnp.einsum('bsc,oc->bso', x, wq).reshape(B_, S_, H, D).transpose(0, 2, 1, 3)
        k = jnp.einsum('bsc,oc->bso', x, wk).reshape(B_, S_, H, D).transpose(0, 2, 1, 3)
        v = jnp.einsum('bsc,oc->bso', x, wv).reshape(B_, S_, H, D).transpose(0, 2, 1, 3)
        inv_freqs = 10000.0 ** (-(jnp.arange(D, dtype=jnp.float32) / D))
        pos = jnp.arange(S_, dtype=jnp.float32)
        freqs = pos[:, None] * inv_freqs[None, :]
        bias = jnp.clip(pope_bias, -2.0 * math.pi, 0.0)
        freqs_with_bias = freqs[None, :, :] + bias[:, None, :]
        q_mag = jax.nn.softplus(q)
        k_mag = jax.nn.softplus(k)
        qp = freqs[None, None, :, :]
        kp = freqs_with_bias[None, :, :, :]
        q_embed = jnp.stack([q_mag * jnp.cos(qp), q_mag * jnp.sin(qp)], axis=-1).reshape(B_, H, S_, 2 * D)
        k_embed = jnp.stack([k_mag * jnp.cos(kp), k_mag * jnp.sin(kp)], axis=-1).reshape(B_, H, S_, 2 * D)
        scores = jnp.einsum('bhsd,bhtd->bhst', q_embed, k_embed) / D ** 0.5
        attn = jax.nn.softmax(scores, axis=-1)
        out = jnp.einsum('bhst,bhtd->bhsd', attn, v)
        out = out.transpose(0, 2, 1, 3).reshape(B_, S_, C)
        return jnp.einsum('bsc,oc->bso', out, wo)

    def _L1_ffn_ref(hidden_states, ln_weight, router_w, w1, w3, w2):
        import jax, jax.numpy as jnp
        import numpy as np
        HIDDEN = 128
        FFN = 352
        N_EXPERTS = 8
        TOP_K = 2
        EPS = 1e-05
        B, S = (2, 256)

        def _rms_norm(x, weight, eps):
            var = jnp.mean(jnp.square(x), axis=-1, keepdims=True)
            return x * jax.lax.rsqrt(var + eps) * weight
        b, s, h = hidden_states.shape
        x = _rms_norm(hidden_states, ln_weight, EPS).reshape(b * s, h)
        logits = x @ router_w
        probs = jax.nn.softmax(logits, axis=-1)
        top_p, top_i = jax.lax.top_k(probs, TOP_K)
        gates = jnp.sum(jax.nn.one_hot(top_i, N_EXPERTS, dtype=x.dtype) * top_p[..., None], axis=1)
        h1 = jnp.einsum('td,edf->tef', x, w1)
        h3 = jnp.einsum('td,edf->tef', x, w3)
        act = jax.nn.silu(h1) * h3
        y = jnp.einsum('tef,efd->ted', act, w2)
        out = jnp.einsum('te,ted->td', gates, y)
        return out.reshape(b, s, h)
    x = L0_attn_x
    xn = _layernorm(x, axis=-1)
    s = _L0_attn_ref(xn, L0_attn_down_w, L0_attn_down_b, L0_attn_up_w, L0_attn_up_b, L0_attn_norm1_w, L0_attn_norm2_w, L0_attn_qkv1_w, L0_attn_qkv1_b, L0_attn_proj1_w, L0_attn_proj1_b, L0_attn_rpb1, L0_attn_qkv2_w, L0_attn_qkv2_b, L0_attn_proj2_w, L0_attn_proj2_b, L0_attn_rpb2, L0_attn_ffn_w1, L0_attn_ffn_b1, L0_attn_ffn_w2, L0_attn_ffn_b2)
    g = _silu(_L0_ffn_ref(xn, L0_ffn_gate_w, L0_ffn_gate_b, L0_ffn_w1, L0_ffn_b1, L0_ffn_w3, L0_ffn_b3, L0_ffn_w2, L0_ffn_b2, L0_ffn_sw1, L0_ffn_sb1, L0_ffn_sw3, L0_ffn_sb3, L0_ffn_sw2, L0_ffn_sb2))
    x = x + s * g
    xn = _layernorm(x, axis=-1)
    s = _L1_attn_ref(xn, L1_attn_wq, L1_attn_wk, L1_attn_wv, L1_attn_wo, L1_attn_pope_bias)
    g = _silu(_L1_ffn_ref(xn, L1_ffn_ln_weight, L1_ffn_router_w, L1_ffn_w1, L1_ffn_w3, L1_ffn_w2))
    x = x + s * g
    return x

_drawn_inputs = setup_inputs


def setup_inputs(seed=0):
    import zlib

    import numpy as np

    out = dict(_drawn_inputs(seed))
    spreads = {'L0_attn_down_b': (0.0, 0.8),
     'L0_attn_up_b': (0.0, 0.1),
     'L0_attn_norm1_w': (1.0, 0.6),
     'L0_attn_norm2_w': (1.0, 0.6),
     'L0_attn_qkv1_b': (0.0, 0.8),
     'L0_attn_proj1_b': (0.0, 0.8),
     'L0_attn_qkv2_b': (0.0, 0.8),
     'L0_attn_proj2_b': (0.0, 0.8),
     'L0_attn_ffn_b1': (0.0, 0.8),
     'L0_attn_ffn_b2': (0.0, 0.1),
     'L1_ffn_ln_weight': (1.0, 0.6)}
    factors = {'L0_attn_down_w': 8.0,
     'L0_attn_up_w': 7.712,
     'L0_attn_qkv1_w': 8.0,
     'L0_attn_proj1_w': 8.0,
     'L0_attn_rpb1': 8.0,
     'L0_attn_qkv2_w': 8.0,
     'L0_attn_proj2_w': 8.0,
     'L0_attn_rpb2': 8.0,
     'L0_attn_ffn_w1': 3.063,
     'L0_attn_ffn_w2': 2.763,
     'L0_ffn_b1': 8.0,
     'L0_ffn_b3': 8.0,
     'L0_ffn_b2': 8.0,
     'L0_ffn_sb1': 8.0,
     'L0_ffn_sb3': 8.0,
     'L0_ffn_sb2': 8.0,
     'L1_attn_wq': 8.0,
     'L1_attn_wk': 8.0,
     'L1_attn_wv': 8.0,
     'L1_attn_wo': 8.0,
     'L1_attn_pope_bias': 8.0,
     'L1_ffn_router_w': 8.0,
     'L1_ffn_w1': 8.0,
     'L1_ffn_w3': 8.0,
     'L1_ffn_w2': 8.0}
    for name, (base, spread) in spreads.items():
        noise = np.random.default_rng([zlib.crc32(name.encode()), seed]).standard_normal(out[name].shape)
        drawn = base * np.exp(spread * noise) if base else spread * noise
        out[name] = jnp.asarray(drawn.astype(out[name].dtype))
    for name, factor in factors.items():
        out[name] = (out[name] * factor).astype(out[name].dtype)
    return out
```

```python
from contextlib import ExitStack

import numpy as np
import concourse.bass as bass
from concourse import mybir

F32 = mybir.dt.float32
F32R = mybir.dt.float32r
ALU = mybir.AluOpType
ACT = mybir.ActivationFunctionType
AX = mybir.AxisListType

B, T, D = 8, 512, 128
NT = T // 128
E = 8
WIN = (10, 20)
SHIFT = (5, 10)
NWIN = (13, 7)
GRP = (WIN[0] * NWIN[0], WIN[1] * NWIN[1])
PADT = 520
XIT_W = SHIFT[1] + 4 * GRP[1]
CHUNKS = [(0, 0, 5), (0, 5, 5), (0, 10, 3)] + [(1, w, 1) for w in range(NWIN[1])]
CHUNK_AT = {2: (0, 3), 3: (3, 7), 4: (7, 10)}
S_AT = (0, NWIN[0] * WIN[0] ** 2)
S_W = S_AT[1] + NWIN[1] * WIN[1] ** 2
H1, HD1 = 16, 8
FF = 352
FCH = [(0, 128), (128, 128), (256, 96)]
NCH = len(FCH)
STEPS = 83
SMALL = 51
SETUP_H, SETUP_V, SETUP_P, SETUP_A = 7, 16, 41, 4
SROWS = 48
LIMIT, ALPHA = 7.0, 1.702

COUNTED = {
    "TensorE":
        "tp down logits gpair lpair y qkv cwt S proj up ffn1 ffn2 qk v fpair mpair y1 mt st pv wo",
    "ScalarE":
        "evac lexp h3g h3l th qkv_sb cwT wexp ppT sqs gelu qabs qexp qln v_sb fth ex silu",
    "GpSimd":
        "rstd gg lc wsub wpv xb emb_sin pstep",
    "VectorE":
        "stats xn xi_sq xi lsub cw gused lused a acc prod S_sb wmax wsum wout x1 h s0 layer0 xrh mag "
        "emb_cos hi lo mx m2 fused acc1 ot out step",
    "DMA":
        "stacked max_stacked",
    "all":
        "arrived",
}


def build(nc, A):
    ctx = ExitStack()
    with ctx:
        def sb(name, shape, dt=F32):
            return ctx.enter_context(nc.sbuf_tensor(name, shape, dt))

        sem = {n: ctx.enter_context(nc.semaphore(n)) for n in " ".join(COUNTED.values()).split()}
        numbers = sorted(s.num for s in sem.values())
        counted = range(numbers[0], numbers[-1] + 1)
        assert len(counted) == len(numbers)
        released = ctx.enter_context(nc.semaphore("released"))
        seen = ctx.enter_context(nc.semaphore("seen"))
        x_loaded = ctx.enter_context(nc.semaphore("x_loaded"))
        small_loaded = ctx.enter_context(nc.semaphore("small_loaded"))
        moe_loaded = ctx.enter_context(nc.semaphore("moe_loaded"))
        stage_loaded = ctx.enter_context(nc.semaphore("stage_loaded"))
        zeroed = ctx.enter_context(nc.semaphore("zeroed"))
        setup = ctx.enter_context(nc.semaphore("setup"))
        setup_pool = ctx.enter_context(nc.semaphore("setup_pool"))
        setup_act = ctx.enter_context(nc.semaphore("setup_act"))
        stacked, max_stacked, arrived = sem["stacked"], sem["max_stacked"], sem["arrived"]
        stored = ctx.enter_context(nc.semaphore("stored"))

        IDENT = sb("IDENT", [128, 128])
        HEADSUM = sb("HEADSUM", [128, 128])
        REV = sb("REV", [128, E])
        NHALF = sb("NHALF", [128, NT])
        DOWN = sb("DOWN", [128, 64])
        DOWNB = sb("DOWNB", [128, 64])
        N1W = sb("N1W", [64, 1])
        N2W = sb("N2W", [128, 1])
        WQKV = sb("WQKV", [64, 2, 96])
        QKVB = sb("QKVB", [128, 2, 3])
        PROJ = sb("PROJ", [128, 2, 4, 32])
        PROJB = sb("PROJB", [64, 1])
        UPW = sb("UPW", [64, 128])
        UPB = sb("UPB", [128, 128])
        RPB = [sb(f"RPB{r}", [128, 2 * WIN[r] - 1]) for r in range(2)]
        BIAS = [sb(f"BIAS{r}", [128, WIN[r], WIN[r]]) for r in range(2)]
        MASK = [sb(f"MASK{r}", [128, WIN[r], WIN[r]]) for r in range(2)]
        FW1 = sb("FW1", [128, 256])
        FB1 = sb("FB1", [128, 2])
        FW2 = sb("FW2", [128, 2, 128])
        FB2 = sb("FB2", [128, 128])
        GATEW = sb("GATEW", [128, E])
        GATEB = sb("GATEB", [128, E])
        W0 = sb("W0", [128, E + 1, 4, 128])
        B0 = sb("B0", [128, E + 1, 4])
        W0D = sb("W0D", [128, E + 1, 128])
        B0D = sb("B0D", [E, 128])
        SB0D = sb("SB0D", [128, 128])
        WATT = sb("WATT", [128, 4, 128])
        POPEB = sb("POPEB", [128, 1])
        TRIG = sb("TRIG", [128, 4, T])
        PB = sb("PB", [128, 6])
        LNW = sb("LNW", [128, 1])
        ROUTW = sb("ROUTW", [128, E])
        W1H = sb("W1H", [128, E, 2, FF], F32R)
        W1L = sb("W1L", [128, E, 2, FF], F32R)
        W1D = sb("W1D", [128, E, NCH, 128])

        XIN = sb("XIN", [128, NT, 128])
        STAT = sb("STAT", [128, NT, 6])
        MV = sb("MV", [128, NT, 2])
        VAR = sb("VAR", [128, NT])
        RSTD = sb("RSTD", [128, NT])
        SQ = sb("SQ", [128, NT])
        XN = sb("XN", [128, NT, 128])
        XNT = sb("XNT", [128, T])
        XI = sb("XI", [128, NT, 64])
        XIT = sb("XIT", [64, XIT_W])
        QKV = [sb(f"QKV{r}", [128, 3, GRP[r]]) for r in range(2)]
        SC = sb("SC", [128, 4100])
        WM = [sb(f"WM{r}", [128, GRP[r]]) for r in range(2)]
        WO = [sb(f"WO{r}", [128, GRP[r]]) for r in range(2)]
        X1 = sb("X1", [128, NT, 128])
        H = sb("H", [128, NT, 128])
        HT = sb("HT", [128, T])
        G = sb("G", [128, 2, 512])
        S0 = sb("S0", [128, NT, 128])
        RT = sb("RT", [128, 8, NT, E])
        RS = sb("RS", [128, 6, NT])
        CW = sb("CW", [128, NT, E])
        UL = sb("UL", [128, 2, 2, 512])
        TH = sb("TH", [128, 2, 512])
        A4 = sb("A4", [128, 4, 512])
        ACC = sb("ACC", [128, NT, 128])
        XRH = sb("XRH", [128, T], F32R)
        XRL = sb("XRL", [128, T], F32R)
        QS = sb("QS", [128, 8, T], F32R)
        KS = sb("KS", [128, 8, T], F32R)
        V = sb("V", [128, NT, H1, HD1 + 1])
        MX = sb("MX", [128, NT, H1])
        DEN = sb("DEN", [128, 2, 32])
        PS = ctx.enter_context(nc.psum_tensor("PS", [128, 8, 512], F32))

        AA, H3 = A4[:, 0:2, :], A4[:, 2:4, :]
        PPT = HT[0:64, :]
        CWT = XN[0:E].rearrange("p t f -> p (t f)")
        XA = XN
        EH = SC[:, 0:4 * T].rearrange("p (c n) -> p c n", c=4)
        M2 = G[0:H1]
        EF = UL[:].rearrange("p a b n -> p (a b) n")
        P = SC[:, 0:4096].rearrange("p (s k n) -> p s k n", s=2, k=NT)
        STAGE = SC[:, 0:4 * 2 * FF].rearrange("p (e b f) -> p e b f", e=4, b=2)
        ntok = lambda ap: ap.rearrange("p (t f) -> p t f", t=NT)

        def bc(ap, shape, axis):
            return ap.unsqueeze(axis).to_broadcast(shape)

        def obank(h):
            return PS[:, 7 if h < 8 else 6, 0:288].rearrange("p (h t d) -> p h t d", h=8, t=NT)

        def end_pass(eng, i):
            eng.wait_ge(sem["out"], 1)
            eng.sem_inc(arrived, 1)
            eng.wait_ge(released, i + 1)

        block = ctx.enter_context(nc.Block())

        @block.sync
        def _(sp):
            x_t = A["x"].rearrange("(b t p) d -> b p t d", b=B, t=NT)
            y_t = A["y"].rearrange("(b t p) d -> b p t d", b=B, t=NT)
            sp.sem_inc(stored, 16)
            sp.dma_start(XIN[:], x_t[0]).then_inc(x_loaded, 16)
            n = [0]

            def small(dst, src):
                sp.dma_start(dst, src).then_inc(small_loaded, 16)
                n[0] += 1

            small(IDENT[:], A["ident"])
            small(HEADSUM[:], A["headsum"])
            small(REV[:], A["rev"])
            small(DOWN[:], A["down_w"])
            small(DOWNB[:], A["down_b"].partition_broadcast(128))
            small(N1W[:], A["norm1_w"])
            small(N2W[:], A["norm2_w"])
            small(UPW[:], A["up_w"])
            small(UPB[:], A["up_b"].partition_broadcast(128))
            sp.wait_ge(zeroed, 2)
            for r in range(2):
                small(WQKV[32 * r:32 * r + 32, r, :], A[f"qkv{r + 1}_w"])
                small(PROJB[32 * r:32 * r + 32, :], A[f"proj{r + 1}_b"])
                for g in range(4):
                    rows = slice(32 * g, 32 * g + 32)
                    small(QKVB[rows, r, :], A[f"qkv{r + 1}_b"])
                    small(PROJ[rows, r, g, :], A[f"proj{r + 1}_w"])
                    small(RPB[r][rows, :], A[f"rpb{r + 1}"])
            small(FW1[:], A["ffn_w1"])
            small(FB1[:], A["ffn_b1"])
            small(FW2[:], A["ffn_w2"].rearrange("(c p) d -> p c d", c=2))
            small(FB2[:], A["ffn_b2"].partition_broadcast(128))
            small(GATEW[:], A["gate_w"])
            small(GATEB[:], A["gate_b"].partition_broadcast(128))
            small(B0[:], A["b0"])
            small(B0D[:], A["b2"])
            small(SB0D[:], A["sb2"].partition_broadcast(128))
            small(WATT[:], A["watt"])
            small(POPEB[:], A["pope_bias"])
            small(TRIG[:, 0:2, :], A["trig"])
            small(LNW[:], A["ln_weight"])
            small(ROUTW[:], A["router_w"])
            assert n[0] == SMALL
            sp.dma_start(W0[:], A["w0"]).then_inc(moe_loaded, 16)
            sp.dma_start(W0D[:], A["w0d"]).then_inc(moe_loaded, 16)
            for c, (f, m) in enumerate(FCH):
                sp.dma_start(W1D[0:m, :, c, :], A["w2"][:, f:f + m, :].rearrange("e f d -> f e d")).then_inc(moe_loaded, 16)
            for half in range(2):
                if half:
                    sp.wait_ge(setup, 2)
                es = slice(4 * half, 4 * half + 4)
                sp.dma_start(STAGE[:, :, 0, :], A["w1"][es].rearrange("e d f -> d e f")).then_inc(stage_loaded, 16)
                sp.dma_start(STAGE[:, :, 1, :], A["w3"][es].rearrange("e d f -> d e f")).then_inc(stage_loaded, 16)

            def one_pass(i, last):
                if not last:
                    sp.wait_ge(sem["layer0"], 1)
                    sp.dma_start(XIN[:], x_t[i + 1]).then_inc(x_loaded, 16)
                for comp in range(4):
                    if comp == 0:
                        sp.wait_ge(sem["hi"], 1)
                        sp.wait_ge(sem["lo"], 1)
                    dst = (QS, KS)[comp // 2]
                    for r, low in enumerate(((0, 0, 1), (0, 1, 0))[comp // 2]):
                        src = EF if low else EH
                        for par in range(2):
                            row = 64 * par + 16 * r + 8 * (comp % 2)
                            sp.dma_start(dst[row:row + 8, :, :].bitcast(F32),
                                         src[64 * par:64 * par + 64, comp, :]).then_inc(stacked, 16)
                sp.wait_ge(sem["m2"], 2)
                for par in range(2):
                    for part in range(2):
                        row = 64 * par + SROWS + part
                        sp.dma_start(QS[row:row + 1, :, :].bitcast(F32),
                                     M2[8 * par:8 * par + 8, part, :]).then_inc(max_stacked, 16)
                sp.wait_ge(sem["out"], 1)
                sp.dma_start(y_t[i], S0[:]).then_inc(stored, 16)
                sp.sem_inc(arrived, 1)
                sp.wait_ge(released, i + 1)
                sp.sem_inc(seen, 1)

            with sp.Fori(0, B - 1) as i:
                one_pass(i, False)
            one_pass(B - 1, True)
            sp.wait_ge(stored, 16 * (B + 1))

        @block.tensor
        def _(pe):
            def signal(ins, name):
                ins.then_inc(sem[name], 1)

            def transposes(i, src, rows, bank):
                for t in range(NT):
                    ins = pe.transpose(PS[0:rows, bank, 128 * t:128 * t + 128], src[:, t, :], IDENT[:])
                signal(ins, "tp")

            def tok_matmul(bank, width, lhs, rhs, name):
                out = PS[:, bank, 0:NT * width].rearrange("p (t f) -> p t f", t=NT)
                for t in range(NT):
                    ins = pe.matmul(out[:, t, :], lhs[:, 128 * t:128 * t + 128], rhs, start=True, stop=True)
                signal(ins, name)

            pe.wait_ge(small_loaded, 16 * SMALL)
            pe.wait_ge(moe_loaded, 16 * 5)
            pe.wait_ge(setup, SETUP_V)
            pe.wait_ge(setup_pool, SETUP_P)
            pe.wait_ge(setup_act, SETUP_A)

            def layer0(i):
                pe.wait_ge(sem["xn"], 1)
                transposes(i, XN, 128, 4)
                pe.wait_ge(sem["evac"], 1)
                tok_matmul(5, 64, XNT, DOWN[:], "down")
                tok_matmul(7, E, XNT, GATEW[:], "logits")
                for k in range(E + 3):
                    if k <= E:
                        for pair, ready, used in ((0, "gpair", "gused"), (1, "lpair", "lused")):
                            if k:
                                pe.wait_ge(sem[used], k)
                            for m in range(2):
                                ins = pe.matmul(PS[:, 2 * pair + m, :], W0[:, k, 2 * pair + m, :], XNT[:],
                                                start=True, stop=True)
                            signal(ins, ready)
                    if k >= 2:
                        e = k - 2
                        pe.wait_ge(sem["a"], e + 1)
                        if e:
                            pe.wait_ge(sem["acc"], e)
                        shared = e == E
                        if shared:
                            pe.wait_ge(sem["cwT"], 1)
                        for t in range(NT):
                            out = PS[:, 6, 128 * t:128 * t + 128]
                            if shared:
                                pe.matmul(out, CWT[:, 128 * t:128 * t + 128], B0D[:], start=True, stop=False)
                            ins = pe.matmul(out, AA[:, e % 2, 128 * t:128 * t + 128], W0D[:, e, :],
                                            start=not shared, stop=True)
                        signal(ins, "y")
                    attention0(i, k)
                pe.wait_ge(sem["gelu"], 2)
                for t in range(NT):
                    for c in range(2):
                        ins = pe.matmul(PS[:, 4, 128 * t:128 * t + 128], G[:, c, 128 * t:128 * t + 128],
                                        FW2[:, c, :], start=c == 0, stop=c == 1)
                signal(ins, "ffn2")

            def attention0(i, k):
                if k == 0:
                    pe.wait_ge(sem["xi"], 1)
                    transposes(i, XI, 64, 4)
                if k == 1:
                    pe.wait_ge(sem["evac"], 2)
                    for r in range(2):
                        for g in range(4):
                            for c in range(3):
                                a = SHIFT[r] + g * GRP[r]
                                ins = pe.matmul(PS[32 * g:32 * g + 32, 5 - r, c * GRP[r]:(c + 1) * GRP[r]],
                                                WQKV[:, r, 32 * c:32 * c + 32], XIT[:, a:a + GRP[r]],
                                                start=True, stop=True)
                        signal(ins, "qkv")
                    pe.wait_ge(sem["cw"], 1)
                    for t in range(NT):
                        ins = pe.transpose(PS[0:E, 7, 128 * t:128 * t + 128], CW[:, t, :], IDENT[:])
                    signal(ins, "cwt")
                if k in CHUNK_AT:
                    for c in range(*CHUNK_AT[k]):
                        r, w, n = CHUNKS[c]
                        width = n * WIN[r] ** 2
                        pe.wait_ge(sem["prod"], c + 1)
                        if c >= 2:
                            pe.wait_ge(sem["S_sb"], c - 1)
                        else:
                            pe.wait_ge(sem["qkv_sb"], 2)
                        signal(pe.matmul(PS[:, 4 + c % 2, 0:width], HEADSUM[:], G[:, c % 2, 0:width],
                                         start=True, stop=True), "S")
                if k == 7:
                    pe.wait_ge(sem["wout"], 2)
                    for r in range(2):
                        for g in range(4):
                            a = SHIFT[r] + g * GRP[r]
                            n = min(GRP[r], T - a)
                            out = PS[32 * r:32 * r + 32, 4, :]
                            ins = pe.matmul(out[:, a:a + n], PROJ[:, r, g, :], WO[r][:, 0:n], start=True, stop=True)
                        ins = pe.matmul(out[:, 0:SHIFT[r]], PROJ[:, r, 3, :],
                                        WO[r][:, PADT - a:PADT - a + SHIFT[r]], start=True, stop=True)
                    signal(ins, "proj")
                if k == 8:
                    pe.wait_ge(sem["ppT"], 1)
                    tok_matmul(5, 128, PPT, UPW[:], "up")
                if k == 9:
                    pe.wait_ge(sem["h"], 1)
                    transposes(i, H, 128, 4)
                if k == 10:
                    pe.wait_ge(sem["evac"], 3)
                    for c in range(2):
                        signal(pe.matmul(PS[:, 5 - c, :], FW1[:, 128 * c:128 * c + 128], HT[:],
                                         start=True, stop=True), "ffn1")

            def scores_for_max(i, h, half):
                n = 2 * h + half
                if n >= 2:
                    pe.wait_ge(sem["mx"], n - 1)
                rows = slice(64 * (h % 2), 64 * (h % 2) + SROWS)
                for s in range(2):
                    t = 2 * half + s
                    ins = pe.matmul(PS[:, 2 * half + s, :], QS[rows, h // 2, 128 * t:128 * t + 128],
                                    KS[rows, h // 2, :], start=True, stop=True)
                signal(ins, "mpair")

            def ff_pair(i, c):
                e, (f, m) = c // NCH, FCH[c % NCH]
                if c:
                    pe.wait_ge(sem["fused"], c)
                for s in range(2):
                    for n, (w, x) in enumerate(((W1H, XRH), (W1H, XRL), (W1L, XRH))):
                        ins = pe.matmul(PS[0:m, 4 + s, :], w[:, e, s, f:f + m], x[:], start=n == 0, stop=n == 2)
                signal(ins, "fpair")

            def ff_down(i, e):
                pe.wait_ge(sem["fused"], NCH * (e + 1))
                if e:
                    pe.wait_ge(sem["acc1"], e)
                for c, (f, m) in enumerate(FCH):
                    for t in range(NT):
                        ins = pe.matmul(PS[:, 6, 128 * t:128 * t + 128],
                                        A4[0:m, (NCH * e + c) % 4, 128 * t:128 * t + 128], W1D[0:m, e, c, :],
                                        start=c == 0 and t == 0, stop=c == NCH - 1 and t == NT - 1,
                                        skip_group_check=True)
                signal(ins, "y1")

            def layer1(i):
                pe.wait_ge(sem["xn"], 2)
                transposes(i, X1, 128, 0)
                pe.wait_ge(sem["h"], 2)
                transposes(i, H, 128, 1)
                pe.wait_ge(sem["evac"], 4)
                for n in range(2):
                    signal(pe.matmul(PS[:, 2 + n, :], WATT[:, n, :], XNT[:], start=True, stop=True), "qk")
                tok_matmul(4, 128, XNT, WATT[:, 2, :], "v")
                pe.wait_ge(sem["evac"], 5)
                tok_matmul(7, E, HT, ROUTW[:], "logits")
                pe.wait_ge(sem["v_sb"], 1)
                pe.wait_ge(sem["xrh"], 2)
                ff_pair(i, 0)
                pe.wait_ge(stacked, 16 * 24)
                for hp in range(8):
                    scores_for_max(i, 2 * hp, 0)
                    if hp:
                        ff_pair(i, 3 * hp)
                    scores_for_max(i, 2 * hp, 1)
                    ff_pair(i, 3 * hp + 1)
                    if hp:
                        ff_down(i, hp - 1)
                    scores_for_max(i, 2 * hp + 1, 0)
                    ff_pair(i, 3 * hp + 2)
                    scores_for_max(i, 2 * hp + 1, 1)
                pe.wait_ge(sem["mx"], 32)
                for t in range(NT):
                    ins = pe.transpose(PS[0:H1, 7, 128 * t:128 * t + 128], MX[:, t, :], IDENT[:])
                signal(ins, "mt")
                ff_down(i, E - 1)
                pe.wait_ge(max_stacked, 16 * 4)
                for h in range(H1 + 1):
                    if h < H1:
                        rows = slice(64 * (h % 2), 64 * (h % 2) + SROWS + 2)
                        for half in range(2):
                            if h:
                                pe.wait_ge(sem["ex"], 2 * h - 1 + half)
                            for s in range(2):
                                k = 2 * half + s
                                ins = pe.matmul(PS[:, 2 * half + s, :], KS[rows, h // 2, 128 * k:128 * k + 128],
                                                QS[rows, h // 2, :], start=True, stop=True)
                            signal(ins, "st")
                    if h:
                        g = h - 1
                        pe.wait_ge(sem["ex"], 2 * g + 2)
                        if g == 0:
                            pe.wait_ge(sem["m2"], 2)
                        if g == 8:
                            pe.wait_ge(sem["acc1"], E)
                        out = obank(g)
                        for q in range(NT):
                            for k in range(NT):
                                ins = pe.matmul(out[:, g % 8, q, :], P[:, g % 2, k, 128 * q:128 * q + 128],
                                                V[:, k, g, :], start=k == 0, stop=k == NT - 1)
                        signal(ins, "pv")
                pe.wait_ge(sem["ot"], 2)
                transposes(i, H, 128, 0)
                pe.wait_ge(sem["evac"], 6)
                tok_matmul(1, 128, HT, WATT[:, 3, :], "wo")

            with pe.Fori(0, B) as i:
                layer0(i)
                layer1(i)
                end_pass(pe, i)

        @block.scalar
        def _(act):
            def go(name, *a, **k):
                act.activation(*a, **k).then_inc(sem[name], 1)

            for n in range(2):
                act.wait_ge(stage_loaded, 32 * (n + 1))
                act.activation(W1H[:, 4 * n:4 * n + 4], STAGE, ACT.Copy).then_inc(setup_act, 1)
            act.wait_ge(small_loaded, 16 * SMALL)
            act.wait_ge(setup_pool, SETUP_P)
            act.wait_ge(setup, SETUP_H)
            act.activation(PB[:, 3:4], PB[:, 1:2], ACT.Sin).then_inc(setup_act, 1)
            act.activation(PB[:, 4:5], PB[:, 2:3], ACT.Sin).then_inc(setup_act, 1)

            def layer0(i):
                act.wait_ge(sem["tp"], 1)
                go("evac", XNT[:], PS[:, 4, :], ACT.Copy)
                for k in range(E + 3):
                    if k <= E:
                        for s, (ready, used, done) in enumerate((("gpair", "gused", "h3g"), ("lpair", "lused", "h3l"))):
                            act.wait_ge(sem[ready], k + 1)
                            if k:
                                act.wait_ge(sem[used], k)
                            go(done, H3[:, s, :], PS[:, 2 * s + 1, :], ACT.Identity, bias=B0[:, k, 2 * s + 1:2 * s + 2])
                        act.wait_ge(sem["gg"], k + 1)
                        if k >= 2:
                            act.wait_ge(sem["a"], k - 1)
                        go("th", TH[:, k % 2, :], UL[:, k % 2, 0, :], ACT.Tanh, scale=0.5 * ALPHA)
                    attention0(i, k)

            def attention0(i, k):
                if k == 0:
                    act.wait_ge(sem["tp"], 2)
                    act.activation(XIT[:, 0:T], PS[0:64, 4, :], ACT.Copy, scale=N1W[:, 0:1])
                    go("evac", XIT[:, PADT:PADT + SHIFT[1]], PS[0:64, 4, 0:SHIFT[1]], ACT.Copy, scale=N1W[:, 0:1])
                    act.wait_ge(sem["lsub"], 1)
                    go("lexp", RT[:, 1], RT[:, 0], ACT.Exp)
                if k == 1:
                    for r in range(2):
                        act.wait_ge(sem["qkv"], r + 1)
                        for c in range(3):
                            ins = act.activation(QKV[r][:, c, :], PS[:, 5 - r, c * GRP[r]:(c + 1) * GRP[r]],
                                                 ACT.Identity, bias=QKVB[:, r, c:c + 1], scale=0.5 if c == 0 else 1.0)
                        ins.then_inc(sem["qkv_sb"], 1)
                    act.wait_ge(sem["cwt"], 1)
                    go("cwT", CWT, PS[0:E, 7, :], ACT.Copy, scale=4.0)
                if k in (3, 5):
                    r = k // 2 - 1
                    act.wait_ge(sem["wsub"], r + 1)
                    s = SC[:, S_AT[r]:S_AT[r] + GRP[r] * WIN[r]]
                    go("wexp", s, s, ACT.Exp)
                if k == 7:
                    act.wait_ge(sem["proj"], 1)
                    go("ppT", PPT, PS[0:64, 4, :], ACT.Identity, bias=PROJB[:, 0:1])
                if k == 8:
                    act.wait_ge(sem["x1"], 1)
                    square_sums()
                if k == 9:
                    act.wait_ge(sem["tp"], 3)
                    go("evac", HT[:], PS[:, 4, :], ACT.Copy, scale=N2W[:, 0:1])
                if k == 10:
                    for c in range(2):
                        act.wait_ge(sem["ffn1"], c + 1)
                        go("gelu", G[:, c, :], PS[:, 5 - c, :], ACT.Gelu, bias=FB1[:, c:c + 1])

            def square_sums():
                for t in range(NT):
                    ins = act.activation(H[:, t, :], X1[:, t, :], ACT.Square, accum_out=SQ[:, t:t + 1])
                ins.then_inc(sem["sqs"], 1)

            def layer1(i):
                act.wait_ge(sem["acc"], E + 1)
                go("silu", TH[:, 0, :], ACC[:].rearrange("p t f -> p (t f)"), ACT.Tanh, scale=0.5)
                act.wait_ge(sem["xn"], 2)
                square_sums()
                act.wait_ge(sem["tp"], 4)
                go("evac", XNT[:], PS[:, 0, :], ACT.Copy)
                act.wait_ge(sem["tp"], 5)
                go("evac", HT[:], PS[:, 1, :], ACT.Copy, scale=LNW[:, 0:1])
                for n in range(2):
                    act.wait_ge(sem["qk"], n + 1)
                    go("qabs", AA[:, n, :], PS[:, 2 + n, :], ACT.Abs)
                for n in range(2):
                    act.wait_ge(sem["qabs"], n + 1)
                    go("qexp", AA[:, n, :], AA[:, n, :], ACT.Exp, scale=-1.0)
                for n in range(2):
                    act.wait_ge(sem["qexp"], n + 1)
                    go("qln", AA[:, n, :], AA[:, n, :], ACT.Ln, bias=1.0)
                act.wait_ge(sem["v"], 1)
                go("v_sb", V[:, :, :, 0:HD1], PS[:, 4, :].rearrange("p (t h d) -> p t h d", t=NT, h=H1), ACT.Copy)
                act.wait_ge(sem["lsub"], 2)
                go("lexp", RT[:, 1], RT[:, 0], ACT.Exp)
                for c in range(E * NCH):
                    f, m = FCH[c % NCH]
                    act.wait_ge(sem["fpair"], c + 1)
                    if c >= 2:
                        act.wait_ge(sem["fused"], c - 1)
                    go("fth", TH[0:m, c % 2, :], PS[0:m, 4, :], ACT.Tanh, scale=0.5)
                for h in range(H1):
                    for half in range(2):
                        act.wait_ge(sem["st"], 2 * h + half + 1)
                        if h >= 2:
                            act.wait_ge(sem["pv"], h - 1)
                        go("ex", P[:, h % 2, 2 * half:2 * half + 2, :], PS[:, 2 * half:2 * half + 2, :], ACT.Exp,
                           scale=HD1 ** -0.5)
                act.wait_ge(sem["tp"], 6)
                go("evac", HT[:], PS[:, 0, :], ACT.Copy)
                act.wait_ge(sem["acc1"], E)
                go("silu", TH[:, 0, :], ACC[:].rearrange("p t f -> p (t f)"), ACT.Tanh, scale=0.5)

            with act.Fori(0, B) as i:
                layer0(i)
                layer1(i)
                end_pass(act, i)

        @block.gpsimd
        def _(pool):
            n = [0]

            def init(ins):
                n[0] += 1
                ins.then_inc(setup_pool, 1)
                pool.wait_ge(setup_pool, n[0])

            pool.memset(WQKV[:], 0.0).then_inc(zeroed, 1)
            pool.wait_ge(zeroed, 1)
            pool.memset(PROJ[:], 0.0).then_inc(zeroed, 1)
            pool.wait_ge(zeroed, 2)
            init(pool.memset(NHALF[:], -0.5))
            for r in range(2):
                init(pool.memset(MASK[r][96:128], 0.0))
            init(pool.memset(XIT[:, T:XIT_W], 0.0))
            init(pool.memset(V[:, :, :, HD1:HD1 + 1], 1.0))
            for row in (32, 96):
                init(pool.memset(KS[row:row + SROWS - 32 + 2].bitcast(F32), 1.0))
            for r in range(2):
                w, s = WIN[r], SHIFT[r]
                init(pool.memset(MASK[r][96:128, 0:w - s, w - s:w], -100.0))
                init(pool.memset(MASK[r][96:128, w - s:w, 0:w - s], -100.0))
            pool.wait_ge(small_loaded, 16 * SMALL)
            for r in range(2):
                w = WIN[r]
                for q in range(w):
                    init(pool.tensor_copy(BIAS[r][:, q, :], RPB[r][:, w - 1 - q:2 * w - 1 - q]))
            assert n[0] == SETUP_P, n[0]
            pool.wait_ge(setup, SETUP_V)
            done = {}

            def go(name, ins):
                done[name] = done.get(name, 0) + 1
                ins.then_inc(sem[name], 1)
                pool.wait_ge(sem[name], done[name])

            def rsqrt(i, k, src, scale, eps):
                go("pstep", pool.tensor_scalar(VAR[:], src, scale, eps, ALU.mult, ALU.add))
                go("rstd", pool.tensor_tensor(RSTD[:], VAR[:], NHALF[:], ALU.pow))

            def layer0(i):
                pool.wait_ge(sem["stats"], 1)
                rsqrt(i, 1, MV[:, :, 1], 1.0, 1e-5)
                pool.wait_ge(sem["xn"], 1)
                go("xb", pool.tensor_tensor(X1[:], XN[:], bc(UPB[:], [128, NT, 128], 1), ALU.add))
                pool.wait_ge(sem["xi_sq"], 1)
                rsqrt(i, 2, SQ[:], 1.0 / 64, 1e-6)
                for k in range(E + 3):
                    if k <= E:
                        u = UL[:, k % 2, 0, :]
                        v = UL[:, k % 2, 1, :]
                        pool.wait_ge(sem["gused"], k + 1)
                        go("gg", pool.tensor_scalar(u, u, LIMIT, None, ALU.min))
                        pool.wait_ge(sem["lused"], k + 1)
                        go("lc", pool.tensor_scalar(v, v, LIMIT, -LIMIT, ALU.min, ALU.max))
                    for r, (k_sub, k_pv) in enumerate(((2, 4), (4, 6))):
                        w = WIN[r]
                        s = SC[:, S_AT[r]:S_AT[r] + GRP[r] * w].rearrange("p (n k) -> p n k", k=w)
                        if k == k_sub:
                            pool.wait_ge(sem["wmax"], r + 1)
                            go("wsub", pool.tensor_tensor(s, s, bc(WM[r][:], [128, GRP[r], w], 2), ALU.subtract))
                        if k == k_pv:
                            pool.wait_ge(sem["wsum"], r + 1)
                            s = s.rearrange("p (w q) k -> p w q k", q=w)
                            v = QKV[r][:, 2, :].rearrange("p (w k) -> p w k", k=w)
                            go("wpv", pool.tensor_tensor(s, s, bc(v, [128, NWIN[r], w, w], 2), ALU.mult))
                    if k == 8:
                        pool.wait_ge(sem["sqs"], 1)
                        rsqrt(i, 3, SQ[:], 1.0 / 128, 1e-6)
                    if k == 9:
                        pool.wait_ge(sem["h"], 1)
                        go("xb", pool.tensor_tensor(X1[:], X1[:], bc(FB2[:], [128, NT, 128], 1), ALU.add))

            def layer1(i):
                pool.wait_ge(sem["stats"], 2)
                rsqrt(i, 4, MV[:, :, 1], 1.0, 1e-5)
                pool.wait_ge(sem["sqs"], 2)
                rsqrt(i, 5, SQ[:], 1.0 / 128, 1e-5)
                for n in range(2):
                    pool.wait_ge(sem["mag"], n + 1)
                    go("emb_sin", pool.tensor_tensor(EF[:, 2 * n + 1, :], TH[:, n, :], TRIG[:, 2 * n + 1, :], ALU.mult))

            with pool.Fori(0, B) as i:
                layer0(i)
                layer1(i)
                pool.wait_ge(sem["out"], 1)
                pool.wait_ge(arrived, 4)
                pool.sem_clear(counted)
                pool.sem_inc(released, 1)

        @block.vector
        def _(dve):
            count = [0]

            def go(name, ins):
                ins.then_inc(sem[name], 1)

            def step(i, ins):
                count[0] += 1
                ins.then_inc(sem["step"], 1)
                dve.wait_ge(sem["step"], count[0])

            n = [0]

            def init(ins):
                n[0] += 1
                ins.then_inc(setup, 1)
                dve.wait_ge(setup, n[0])

            for half in range(2):
                dve.wait_ge(setup_act, half + 1)
                hi = W1H[:, 4 * half:4 * half + 4]
                init(dve.tensor_tensor(W1L[:, 4 * half:4 * half + 4], STAGE, hi.bitcast(F32), ALU.subtract))
                if half == 0:
                    init(dve.memset(PB[:, 5:6], 0.0))
            dve.wait_ge(small_loaded, 16 * SMALL)
            pi = float(np.pi)
            init(dve.tensor_scalar(PB[:, 0:1], POPEB[:], 0.0, -2.0 * pi, ALU.min, ALU.max))
            init(dve.tensor_scalar(PB[:, 1:2], PB[:, 0:1], pi, 0.5, ALU.add, ALU.mult))
            init(dve.scalar_tensor_tensor(PB[:, 2:3], PB[:, 1:2], -1.0, PB[:, 1:2], ALU.mult, ALU.min))
            init(dve.tensor_scalar(PB[:, 2:3], PB[:, 2:3], pi / 2, None, ALU.add))
            assert n[0] == SETUP_H
            dve.wait_ge(setup_act, SETUP_A)
            init(dve.scalar_tensor_tensor(PB[:, 0:1], PB[:, 3:4], 2.0, PB[:, 4:5], ALU.mult, ALU.mult))
            init(dve.scalar_tensor_tensor(PB[:, 1:2], PB[:, 3:4], 2.0, PB[:, 3:4], ALU.mult, ALU.mult))
            init(dve.tensor_scalar(PB[:, 1:2], PB[:, 1:2], 1.0, None, ALU.subtract))
            init(dve.tensor_scalar(PB[:, 2:3], PB[:, 0:1], -1.0, None, ALU.mult))
            for m, (first, second) in enumerate(((0, 0), (1, 2))):
                init(dve.tensor_scalar(TRIG[:, 2 + m, :], TRIG[:, m, :], PB[:, 1:2], None, ALU.mult))
                init(dve.scalar_tensor_tensor(TRIG[:, 2 + m, :], TRIG[:, 1 - m, :], PB[:, second:second + 1],
                                              TRIG[:, 2 + m, :], ALU.mult, ALU.add))
            init(dve.tensor_scalar(QKVB[:, :, 0:1], QKVB[:, :, 0:1], 0.5, None, ALU.mult))
            assert n[0] == SETUP_V, n[0]
            dve.wait_ge(setup_pool, SETUP_P)
            dve.wait_ge(moe_loaded, 16 * 5)

            def layernorm(i, k, src, dst):
                for t in range(NT):
                    ins = dve.bn_stats(STAT[:, t, :], src[:, t, :])
                step(i, ins)
                for t in range(NT):
                    ins = dve.bn_aggr(MV[:, t, :], STAT[:, t, :])
                go("stats", ins)
                dve.wait_ge(sem["stats"], k)
                dve.wait_ge(sem["rstd"], 3 * k - 2)
                for t in range(NT):
                    ins = dve.tensor_scalar(dst[:, t, :], src[:, t, :], MV[:, t, 0:1], RSTD[:, t:t + 1],
                                            ALU.subtract, ALU.mult)
                go("xn", ins)

            def routing(i, k, biased):
                s4 = [128, NT, E]
                logits = ntok(PS[:, 7, 0:NT * E])
                dve.wait_ge(sem["logits"], k)
                step(i, dve.tensor_reduce(RS[:, 0], logits, AX.X, ALU.max))
                go("lsub", dve.tensor_tensor(RT[:, 0], logits, bc(RS[:, 0], s4, 2), ALU.subtract))
                dve.wait_ge(sem["lexp"], k)
                step(i, dve.tensor_reduce(RS[:, 1], RT[:, 1], AX.X, ALU.add))
                step(i, dve.reciprocal(RS[:, 2], RS[:, 1]))
                step(i, dve.tensor_tensor(RT[:, 1], RT[:, 1], bc(RS[:, 2], s4, 2), ALU.mult))
                key = 1
                if biased:
                    key = 2
                    step(i, dve.tensor_tensor(RT[:, 2], RT[:, 1], bc(GATEB[:], s4, 1), ALU.add))
                for pick in range(2):
                    hot = RT[:, 3 + pick]
                    step(i, dve.tensor_reduce(RS[:, 3], RT[:, key], AX.X, ALU.max))
                    step(i, dve.tensor_tensor(hot, RT[:, key], bc(RS[:, 3], s4, 2), ALU.is_equal))
                    step(i, dve.tensor_tensor(hot, hot, bc(REV[:], s4, 1), ALU.mult))
                    step(i, dve.tensor_reduce(RS[:, 3], hot, AX.X, ALU.max))
                    step(i, dve.tensor_tensor(hot, hot, bc(RS[:, 3], s4, 2), ALU.is_equal))
                    if pick == 0:
                        step(i, dve.scalar_tensor_tensor(RT[:, 5], hot, -1e30, RT[:, key], ALU.mult, ALU.add))
                        key = 5
                step(i, dve.tensor_tensor(RT[:, 6], RT[:, 3], RT[:, 4], ALU.add))
                go("cw", dve.scalar_tensor_tensor(CW[:], RT[:, 6], 0.5, RT[:, 1], ALU.mult, ALU.mult))
                dve.wait_ge(sem["cw"], k)

            def layer0(i):
                dve.wait_ge(x_loaded, 16 * (i + 1))
                layernorm(i, 1, XIN, XN)
                for k in range(E + 3):
                    if k <= E:
                        for s, (pair, h3, used) in enumerate((("gpair", "h3g", "gused"), ("lpair", "h3l", "lused"))):
                            dve.wait_ge(sem[pair], k + 1)
                            dve.wait_ge(sem[h3], k + 1)
                            if k >= 2:
                                dve.wait_ge(sem["a"], k - 1)
                            go(used, dve.scalar_tensor_tensor(UL[:, k % 2, s, :], PS[:, 2 * s, :],
                                                              B0[:, k, 2 * s:2 * s + 1], H3[:, s, :], ALU.add, ALU.mult))
                    if 1 <= k <= E + 1:
                        e = k - 1
                        th = TH[:, e % 2, :]
                        dve.wait_ge(sem["th"], e + 1)
                        step(i, dve.scalar_tensor_tensor(th, th, 1.0, UL[:, e % 2, 0, :], ALU.add, ALU.mult))
                        dve.wait_ge(sem["lc"], e + 1)
                        if e >= 2:
                            dve.wait_ge(sem["y"], e - 1)
                        go("a", dve.scalar_tensor_tensor(AA[:, e % 2, :], UL[:, e % 2, 1, :], 1.0, th, ALU.add, ALU.mult))
                    if k >= 2:
                        e = k - 2
                        dve.wait_ge(sem["y"], e + 1)
                        if e:
                            dve.wait_ge(sem["acc"], e)
                        for t in range(NT):
                            gate = CW[:, t, e:e + 1] if e < E else 0.5
                            ins = dve.scalar_tensor_tensor(ACC[:, t, :], PS[:, 6, 128 * t:128 * t + 128], gate,
                                                           ACC[:, t, :] if e else SB0D[:], ALU.mult, ALU.add)
                        go("acc", ins)
                    attention0(i, k)
                dve.wait_ge(sem["ffn2"], 1)
                dve.wait_ge(sem["xb"], 2)
                dve.wait_ge(stored, 16 * (i + 1))
                step(i, dve.tensor_tensor(S0[:], ntok(PS[:, 4, :]), X1[:], ALU.add))
                dve.wait_ge(sem["silu"], 1)
                step(i, dve.scalar_tensor_tensor(ACC[:], ntok(TH[:, 0, :]), 1.0, ACC[:], ALU.add, ALU.mult))
                step(i, dve.scalar_tensor_tensor(ACC[:], ACC[:], 0.5, S0[:], ALU.mult, ALU.mult))
                go("layer0", dve.tensor_tensor(XA[:], ACC[:], XIN[:], ALU.add))
                dve.wait_ge(sem["layer0"], 1)

            def attention0(i, k):
                if k == 0:
                    dve.wait_ge(sem["down"], 1)
                    step(i, dve.tensor_tensor(XI[:], ntok(PS[:, 5, 0:256]), bc(DOWNB[:], [128, NT, 64], 1), ALU.add))
                    step(i, dve.tensor_tensor(H[:, :, 0:64], XI[:], XI[:], ALU.mult))
                    go("xi_sq", dve.tensor_reduce(SQ[:], H[:, :, 0:64], AX.X, ALU.add))
                    dve.wait_ge(sem["rstd"], 2)
                    go("xi", dve.tensor_tensor(XI[:], XI[:], bc(RSTD[:], [128, NT, 64], 2), ALU.mult))
                    routing(i, 1, True)
                if k in CHUNK_AT:
                    first, last = CHUNK_AT[k]
                    if k == 2:
                        dve.wait_ge(sem["qkv_sb"], 2)
                    for c in range(first, last + 2):
                        if c < last:
                            r, w, m = CHUNKS[c]
                            q, kk = (QKV[r][:, j, :].rearrange("p (w q) -> p w q", q=WIN[r])[:, w:w + m] for j in range(2))
                            full = [128, m, WIN[r], WIN[r]]
                            if c >= 2:
                                dve.wait_ge(sem["S"], c - 1)
                            dst = G[:, c % 2, 0:m * WIN[r] ** 2].rearrange("p (w q k) -> p w q k", w=m, q=WIN[r])
                            go("prod", dve.tensor_tensor(dst, bc(q, full, 3), bc(kk, full, 2), ALU.mult))
                        if c - 2 >= first:
                            r, w, m = CHUNKS[c - 2]
                            a = WIN[r] ** 2
                            dve.wait_ge(sem["S"], c - 1)
                            dst = SC[:, S_AT[r] + w * a:S_AT[r] + (w + m) * a].rearrange("p (w a) -> p w a", w=m)
                            src = PS[:, 4 + c % 2, 0:m * a].rearrange("p (w a) -> p w a", w=m)
                            bias = BIAS[r][:].rearrange("p q k -> p (q k)")
                            go("S_sb", dve.tensor_tensor(dst, src, bc(bias, [128, m, a], 1), ALU.add))
                            dve.wait_ge(sem["S_sb"], c - 1)
                if k in (2, 4):
                    r = k // 2 - 1
                    w, lastw = WIN[r], (PADT // WIN[r] - 1) % NWIN[r]
                    s = SC[96:128, S_AT[r] + lastw * w * w:S_AT[r] + (lastw + 1) * w * w]
                    step(i, dve.tensor_tensor(s, s, MASK[r][96:128].rearrange("p q k -> p (q k)"), ALU.add))
                    s = SC[:, S_AT[r]:S_AT[r] + GRP[r] * w].rearrange("p (n k) -> p n k", k=w)
                    go("wmax", dve.tensor_reduce(WM[r][:], s, AX.X, ALU.max))
                if k in (4, 6):
                    r = k // 2 - 2
                    s = SC[:, S_AT[r]:S_AT[r] + GRP[r] * WIN[r]].rearrange("p (n k) -> p n k", k=WIN[r])
                    dve.wait_ge(sem["wexp"], r + 1)
                    go("wsum", dve.tensor_reduce(WM[r][:], s, AX.X, ALU.add))
                    dve.wait_ge(sem["wsum"], r + 1)
                    step(i, dve.reciprocal(WM[r][:], WM[r][:]))
                if k in (5, 7):
                    r = k // 2 - 2
                    s = SC[:, S_AT[r]:S_AT[r] + GRP[r] * WIN[r]].rearrange("p (n k) -> p n k", k=WIN[r])
                    dve.wait_ge(sem["wpv"], r + 1)
                    step(i, dve.tensor_reduce(WO[r][:], s, AX.X, ALU.add))
                    go("wout", dve.tensor_tensor(WO[r][:], WO[r][:], WM[r][:], ALU.mult))
                if k == 8:
                    dve.wait_ge(sem["up"], 1)
                    dve.wait_ge(sem["xb"], 1)
                    go("x1", dve.tensor_tensor(X1[:], ntok(PS[:, 5, :]), X1[:], ALU.add))
                    dve.wait_ge(sem["x1"], 1)
                    dve.wait_ge(sem["rstd"], 3)
                    go("h", dve.tensor_tensor(H[:], X1[:], bc(RSTD[:], [128, NT, 128], 2), ALU.mult))

            def chunk(i, c):
                m = FCH[c % NCH][1]
                th = TH[0:m, c % 2, :]
                dve.wait_ge(sem["fpair"], c + 1)
                dve.wait_ge(sem["fth"], c + 1)
                step(i, dve.scalar_tensor_tensor(th, th, 1.0, PS[0:m, 4, :], ALU.add, ALU.mult))
                if c >= 4:
                    dve.wait_ge(sem["y1"], (c - 4) // NCH + 1)
                go("fused", dve.tensor_tensor(A4[0:m, c % 4, :], PS[0:m, 5, :], th, ALU.mult))

            def accumulate(i, e):
                dve.wait_ge(sem["y1"], e + 1)
                if e:
                    dve.wait_ge(sem["acc1"], e)
                for t in range(NT):
                    y, gate = PS[:, 6, 128 * t:128 * t + 128], CW[:, t, e:e + 1]
                    if e:
                        ins = dve.scalar_tensor_tensor(ACC[:, t, :], y, gate, ACC[:, t, :], ALU.mult, ALU.add)
                    else:
                        ins = dve.tensor_scalar(ACC[:, t, :], y, gate, None, ALU.mult)
                go("acc1", ins)

            def row_max(i, h, half):
                dve.wait_ge(sem["mpair"], 2 * h + half + 1)
                go("mx", dve.tensor_reduce(MX[:, 2 * half:2 * half + 2, 8 * (h % 2) + h // 2], PS[:, 2 * half:2 * half + 2, :], AX.X, ALU.max))

            def layer1(i):
                layernorm(i, 2, XA, X1)
                dve.wait_ge(sem["xn"], 2)
                dve.wait_ge(sem["rstd"], 5)
                go("h", dve.tensor_tensor(H[:], X1[:], bc(RSTD[:], [128, NT, 128], 2), ALU.mult))
                for n in range(2):
                    dve.wait_ge(sem["qln"], n + 1)
                    go("mag", dve.scalar_tensor_tensor(TH[:, n, :], PS[:, 2 + n, :], 0.0, AA[:, n, :], ALU.max, ALU.add))
                for n in range(2):
                    dve.wait_ge(sem["mag"], n + 1)
                    go("emb_cos", dve.tensor_tensor(EF[:, 2 * n, :], TH[:, n, :], TRIG[:, 2 * n, :], ALU.mult))
                dve.wait_ge(sem["emb_cos"], 2)
                dve.wait_ge(sem["emb_sin"], 2)
                go("hi", dve.tensor_copy(EH.bitcast(F32R), EF))
                dve.wait_ge(sem["hi"], 1)
                go("lo", dve.tensor_tensor(EF, EF, EH, ALU.subtract))
                dve.wait_ge(sem["evac"], 5)
                go("xrh", dve.tensor_copy(XRH[:], HT[:]))
                dve.wait_ge(sem["xrh"], 1)
                go("xrh", dve.tensor_tensor(XRL[:], HT[:], XRH[:].bitcast(F32), ALU.subtract))
                routing(i, 2, False)
                chunk(i, 0)
                for hp in range(8):
                    row_max(i, 2 * hp, 0)
                    if hp:
                        chunk(i, 3 * hp)
                    row_max(i, 2 * hp, 1)
                    chunk(i, 3 * hp + 1)
                    if hp:
                        accumulate(i, hp - 1)
                    row_max(i, 2 * hp + 1, 0)
                    chunk(i, 3 * hp + 2)
                    row_max(i, 2 * hp + 1, 1)
                dve.wait_ge(sem["mt"], 1)
                go("m2", dve.tensor_scalar(M2[:, 0, :].bitcast(F32R), PS[0:H1, 7, :], -1.0, None, ALU.mult))
                dve.wait_ge(sem["m2"], 1)
                go("m2", dve.scalar_tensor_tensor(M2[:, 1, :].bitcast(F32R), PS[0:H1, 7, :], -1.0, M2[:, 0, :],
                                                  ALU.mult, ALU.subtract))
                accumulate(i, E - 1)
                for g in range(2):
                    dve.wait_ge(sem["pv"], 8 * g + 8)
                    o = obank(8 * g)
                    den = DEN[:, g, :].rearrange("p (h t) -> p h t", h=8)
                    step(i, dve.reciprocal(den, o[:, :, :, HD1]))
                    dst = H[:].rearrange("p t (h d) -> p h t d", h=H1)[:, 8 * g:8 * g + 8]
                    go("ot", dve.tensor_tensor(dst, o[:, :, :, 0:HD1], bc(den, [128, 8, NT, HD1], 3), ALU.mult))
                dve.wait_ge(sem["silu"], 2)
                step(i, dve.scalar_tensor_tensor(ACC[:], ntok(TH[:, 0, :]), 1.0, ACC[:], ALU.add, ALU.mult))
                dve.wait_ge(sem["wo"], 1)
                step(i, dve.scalar_tensor_tensor(ACC[:], ACC[:], 0.5, ntok(PS[:, 1, :]), ALU.mult, ALU.mult))
                go("out", dve.tensor_tensor(S0[:], ACC[:], XA[:], ALU.add))

            with dve.Fori(0, B) as i:
                layer0(i)
                layer1(i)
                end_pass(dve, i)
            assert count[0] == STEPS, count[0]


def kernel(**inputs):
    import concourse.bacc as bacc
    from concourse.bass_utils import run_bass_kernel_spmd

    g = {n: np.asarray(v) for n, v in inputs.items()}
    dense = np.ascontiguousarray
    w1 = np.concatenate([g["L0_ffn_w1"], g["L0_ffn_sw1"][None]])
    w3 = np.concatenate([g["L0_ffn_w3"], g["L0_ffn_sw3"][None]])
    b1 = np.concatenate([g["L0_ffn_b1"], g["L0_ffn_sb1"][None]])
    b3 = np.concatenate([g["L0_ffn_b3"], g["L0_ffn_sb3"][None]])
    w0 = np.stack([w1[:, ::2], w3[:, ::2], w1[:, 1::2], w3[:, 1::2]], 1).transpose(3, 0, 1, 2)
    b0 = np.stack([b1[:, ::2], b3[:, ::2], b1[:, 1::2], b3[:, 1::2]], 1).transpose(2, 0, 1)
    w0d = np.concatenate([g["L0_ffn_w2"], g["L0_ffn_sw2"][None]]).transpose(2, 0, 1)
    order = np.array([(2 * j + par) * HD1 + d for par in range(2) for d in range(HD1) for j in range(8)])
    watt = np.stack([g["L1_attn_wq"].T[:, order], g["L1_attn_wk"].T[:, order],
                     g["L1_attn_wv"].T, g["L1_attn_wo"].T], 1)
    inv = np.float32(10000.0) ** (-(np.arange(HD1, dtype=np.float32) / np.float32(HD1)))
    freq = np.arange(T, dtype=np.float32)[None, :] * inv.astype(np.float32)[:, None]
    freq = freq[order % HD1].astype(np.float64)
    trig = np.stack([np.cos(freq), np.sin(freq)], 1).astype(np.float32)
    arrays = {
        "x": g["L0_attn_x"].reshape(B * T, D),
        "ident": np.eye(128, dtype=np.float32),
        "headsum": np.kron(np.eye(32, dtype=np.float32), np.ones((4, 4), np.float32)),
        "rev": np.tile(np.arange(E, 0, -1, dtype=np.float32), (128, 1)),
        "trig": trig, "w0": w0, "b0": b0, "w0d": w0d, "watt": watt,
        "rpb1": np.repeat(g["L0_attn_rpb1"][::-1].T, 4, 0), "rpb2": np.repeat(g["L0_attn_rpb2"][::-1].T, 4, 0),
        "gate_w": g["L0_ffn_gate_w"].T, "gate_b": g["L0_ffn_gate_b"], "b2": g["L0_ffn_b2"], "sb2": g["L0_ffn_sb2"],
        "pope_bias": g["L1_attn_pope_bias"].reshape(-1)[order],
        "ln_weight": g["L1_ffn_ln_weight"], "router_w": g["L1_ffn_router_w"],
        "w1": g["L1_ffn_w1"], "w3": g["L1_ffn_w3"], "w2": g["L1_ffn_w2"],
    }
    for n in ("down_w", "down_b", "up_w", "up_b", "norm1_w", "norm2_w", "qkv1_w", "qkv1_b", "proj1_w", "proj1_b",
              "qkv2_w", "qkv2_b", "proj2_w", "proj2_b", "ffn_w1", "ffn_b1", "ffn_w2", "ffn_b2"):
        arrays[n] = g[f"L0_attn_{n}"]
    for n, width in (("qkv1_b", 3), ("qkv2_b", 3), ("ffn_b1", 2), ("norm1_w", 1), ("norm2_w", 1), ("proj1_b", 1),
                     ("proj2_b", 1), ("pope_bias", 1), ("ln_weight", 1)):
        arrays[n] = arrays[n].reshape(width, -1).T
    nc = bacc.Bacc("TRN2", target_bir_lowering=False, num_devices=1)
    ins, aps = {}, {}
    for n, a in arrays.items():
        ins[f"in_{n}"] = dense(a)
        aps[n] = nc.dram_tensor(f"in_{n}", a.shape, mybir.dt.from_np(a.dtype), kind="ExternalInput").ap()
    aps["y"] = nc.dram_tensor("out_y", (B * T, D), F32, kind="ExternalOutput").ap()
    build(nc, aps)
    r = run_bass_kernel_spmd(nc, [ins], core_ids=[0])
    return r.results[0]["out_y"].reshape(B, T, D)
```

```python
from contextlib import ExitStack

import numpy as np
import concourse.bass as bass
from concourse import mybir

F32 = mybir.dt.float32
F32R = mybir.dt.float32r
ALU = mybir.AluOpType
ACT = mybir.ActivationFunctionType
AX = mybir.AxisListType

B, T, D = 8, 512, 128
NT = T // 128
E = 8
WIN = (10, 20)
SHIFT = (5, 10)
NWIN = (13, 7)
GRP = (WIN[0] * NWIN[0], WIN[1] * NWIN[1])
PADT = 520
XIT_W = SHIFT[1] + 4 * GRP[1]
CHUNKS = [(0, 0, 5), (0, 5, 5), (0, 10, 3)] + [(1, w, 1) for w in range(NWIN[1])]
CHUNK_AT = {2: (0, 3), 3: (3, 7), 4: (7, 10)}
S_AT = (0, NWIN[0] * WIN[0] ** 2)
S_W = S_AT[1] + NWIN[1] * WIN[1] ** 2
H1, HD1 = 16, 8
FF = 352
FCH = [(0, 128), (128, 128), (256, 96)]
NCH = len(FCH)
V_W = H1 * (HD1 + 1) + 32 - (HD1 + 1)
SMALL = 51
SETUP_H, SETUP_V, SETUP_P, SETUP_A = 7, 16, 41, 4
LEAD = 6
SROWS = 48
LIMIT, ALPHA = 7.0, 1.702

COUNTED = {
    "TensorE":
        "tp down logits gpair lpair y qkv cwt S proj up ffn1 ffn2 qk v fpair mpair y1 oq mt st pv wo",
    "ScalarE":
        "evac lexp h3g h3l th ys ys1 qkv_sb cwT wexp ppT sqs gelu qabs qexp qln v_sb fth ex silu",
    "GpSimd":
        "rstd gg lc wsub wpv xb emb_sin pstep",
    "VectorE":
        "stats xn xi_sq xi lsub cw gused lused a acc prod S_sb wmax wsum wout x1 h s0 layer0 xrh mag "
        "emb_cos hi lo mx m2 fused acc1 oe ot out step",
    "DMA":
        "stacked max_stacked",
    "all":
        "arrived",
}


def plan1():
    pairs, out, c = 2 * H1, [], 0
    for n in range(pairs + 1):
        upto = LEAD + (E * NCH - LEAD) * n // pairs
        while c < upto:
            out.append(("chunk", c))
            if c % NCH == 0 and c:
                out.append(("down", c // NCH - 1))
            c += 1
        if n < pairs:
            out.append(("max", n))
    return out


def build(nc, A):
    ctx = ExitStack()
    with ctx:
        def sb(name, shape, dt=F32):
            return ctx.enter_context(nc.sbuf_tensor(name, shape, dt))

        sem = {n: ctx.enter_context(nc.semaphore(n)) for n in " ".join(COUNTED.values()).split()}
        numbers = sorted(s.num for s in sem.values())
        counted = range(numbers[0], numbers[-1] + 1)
        assert len(counted) == len(numbers)
        released = ctx.enter_context(nc.semaphore("released"))
        seen = ctx.enter_context(nc.semaphore("seen"))
        x_loaded = ctx.enter_context(nc.semaphore("x_loaded"))
        small_loaded = ctx.enter_context(nc.semaphore("small_loaded"))
        moe_loaded = ctx.enter_context(nc.semaphore("moe_loaded"))
        stage_loaded = ctx.enter_context(nc.semaphore("stage_loaded"))
        zeroed = ctx.enter_context(nc.semaphore("zeroed"))
        setup = ctx.enter_context(nc.semaphore("setup"))
        setup_pool = ctx.enter_context(nc.semaphore("setup_pool"))
        setup_act = ctx.enter_context(nc.semaphore("setup_act"))
        stacked, max_stacked, arrived = sem["stacked"], sem["max_stacked"], sem["arrived"]
        stored = ctx.enter_context(nc.semaphore("stored"))

        IDENT = sb("IDENT", [128, 128])
        HEADSUM = sb("HEADSUM", [128, 128])
        REV = sb("REV", [128, E])
        NHALF = sb("NHALF", [128, NT])
        DOWN = sb("DOWN", [128, 64])
        DOWNB = sb("DOWNB", [128, 64])
        N1W = sb("N1W", [64, 1])
        N2W = sb("N2W", [128, 1])
        WQKV = sb("WQKV", [64, 2, 96])
        QKVB = sb("QKVB", [128, 2, 3])
        PROJ = sb("PROJ", [128, 2, 4, 32])
        PROJB = sb("PROJB", [64, 1])
        UPW = sb("UPW", [64, 128])
        UPB = sb("UPB", [128, 128])
        RPB = [sb(f"RPB{r}", [128, 2 * WIN[r] - 1]) for r in range(2)]
        BIAS = [sb(f"BIAS{r}", [128, WIN[r], WIN[r]]) for r in range(2)]
        MASK = [sb(f"MASK{r}", [128, WIN[r], WIN[r]]) for r in range(2)]
        FW1 = sb("FW1", [128, 256])
        FB1 = sb("FB1", [128, 2])
        FW2 = sb("FW2", [128, 2, 128])
        FB2 = sb("FB2", [128, 128])
        GATEW = sb("GATEW", [128, E])
        GATEB = sb("GATEB", [128, E])
        W0 = sb("W0", [128, E + 1, 4, 128])
        B0 = sb("B0", [128, E + 1, 4])
        W0D = sb("W0D", [128, E + 1, 128])
        B0D = sb("B0D", [E, 128])
        SB0D = sb("SB0D", [128, 128])
        WATT = sb("WATT", [128, 4, 128])
        POPEB = sb("POPEB", [128, 1])
        TRIG = sb("TRIG", [128, 4, T])
        PB = sb("PB", [128, 6])
        LNW = sb("LNW", [128, 1])
        ROUTW = sb("ROUTW", [128, E])
        W1H = sb("W1H", [128, E, 2, FF], F32R)
        W1L = sb("W1L", [128, E, 2, FF], F32R)
        W1D = sb("W1D", [128, E, NCH, 128])

        XIN = sb("XIN", [128, NT, 128])
        STAT = sb("STAT", [128, NT, 6])
        MV = sb("MV", [128, NT, 2])
        VAR = sb("VAR", [128, NT])
        RSTD = sb("RSTD", [128, NT])
        SQ = sb("SQ", [128, NT])
        XN = sb("XN", [128, NT, 128])
        XNT = sb("XNT", [128, T])
        XI = sb("XI", [128, NT, 64])
        XIT = sb("XIT", [64, XIT_W])
        QKV = [sb(f"QKV{r}", [128, 3, GRP[r]]) for r in range(2)]
        SC = sb("SC", [128, 4100])
        WM = [sb(f"WM{r}", [128, GRP[r]]) for r in range(2)]
        WO = [sb(f"WO{r}", [128, GRP[r]]) for r in range(2)]
        X1 = sb("X1", [128, NT, 128])
        H = sb("H", [128, NT, 128])
        HT = sb("HT", [128, T])
        G = sb("G", [128, 2, 512])
        S0 = sb("S0", [128, NT, 128])
        RT = sb("RT", [128, 8, NT, E])
        RS = sb("RS", [128, 6, NT])
        CW = sb("CW", [128, NT, E])
        UL = sb("UL", [128, 2, 2, 512])
        TH = sb("TH", [128, 2, 512])
        A4 = sb("A4", [128, 4, 512])
        ACC = sb("ACC", [128, NT, 128])
        XRH = sb("XRH", [128, T], F32R)
        XRL = sb("XRL", [128, T], F32R)
        QS = sb("QS", [128, 8, T], F32R)
        KS = sb("KS", [128, 8, T], F32R)
        V = sb("V", [128, NT, V_W])
        MX = sb("MX", [128, NT, H1])
        DEN = sb("DEN", [128, 4, 16])
        PS = ctx.enter_context(nc.psum_tensor("PS", [128, 8, 512], F32))

        AA, H3 = A4[:, 0:2, :], A4[:, 2:4, :]
        PPT = HT[0:64, :]
        CWT = XN[0:E].rearrange("p t f -> p (t f)")
        XA = XN
        YS = S0
        EH = SC[:, 0:4 * T].rearrange("p (c n) -> p c n", c=4)
        M2 = G[0:H1]
        EF = UL[:].rearrange("p a b n -> p (a b) n")
        P = SC[:, 0:4096].rearrange("p (s a n) -> p s a n", s=2, a=4)
        STAGE = SC[:, 0:4 * 2 * FF].rearrange("p (e b f) -> p e b f", e=4, b=2)
        ntok = lambda ap: ap.rearrange("p (t f) -> p t f", t=NT)

        def bc(ap, shape, axis):
            return ap.unsqueeze(axis).to_broadcast(shape)

        def end_pass(eng, i):
            eng.wait_ge(sem["out"], 1)
            eng.sem_inc(arrived, 1)
            eng.wait_ge(released, i + 1)

        block = ctx.enter_context(nc.Block())

        @block.sync
        def _(sp):
            x_t = A["x"].rearrange("(b t p) d -> b p t d", b=B, t=NT)
            y_t = A["y"].rearrange("(b t p) d -> b p t d", b=B, t=NT)
            sp.sem_inc(stored, 16)
            sp.dma_start(XIN[:], x_t[0]).then_inc(x_loaded, 16)
            n = [0]

            def small(dst, src):
                sp.dma_start(dst, src).then_inc(small_loaded, 16)
                n[0] += 1

            small(IDENT[:], A["ident"])
            small(HEADSUM[:], A["headsum"])
            small(REV[:], A["rev"])
            small(DOWN[:], A["down_w"])
            small(DOWNB[:], A["down_b"].partition_broadcast(128))
            small(N1W[:], A["norm1_w"])
            small(N2W[:], A["norm2_w"])
            small(UPW[:], A["up_w"])
            small(UPB[:], A["up_b"].partition_broadcast(128))
            sp.wait_ge(zeroed, 2)
            for r in range(2):
                small(WQKV[32 * r:32 * r + 32, r, :], A[f"qkv{r + 1}_w"])
                small(PROJB[32 * r:32 * r + 32, :], A[f"proj{r + 1}_b"])
                for g in range(4):
                    rows = slice(32 * g, 32 * g + 32)
                    small(QKVB[rows, r, :], A[f"qkv{r + 1}_b"])
                    small(PROJ[rows, r, g, :], A[f"proj{r + 1}_w"])
                    small(RPB[r][rows, :], A[f"rpb{r + 1}"])
            small(FW1[:], A["ffn_w1"])
            small(FB1[:], A["ffn_b1"])
            small(FW2[:], A["ffn_w2"].rearrange("(c p) d -> p c d", c=2))
            small(FB2[:], A["ffn_b2"].partition_broadcast(128))
            small(GATEW[:], A["gate_w"])
            small(GATEB[:], A["gate_b"].partition_broadcast(128))
            small(B0[:], A["b0"])
            small(B0D[:], A["b2"])
            small(SB0D[:], A["sb2"].partition_broadcast(128))
            small(WATT[:], A["watt"])
            small(POPEB[:], A["pope_bias"])
            small(TRIG[:, 0:2, :], A["trig"])
            small(LNW[:], A["ln_weight"])
            small(ROUTW[:], A["router_w"])
            assert n[0] == SMALL
            sp.dma_start(W0[:], A["w0"]).then_inc(moe_loaded, 16)
            sp.dma_start(W0D[:], A["w0d"]).then_inc(moe_loaded, 16)
            for c, (f, m) in enumerate(FCH):
                sp.dma_start(W1D[0:m, :, c, :], A["w2"][:, f:f + m, :].rearrange("e f d -> f e d")).then_inc(moe_loaded, 16)
            for half in range(2):
                if half:
                    sp.wait_ge(setup, 2)
                es = slice(4 * half, 4 * half + 4)
                sp.dma_start(STAGE[:, :, 0, :], A["w1"][es].rearrange("e d f -> d e f")).then_inc(stage_loaded, 16)
                sp.dma_start(STAGE[:, :, 1, :], A["w3"][es].rearrange("e d f -> d e f")).then_inc(stage_loaded, 16)

            def one_pass(i, last):
                if not last:
                    sp.wait_ge(sem["layer0"], 1)
                    sp.dma_start(XIN[:], x_t[i + 1]).then_inc(x_loaded, 16)
                for comp in range(4):
                    if comp == 0:
                        sp.wait_ge(sem["hi"], 1)
                        sp.wait_ge(sem["lo"], 1)
                    dst = (QS, KS)[comp // 2]
                    for r, low in enumerate(((0, 0, 1), (0, 1, 0))[comp // 2]):
                        src = EF if low else EH
                        for par in range(2):
                            row = 64 * par + 16 * r + 8 * (comp % 2)
                            sp.dma_start(dst[row:row + 8, :, :].bitcast(F32),
                                         src[64 * par:64 * par + 64, comp, :]).then_inc(stacked, 16)
                sp.wait_ge(sem["m2"], 2)
                for par in range(2):
                    for part in range(2):
                        row = 64 * par + SROWS + part
                        sp.dma_start(QS[row:row + 1, :, :].bitcast(F32),
                                     M2[8 * par:8 * par + 8, part, :]).then_inc(max_stacked, 16)
                sp.wait_ge(sem["out"], 1)
                sp.dma_start(y_t[i], S0[:]).then_inc(stored, 16)
                sp.sem_inc(arrived, 1)
                sp.wait_ge(released, i + 1)
                sp.sem_inc(seen, 1)

            with sp.Fori(0, B - 1) as i:
                one_pass(i, False)
            one_pass(B - 1, True)
            sp.wait_ge(stored, 16 * (B + 1))

        @block.tensor
        def _(pe):
            def signal(ins, name):
                ins.then_inc(sem[name], 1)

            def transposes(i, src, rows, bank):
                for t in range(NT):
                    ins = pe.transpose(PS[0:rows, bank, 128 * t:128 * t + 128], src[:, t, :], IDENT[:])
                signal(ins, "tp")

            def tok_matmul(bank, width, lhs, rhs, name):
                out = PS[:, bank, 0:NT * width].rearrange("p (t f) -> p t f", t=NT)
                for t in range(NT):
                    ins = pe.matmul(out[:, t, :], lhs[:, 128 * t:128 * t + 128], rhs, start=True, stop=True)
                signal(ins, name)

            pe.wait_ge(small_loaded, 16 * SMALL)
            pe.wait_ge(moe_loaded, 16 * 5)
            pe.wait_ge(setup, SETUP_V)
            pe.wait_ge(setup_pool, SETUP_P)
            pe.wait_ge(setup_act, SETUP_A)

            def layer0(i):
                pe.wait_ge(sem["xn"], 1)
                transposes(i, XN, 128, 4)
                pe.wait_ge(sem["evac"], 1)
                tok_matmul(5, 64, XNT, DOWN[:], "down")
                tok_matmul(7, E, XNT, GATEW[:], "logits")
                for k in range(E + 3):
                    if k <= E:
                        for pair, ready, used in ((0, "gpair", "gused"), (1, "lpair", "lused")):
                            if k:
                                pe.wait_ge(sem[used], k)
                            for m in range(2):
                                ins = pe.matmul(PS[:, 2 * pair + m, :], W0[:, k, 2 * pair + m, :], XNT[:],
                                                start=True, stop=True)
                            signal(ins, ready)
                    if k >= 2:
                        e = k - 2
                        pe.wait_ge(sem["a"], e + 1)
                        if e:
                            pe.wait_ge(sem["ys"], e)
                        shared = e == E
                        if shared:
                            pe.wait_ge(sem["cwT"], 1)
                        for t in range(NT):
                            out = PS[:, 6, 128 * t:128 * t + 128]
                            if shared:
                                pe.matmul(out, CWT[:, 128 * t:128 * t + 128], B0D[:], start=True, stop=False)
                            ins = pe.matmul(out, AA[:, e % 2, 128 * t:128 * t + 128], W0D[:, e, :],
                                            start=not shared, stop=True)
                        signal(ins, "y")
                    attention0(i, k)
                pe.wait_ge(sem["gelu"], 2)
                for t in range(NT):
                    for c in range(2):
                        ins = pe.matmul(PS[:, 4, 128 * t:128 * t + 128], G[:, c, 128 * t:128 * t + 128],
                                        FW2[:, c, :], start=c == 0, stop=c == 1)
                signal(ins, "ffn2")

            def attention0(i, k):
                if k == 0:
                    pe.wait_ge(sem["xi"], 1)
                    transposes(i, XI, 64, 4)
                if k == 1:
                    pe.wait_ge(sem["evac"], 2)
                    for r in range(2):
                        for g in range(4):
                            for c in range(3):
                                a = SHIFT[r] + g * GRP[r]
                                ins = pe.matmul(PS[32 * g:32 * g + 32, 5 - r, c * GRP[r]:(c + 1) * GRP[r]],
                                                WQKV[:, r, 32 * c:32 * c + 32], XIT[:, a:a + GRP[r]],
                                                start=True, stop=True)
                        signal(ins, "qkv")
                    pe.wait_ge(sem["cw"], 1)
                    for t in range(NT):
                        ins = pe.transpose(PS[0:E, 7, 128 * t:128 * t + 128], CW[:, t, :], IDENT[:])
                    signal(ins, "cwt")
                if k in CHUNK_AT:
                    for c in range(*CHUNK_AT[k]):
                        r, w, n = CHUNKS[c]
                        width = n * WIN[r] ** 2
                        pe.wait_ge(sem["prod"], c + 1)
                        if c >= 2:
                            pe.wait_ge(sem["S_sb"], c - 1)
                        else:
                            pe.wait_ge(sem["qkv_sb"], 2)
                        signal(pe.matmul(PS[:, 4 + c % 2, 0:width], HEADSUM[:], G[:, c % 2, 0:width],
                                         start=True, stop=True), "S")
                if k == 7:
                    pe.wait_ge(sem["wout"], 2)
                    for r in range(2):
                        for g in range(4):
                            a = SHIFT[r] + g * GRP[r]
                            n = min(GRP[r], T - a)
                            out = PS[32 * r:32 * r + 32, 4, :]
                            ins = pe.matmul(out[:, a:a + n], PROJ[:, r, g, :], WO[r][:, 0:n], start=True, stop=True)
                        ins = pe.matmul(out[:, 0:SHIFT[r]], PROJ[:, r, 3, :],
                                        WO[r][:, PADT - a:PADT - a + SHIFT[r]], start=True, stop=True)
                    signal(ins, "proj")
                if k == 8:
                    pe.wait_ge(sem["ppT"], 1)
                    tok_matmul(5, 128, PPT, UPW[:], "up")
                if k == 9:
                    pe.wait_ge(sem["h"], 1)
                    transposes(i, H, 128, 4)
                if k == 10:
                    pe.wait_ge(sem["evac"], 3)
                    for c in range(2):
                        signal(pe.matmul(PS[:, 5 - c, :], FW1[:, 128 * c:128 * c + 128], HT[:],
                                         start=True, stop=True), "ffn1")

            def scores_for_max(i, h, half):
                n = 2 * h + half
                if n >= 2:
                    pe.wait_ge(sem["mx"], n - 1)
                rows = slice(64 * (h % 2), 64 * (h % 2) + SROWS)
                for s in range(2):
                    t = 2 * half + s
                    ins = pe.matmul(PS[:, 2 * half + s, :], QS[rows, h // 2, 128 * t:128 * t + 128],
                                    KS[rows, h // 2, :], start=True, stop=True)
                signal(ins, "mpair")

            def ff_pair(i, c):
                e, (f, m) = c // NCH, FCH[c % NCH]
                if c:
                    pe.wait_ge(sem["fused"], c)
                for s in range(2):
                    for n, (w, x) in enumerate(((W1H, XRH), (W1H, XRL), (W1L, XRH))):
                        ins = pe.matmul(PS[0:m, 4 + s, :], w[:, e, s, f:f + m], x[:], start=n == 0, stop=n == 2)
                signal(ins, "fpair")

            def ff_down(i, e):
                pe.wait_ge(sem["fused"], NCH * (e + 1))
                if e:
                    pe.wait_ge(sem["ys1"], e)
                for c, (f, m) in enumerate(FCH):
                    for t in range(NT):
                        ins = pe.matmul(PS[:, 6, 128 * t:128 * t + 128],
                                        A4[0:m, (NCH * e + c) % 4, 128 * t:128 * t + 128], W1D[0:m, e, c, :],
                                        start=c == 0 and t == 0, stop=c == NCH - 1 and t == NT - 1,
                                        skip_group_check=True)
                signal(ins, "y1")

            def layer1(i):
                pe.wait_ge(sem["xn"], 2)
                transposes(i, X1, 128, 0)
                pe.wait_ge(sem["h"], 2)
                transposes(i, H, 128, 1)
                pe.wait_ge(sem["evac"], 4)
                for n in range(2):
                    signal(pe.matmul(PS[:, 2 + n, :], WATT[:, n, :], XNT[:], start=True, stop=True), "qk")
                tok_matmul(4, 128, XNT, WATT[:, 2, :], "v")
                pe.wait_ge(sem["evac"], 5)
                tok_matmul(7, E, HT, ROUTW[:], "logits")
                pe.wait_ge(sem["v_sb"], 1)
                pe.wait_ge(sem["xrh"], 2)
                for what, n in plan1():
                    if what == "chunk":
                        ff_pair(i, n)
                    elif what == "down":
                        ff_down(i, n)
                    else:
                        if n == 0:
                            pe.wait_ge(stacked, 16 * 24)
                        scores_for_max(i, n // 2, n % 2)
                pe.wait_ge(sem["mx"], 32)
                for t in range(NT):
                    ins = pe.transpose(PS[0:H1, 7, 128 * t:128 * t + 128], MX[:, t, :], IDENT[:])
                signal(ins, "mt")
                ff_down(i, E - 1)
                pe.wait_ge(max_stacked, 16 * 4)
                for n in range(4 * NT + 2):
                    if n < 4 * NT:
                        k = n % NT
                        for half in range(2):
                            if n:
                                pe.wait_ge(sem["ex"], 2 * n - 1 + half)
                            for a in range(2 * half, 2 * half + 2):
                                h = n // NT * 4 + a
                                rows = slice(64 * (h % 2), 64 * (h % 2) + SROWS + 2)
                                ins = pe.matmul(PS[:, a, :], KS[rows, h // 2, 128 * k:128 * k + 128],
                                                QS[rows, h // 2, :], start=True, stop=True)
                            signal(ins, "st")
                    if 1 <= n <= 4 * NT:
                        g, k = divmod(n - 1, NT)
                        pe.wait_ge(sem["ex"], 2 * n)
                        if n == 1:
                            pe.wait_ge(sem["m2"], 2)
                        if n == 5:
                            pe.wait_ge(sem["ys1"], E)
                        if g >= 2 and k == 0:
                            pe.wait_ge(sem["oe"], g - 1)
                        for a in range(4):
                            at = (4 * g + a) * (HD1 + 1)
                            ins = pe.matmul(PS[32 * a:32 * a + 32, 7 - g % 2, :], V[:, k, at:at + 32],
                                            P[:, (n - 1) % 2, a, :], start=k == 0, stop=k == NT - 1)
                        signal(ins, "pv")
                    if n >= 2 and (n - 2) % NT == NT - 1:
                        g = (n - 2) // NT
                        pe.wait_ge(sem["oe"], g + 1)
                        if g >= 2:
                            pe.wait_ge(sem["ot"], g - 1)
                        for t in range(NT):
                            ins = pe.transpose(PS[:, 4 + g % 2, 128 * t:128 * t + 128],
                                               A4[:, g % 2, 128 * t:128 * t + 128], IDENT[:])
                        signal(ins, "oq")
                pe.wait_ge(sem["ot"], 4)
                transposes(i, H, 128, 0)
                pe.wait_ge(sem["evac"], 6)
                tok_matmul(1, 128, HT, WATT[:, 3, :], "wo")

            with pe.Fori(0, B) as i:
                layer0(i)
                layer1(i)
                end_pass(pe, i)

        @block.scalar
        def _(act):
            def go(name, *a, **k):
                act.activation(*a, **k).then_inc(sem[name], 1)

            for n in range(2):
                act.wait_ge(stage_loaded, 32 * (n + 1))
                act.activation(W1H[:, 4 * n:4 * n + 4], STAGE, ACT.Copy).then_inc(setup_act, 1)
            act.wait_ge(small_loaded, 16 * SMALL)
            act.wait_ge(setup_pool, SETUP_P)
            act.wait_ge(setup, SETUP_H)
            act.activation(PB[:, 3:4], PB[:, 1:2], ACT.Sin).then_inc(setup_act, 1)
            act.activation(PB[:, 4:5], PB[:, 2:3], ACT.Sin).then_inc(setup_act, 1)

            def layer0(i):
                act.wait_ge(sem["tp"], 1)
                go("evac", XNT[:], PS[:, 4, :], ACT.Copy)
                for k in range(E + 3):
                    if k <= E:
                        for s, (ready, used, done) in enumerate((("gpair", "gused", "h3g"), ("lpair", "lused", "h3l"))):
                            act.wait_ge(sem[ready], k + 1)
                            if k:
                                act.wait_ge(sem[used], k)
                            go(done, H3[:, s, :], PS[:, 2 * s + 1, :], ACT.Identity, bias=B0[:, k, 2 * s + 1:2 * s + 2])
                        act.wait_ge(sem["gg"], k + 1)
                        if k >= 2:
                            act.wait_ge(sem["a"], k - 1)
                        go("th", TH[:, k % 2, :], UL[:, k % 2, 0, :], ACT.Silu, scale=ALPHA)
                    if k >= 2:
                        e = k - 2
                        act.wait_ge(sem["y"], e + 1)
                        if e == 0:
                            act.wait_ge(stored, 16 * (i + 1))
                        if e:
                            act.wait_ge(sem["acc"], e)
                        weighted(e, "ys", CW[:, :, e:e + 1] if e < E else None)
                    attention0(i, k)

            def weighted(e, name, gate):
                for t in range(NT):
                    ins = act.activation(YS[:, t, :], PS[:, 6, 128 * t:128 * t + 128], ACT.Copy,
                                         scale=1.0 / ALPHA if gate is None else gate[:, t, :])
                ins.then_inc(sem[name], 1)

            def attention0(i, k):
                if k == 0:
                    act.wait_ge(sem["tp"], 2)
                    act.activation(XIT[:, 0:T], PS[0:64, 4, :], ACT.Copy, scale=N1W[:, 0:1])
                    go("evac", XIT[:, PADT:PADT + SHIFT[1]], PS[0:64, 4, 0:SHIFT[1]], ACT.Copy, scale=N1W[:, 0:1])
                    act.wait_ge(sem["lsub"], 1)
                    go("lexp", RT[:, 1], RT[:, 0], ACT.Exp)
                if k == 1:
                    for r in range(2):
                        act.wait_ge(sem["qkv"], r + 1)
                        for c in range(3):
                            ins = act.activation(QKV[r][:, c, :], PS[:, 5 - r, c * GRP[r]:(c + 1) * GRP[r]],
                                                 ACT.Identity, bias=QKVB[:, r, c:c + 1], scale=0.5 if c == 0 else 1.0)
                        ins.then_inc(sem["qkv_sb"], 1)
                    act.wait_ge(sem["cwt"], 1)
                    go("cwT", CWT, PS[0:E, 7, :], ACT.Copy, scale=ALPHA ** 2)
                if k in (3, 5):
                    r = k // 2 - 1
                    act.wait_ge(sem["wsub"], r + 1)
                    s = SC[:, S_AT[r]:S_AT[r] + GRP[r] * WIN[r]]
                    go("wexp", s, s, ACT.Exp)
                if k == 7:
                    act.wait_ge(sem["proj"], 1)
                    go("ppT", PPT, PS[0:64, 4, :], ACT.Identity, bias=PROJB[:, 0:1])
                if k == 8:
                    act.wait_ge(sem["x1"], 1)
                    square_sums()
                if k == 9:
                    act.wait_ge(sem["tp"], 3)
                    go("evac", HT[:], PS[:, 4, :], ACT.Copy, scale=N2W[:, 0:1])
                if k == 10:
                    for c in range(2):
                        act.wait_ge(sem["ffn1"], c + 1)
                        go("gelu", G[:, c, :], PS[:, 5 - c, :], ACT.Gelu, bias=FB1[:, c:c + 1])

            def square_sums():
                for t in range(NT):
                    ins = act.activation(H[:, t, :], X1[:, t, :], ACT.Square, accum_out=SQ[:, t:t + 1])
                ins.then_inc(sem["sqs"], 1)

            def layer1(i):
                act.wait_ge(sem["acc"], E + 1)
                go("silu", TH[:, 0, :], ACC[:].rearrange("p t f -> p (t f)"), ACT.Tanh, scale=0.5)
                act.wait_ge(sem["xn"], 2)
                square_sums()
                act.wait_ge(sem["tp"], 4)
                go("evac", XNT[:], PS[:, 0, :], ACT.Copy)
                act.wait_ge(sem["tp"], 5)
                go("evac", HT[:], PS[:, 1, :], ACT.Copy, scale=LNW[:, 0:1])
                for n in range(2):
                    act.wait_ge(sem["qk"], n + 1)
                    go("qabs", AA[:, n, :], PS[:, 2 + n, :], ACT.Abs)
                for n in range(2):
                    act.wait_ge(sem["qabs"], n + 1)
                    go("qexp", AA[:, n, :], AA[:, n, :], ACT.Exp, scale=-1.0)
                for n in range(2):
                    act.wait_ge(sem["qexp"], n + 1)
                    go("qln", AA[:, n, :], AA[:, n, :], ACT.Ln, bias=1.0)
                act.wait_ge(sem["v"], 1)
                go("v_sb", V[:, :, 0:H1 * (HD1 + 1)].rearrange("p t (h d) -> p t h d", h=H1)[:, :, :, 0:HD1], PS[:, 4, :].rearrange("p (t h d) -> p t h d", t=NT, h=H1), ACT.Copy)
                act.wait_ge(sem["lsub"], 2)
                go("lexp", RT[:, 1], RT[:, 0], ACT.Exp)
                for what, n in plan1() + [("down", E - 1)]:
                    if what == "chunk":
                        m = FCH[n % NCH][1]
                        act.wait_ge(sem["fpair"], n + 1)
                        if n == 0:
                            act.wait_ge(sem["emb_cos"], 2)
                            act.wait_ge(sem["emb_sin"], 2)
                        if n >= 2:
                            act.wait_ge(sem["fused"], n - 1)
                        go("fth", TH[0:m, n % 2, :], PS[0:m, 4, :], ACT.Silu)
                    elif what == "down":
                        act.wait_ge(sem["y1"], n + 1)
                        if n:
                            act.wait_ge(sem["acc1"], n)
                        weighted(n, "ys1", CW[:, :, n:n + 1])
                for n in range(4 * NT):
                    for half in range(2):
                        act.wait_ge(sem["st"], 2 * n + half + 1)
                        if n >= 2:
                            act.wait_ge(sem["pv"], n - 1)
                        go("ex", P[:, n % 2, 2 * half:2 * half + 2, :], PS[:, 2 * half:2 * half + 2, :], ACT.Exp,
                           scale=HD1 ** -0.5)
                act.wait_ge(sem["tp"], 6)
                go("evac", HT[:], PS[:, 0, :], ACT.Copy)
                act.wait_ge(sem["acc1"], E)
                go("silu", TH[:, 0, :], ACC[:].rearrange("p t f -> p (t f)"), ACT.Tanh, scale=0.5)

            with act.Fori(0, B) as i:
                layer0(i)
                layer1(i)
                end_pass(act, i)

        @block.gpsimd
        def _(pool):
            n = [0]

            def init(ins):
                n[0] += 1
                ins.then_inc(setup_pool, 1)
                pool.wait_ge(setup_pool, n[0])

            pool.memset(WQKV[:], 0.0).then_inc(zeroed, 1)
            pool.wait_ge(zeroed, 1)
            pool.memset(PROJ[:], 0.0).then_inc(zeroed, 1)
            pool.wait_ge(zeroed, 2)
            init(pool.memset(NHALF[:], -0.5))
            for r in range(2):
                init(pool.memset(MASK[r][96:128], 0.0))
            init(pool.memset(XIT[:, T:XIT_W], 0.0))
            init(pool.memset(V[:], 1.0))
            for row in (32, 96):
                init(pool.memset(KS[row:row + SROWS - 32 + 2].bitcast(F32), 1.0))
            for r in range(2):
                w, s = WIN[r], SHIFT[r]
                init(pool.memset(MASK[r][96:128, 0:w - s, w - s:w], -100.0))
                init(pool.memset(MASK[r][96:128, w - s:w, 0:w - s], -100.0))
            pool.wait_ge(small_loaded, 16 * SMALL)
            for r in range(2):
                w = WIN[r]
                for q in range(w):
                    init(pool.tensor_copy(BIAS[r][:, q, :], RPB[r][:, w - 1 - q:2 * w - 1 - q]))
            assert n[0] == SETUP_P, n[0]
            pool.wait_ge(setup, SETUP_V)
            done = {}

            def go(name, ins):
                done[name] = done.get(name, 0) + 1
                ins.then_inc(sem[name], 1)
                pool.wait_ge(sem[name], done[name])

            def rsqrt(i, k, src, scale, eps):
                go("pstep", pool.tensor_scalar(VAR[:], src, scale, eps, ALU.mult, ALU.add))
                go("rstd", pool.tensor_tensor(RSTD[:], VAR[:], NHALF[:], ALU.pow))

            def layer0(i):
                pool.wait_ge(sem["stats"], 1)
                rsqrt(i, 1, MV[:, :, 1], 1.0, 1e-5)
                pool.wait_ge(sem["xn"], 1)
                go("xb", pool.tensor_tensor(X1[:], XN[:], bc(UPB[:], [128, NT, 128], 1), ALU.add))
                pool.wait_ge(sem["xi_sq"], 1)
                rsqrt(i, 2, SQ[:], 1.0 / 64, 1e-6)
                for k in range(E + 3):
                    if k <= E:
                        v = UL[:, k % 2, 1, :]
                        pool.wait_ge(sem["lused"], k + 1)
                        go("lc", pool.tensor_scalar(v, v, LIMIT, -LIMIT, ALU.min, ALU.max))
                    if k >= 2:
                        e = k - 2
                        pool.wait_ge(sem["ys"], e + 1)
                        if e:
                            go("acc", pool.tensor_tensor(ACC[:], YS[:], ACC[:], ALU.add))
                        else:
                            go("acc", pool.tensor_tensor(ACC[:], YS[:], bc(SB0D[:], [128, NT, 128], 1), ALU.add))
                    for r, (k_sub, k_pv) in enumerate(((2, 4), (4, 6))):
                        w = WIN[r]
                        s = SC[:, S_AT[r]:S_AT[r] + GRP[r] * w].rearrange("p (n k) -> p n k", k=w)
                        if k == k_sub:
                            pool.wait_ge(sem["wmax"], r + 1)
                            go("wsub", pool.tensor_tensor(s, s, bc(WM[r][:], [128, GRP[r], w], 2), ALU.subtract))
                        if k == k_pv:
                            pool.wait_ge(sem["wsum"], r + 1)
                            s = s.rearrange("p (w q) k -> p w q k", q=w)
                            v = QKV[r][:, 2, :].rearrange("p (w k) -> p w k", k=w)
                            go("wpv", pool.tensor_tensor(s, s, bc(v, [128, NWIN[r], w, w], 2), ALU.mult))
                    if k == 8:
                        pool.wait_ge(sem["sqs"], 1)
                        rsqrt(i, 3, SQ[:], 1.0 / 128, 1e-6)
                    if k == 9:
                        pool.wait_ge(sem["h"], 1)
                        go("xb", pool.tensor_tensor(X1[:], X1[:], bc(FB2[:], [128, NT, 128], 1), ALU.add))

            def layer1(i):
                pool.wait_ge(sem["stats"], 2)
                rsqrt(i, 4, MV[:, :, 1], 1.0, 1e-5)
                pool.wait_ge(sem["sqs"], 2)
                rsqrt(i, 5, SQ[:], 1.0 / 128, 1e-5)
                for n in range(2):
                    pool.wait_ge(sem["mag"], n + 1)
                    go("emb_sin", pool.tensor_tensor(EF[:, 2 * n + 1, :], TH[:, n, :], TRIG[:, 2 * n + 1, :], ALU.mult))
                for e in range(E):
                    pool.wait_ge(sem["ys1"], e + 1)
                    if e:
                        go("acc1", pool.tensor_tensor(ACC[:], YS[:], ACC[:], ALU.add))
                    else:
                        go("acc1", pool.tensor_copy(ACC[:], YS[:]))

            with pool.Fori(0, B) as i:
                layer0(i)
                layer1(i)
                pool.wait_ge(sem["out"], 1)
                pool.wait_ge(arrived, 4)
                pool.sem_clear(counted)
                pool.sem_inc(released, 1)

        @block.vector
        def _(dve):
            count = [0]

            def go(name, ins):
                ins.then_inc(sem[name], 1)

            def step(i, ins):
                count[0] += 1
                ins.then_inc(sem["step"], 1)
                dve.wait_ge(sem["step"], count[0])

            n = [0]

            def init(ins):
                n[0] += 1
                ins.then_inc(setup, 1)
                dve.wait_ge(setup, n[0])

            for half in range(2):
                dve.wait_ge(setup_act, half + 1)
                hi = W1H[:, 4 * half:4 * half + 4]
                init(dve.tensor_tensor(W1L[:, 4 * half:4 * half + 4], STAGE, hi.bitcast(F32), ALU.subtract))
                if half == 0:
                    init(dve.memset(PB[:, 5:6], 0.0))
            dve.wait_ge(small_loaded, 16 * SMALL)
            pi = float(np.pi)
            init(dve.tensor_scalar(PB[:, 0:1], POPEB[:], 0.0, -2.0 * pi, ALU.min, ALU.max))
            init(dve.tensor_scalar(PB[:, 1:2], PB[:, 0:1], pi, 0.5, ALU.add, ALU.mult))
            init(dve.scalar_tensor_tensor(PB[:, 2:3], PB[:, 1:2], -1.0, PB[:, 1:2], ALU.mult, ALU.min))
            init(dve.tensor_scalar(PB[:, 2:3], PB[:, 2:3], pi / 2, None, ALU.add))
            assert n[0] == SETUP_H
            dve.wait_ge(setup_act, SETUP_A)
            init(dve.scalar_tensor_tensor(PB[:, 0:1], PB[:, 3:4], 2.0, PB[:, 4:5], ALU.mult, ALU.mult))
            init(dve.scalar_tensor_tensor(PB[:, 1:2], PB[:, 3:4], 2.0, PB[:, 3:4], ALU.mult, ALU.mult))
            init(dve.tensor_scalar(PB[:, 1:2], PB[:, 1:2], 1.0, None, ALU.subtract))
            init(dve.tensor_scalar(PB[:, 2:3], PB[:, 0:1], -1.0, None, ALU.mult))
            for m, (first, second) in enumerate(((0, 0), (1, 2))):
                init(dve.tensor_scalar(TRIG[:, 2 + m, :], TRIG[:, m, :], PB[:, 1:2], None, ALU.mult))
                init(dve.scalar_tensor_tensor(TRIG[:, 2 + m, :], TRIG[:, 1 - m, :], PB[:, second:second + 1],
                                              TRIG[:, 2 + m, :], ALU.mult, ALU.add))
            init(dve.tensor_scalar(QKVB[:, :, 0:1], QKVB[:, :, 0:1], 0.5, None, ALU.mult))
            assert n[0] == SETUP_V, n[0]
            dve.wait_ge(setup_pool, SETUP_P)
            dve.wait_ge(moe_loaded, 16 * 5)

            def layernorm(i, k, src, dst):
                for t in range(NT):
                    ins = dve.bn_stats(STAT[:, t, :], src[:, t, :])
                step(i, ins)
                for t in range(NT):
                    ins = dve.bn_aggr(MV[:, t, :], STAT[:, t, :])
                go("stats", ins)
                dve.wait_ge(sem["stats"], k)
                dve.wait_ge(sem["rstd"], 3 * k - 2)
                for t in range(NT):
                    ins = dve.tensor_scalar(dst[:, t, :], src[:, t, :], MV[:, t, 0:1], RSTD[:, t:t + 1],
                                            ALU.subtract, ALU.mult)
                go("xn", ins)

            def routing_logits(i, k):
                logits = ntok(PS[:, 7, 0:NT * E])
                dve.wait_ge(sem["logits"], k)
                step(i, dve.tensor_reduce(RS[:, 0], logits, AX.X, ALU.max))
                go("lsub", dve.tensor_tensor(RT[:, 0], logits, bc(RS[:, 0], [128, NT, E], 2), ALU.subtract))

            def routing(i, k, biased, scale):
                s4 = [128, NT, E]
                dve.wait_ge(sem["lexp"], k)
                step(i, dve.tensor_reduce(RS[:, 1], RT[:, 1], AX.X, ALU.add))
                step(i, dve.reciprocal(RS[:, 2], RS[:, 1]))
                step(i, dve.tensor_tensor(RT[:, 1], RT[:, 1], bc(RS[:, 2], s4, 2), ALU.mult))
                key = 1
                if biased:
                    key = 2
                    step(i, dve.tensor_tensor(RT[:, 2], RT[:, 1], bc(GATEB[:], s4, 1), ALU.add))
                for pick in range(2):
                    hot = RT[:, 3 + pick]
                    step(i, dve.tensor_reduce(RS[:, 3], RT[:, key], AX.X, ALU.max))
                    step(i, dve.tensor_tensor(hot, RT[:, key], bc(RS[:, 3], s4, 2), ALU.is_equal))
                    step(i, dve.tensor_tensor(hot, hot, bc(REV[:], s4, 1), ALU.mult))
                    step(i, dve.tensor_reduce(RS[:, 3], hot, AX.X, ALU.max))
                    step(i, dve.tensor_tensor(hot, hot, bc(RS[:, 3], s4, 2), ALU.is_equal))
                    if pick == 0:
                        step(i, dve.scalar_tensor_tensor(RT[:, 5], hot, -1e30, RT[:, key], ALU.mult, ALU.add))
                        key = 5
                step(i, dve.tensor_tensor(RT[:, 6], RT[:, 3], RT[:, 4], ALU.add))
                go("cw", dve.scalar_tensor_tensor(CW[:], RT[:, 6], scale, RT[:, 1], ALU.mult, ALU.mult))
                dve.wait_ge(sem["cw"], k)

            def layer0(i):
                dve.wait_ge(x_loaded, 16 * (i + 1))
                layernorm(i, 1, XIN, XN)
                for k in range(E + 3):
                    if k <= E:
                        for s, (pair, h3, used) in enumerate((("gpair", "h3g", "gused"), ("lpair", "h3l", "lused"))):
                            dve.wait_ge(sem[pair], k + 1)
                            dve.wait_ge(sem[h3], k + 1)
                            if k >= 2:
                                dve.wait_ge(sem["a"], k - 1)
                            go(used, dve.scalar_tensor_tensor(UL[:, k % 2, s, :], PS[:, 2 * s, :],
                                                              B0[:, k, 2 * s:2 * s + 1], H3[:, s, :], ALU.add, ALU.mult))
                        dve.wait_ge(sem["gused"], k + 1)
                        u = UL[:, k % 2, 0, :]
                        go("gg", dve.tensor_scalar(u, u, LIMIT, None, ALU.min))
                    if 1 <= k <= E + 1:
                        e = k - 1
                        th = TH[:, e % 2, :]
                        dve.wait_ge(sem["th"], e + 1)
                        dve.wait_ge(sem["lc"], e + 1)
                        if e >= 2:
                            dve.wait_ge(sem["y"], e - 1)
                        go("a", dve.scalar_tensor_tensor(AA[:, e % 2, :], UL[:, e % 2, 1, :], 1.0, th, ALU.add, ALU.mult))
                    attention0(i, k)
                dve.wait_ge(sem["ffn2"], 1)
                dve.wait_ge(sem["xb"], 2)
                dve.wait_ge(sem["acc"], E + 1)
                step(i, dve.tensor_tensor(S0[:], ntok(PS[:, 4, :]), X1[:], ALU.add))
                dve.wait_ge(sem["silu"], 1)
                step(i, dve.scalar_tensor_tensor(ACC[:], ntok(TH[:, 0, :]), 1.0, ACC[:], ALU.add, ALU.mult))
                step(i, dve.scalar_tensor_tensor(ACC[:], ACC[:], 0.5, S0[:], ALU.mult, ALU.mult))
                go("layer0", dve.tensor_tensor(XA[:], ACC[:], XIN[:], ALU.add))
                dve.wait_ge(sem["layer0"], 1)

            def attention0(i, k):
                if k == 0:
                    dve.wait_ge(sem["down"], 1)
                    step(i, dve.tensor_tensor(XI[:], ntok(PS[:, 5, 0:256]), bc(DOWNB[:], [128, NT, 64], 1), ALU.add))
                    step(i, dve.tensor_tensor(H[:, :, 0:64], XI[:], XI[:], ALU.mult))
                    go("xi_sq", dve.tensor_reduce(SQ[:], H[:, :, 0:64], AX.X, ALU.add))
                    dve.wait_ge(sem["rstd"], 2)
                    go("xi", dve.tensor_tensor(XI[:], XI[:], bc(RSTD[:], [128, NT, 64], 2), ALU.mult))
                    routing_logits(i, 1)
                    routing(i, 1, True, 1.0 / ALPHA)
                if k in CHUNK_AT:
                    first, last = CHUNK_AT[k]
                    if k == 2:
                        dve.wait_ge(sem["qkv_sb"], 2)
                    for c in range(first, last + 2):
                        if c < last:
                            r, w, m = CHUNKS[c]
                            q, kk = (QKV[r][:, j, :].rearrange("p (w q) -> p w q", q=WIN[r])[:, w:w + m] for j in range(2))
                            full = [128, m, WIN[r], WIN[r]]
                            if c >= 2:
                                dve.wait_ge(sem["S"], c - 1)
                            dst = G[:, c % 2, 0:m * WIN[r] ** 2].rearrange("p (w q k) -> p w q k", w=m, q=WIN[r])
                            go("prod", dve.tensor_tensor(dst, bc(q, full, 3), bc(kk, full, 2), ALU.mult))
                        if c - 2 >= first:
                            r, w, m = CHUNKS[c - 2]
                            a = WIN[r] ** 2
                            dve.wait_ge(sem["S"], c - 1)
                            dst = SC[:, S_AT[r] + w * a:S_AT[r] + (w + m) * a].rearrange("p (w a) -> p w a", w=m)
                            src = PS[:, 4 + c % 2, 0:m * a].rearrange("p (w a) -> p w a", w=m)
                            bias = BIAS[r][:].rearrange("p q k -> p (q k)")
                            go("S_sb", dve.tensor_tensor(dst, src, bc(bias, [128, m, a], 1), ALU.add))
                            dve.wait_ge(sem["S_sb"], c - 1)
                if k in (2, 4):
                    r = k // 2 - 1
                    w, lastw = WIN[r], (PADT // WIN[r] - 1) % NWIN[r]
                    s = SC[96:128, S_AT[r] + lastw * w * w:S_AT[r] + (lastw + 1) * w * w]
                    step(i, dve.tensor_tensor(s, s, MASK[r][96:128].rearrange("p q k -> p (q k)"), ALU.add))
                    s = SC[:, S_AT[r]:S_AT[r] + GRP[r] * w].rearrange("p (n k) -> p n k", k=w)
                    go("wmax", dve.tensor_reduce(WM[r][:], s, AX.X, ALU.max))
                if k in (4, 6):
                    r = k // 2 - 2
                    s = SC[:, S_AT[r]:S_AT[r] + GRP[r] * WIN[r]].rearrange("p (n k) -> p n k", k=WIN[r])
                    dve.wait_ge(sem["wexp"], r + 1)
                    go("wsum", dve.tensor_reduce(WM[r][:], s, AX.X, ALU.add))
                    dve.wait_ge(sem["wsum"], r + 1)
                    step(i, dve.reciprocal(WM[r][:], WM[r][:]))
                if k in (5, 7):
                    r = k // 2 - 2
                    s = SC[:, S_AT[r]:S_AT[r] + GRP[r] * WIN[r]].rearrange("p (n k) -> p n k", k=WIN[r])
                    dve.wait_ge(sem["wpv"], r + 1)
                    step(i, dve.tensor_reduce(WO[r][:], s, AX.X, ALU.add))
                    go("wout", dve.tensor_tensor(WO[r][:], WO[r][:], WM[r][:], ALU.mult))
                if k == 8:
                    dve.wait_ge(sem["up"], 1)
                    dve.wait_ge(sem["xb"], 1)
                    go("x1", dve.tensor_tensor(X1[:], ntok(PS[:, 5, :]), X1[:], ALU.add))
                    dve.wait_ge(sem["x1"], 1)
                    dve.wait_ge(sem["rstd"], 3)
                    go("h", dve.tensor_tensor(H[:], X1[:], bc(RSTD[:], [128, NT, 128], 2), ALU.mult))

            def chunk(i, c):
                m = FCH[c % NCH][1]
                th = TH[0:m, c % 2, :]
                dve.wait_ge(sem["fpair"], c + 1)
                dve.wait_ge(sem["fth"], c + 1)
                if c >= 4:
                    dve.wait_ge(sem["y1"], (c - 4) // NCH + 1)
                go("fused", dve.tensor_tensor(A4[0:m, c % 4, :], PS[0:m, 5, :], th, ALU.mult))

            def row_max(i, h, half):
                dve.wait_ge(sem["mpair"], 2 * h + half + 1)
                go("mx", dve.tensor_reduce(MX[:, 2 * half:2 * half + 2, 8 * (h % 2) + h // 2], PS[:, 2 * half:2 * half + 2, :], AX.X, ALU.max))

            def layer1(i):
                layernorm(i, 2, XA, X1)
                dve.wait_ge(sem["xn"], 2)
                dve.wait_ge(sem["rstd"], 5)
                go("h", dve.tensor_tensor(H[:], X1[:], bc(RSTD[:], [128, NT, 128], 2), ALU.mult))
                dve.wait_ge(sem["evac"], 5)
                go("xrh", dve.tensor_copy(XRH[:], HT[:]))
                dve.wait_ge(sem["xrh"], 1)
                go("xrh", dve.tensor_tensor(XRL[:], HT[:], XRH[:].bitcast(F32), ALU.subtract))
                routing_logits(i, 2)
                for n in range(2):
                    dve.wait_ge(sem["qln"], n + 1)
                    go("mag", dve.scalar_tensor_tensor(TH[:, n, :], PS[:, 2 + n, :], 0.0, AA[:, n, :], ALU.max, ALU.add))
                for n in range(2):
                    dve.wait_ge(sem["mag"], n + 1)
                    go("emb_cos", dve.tensor_tensor(EF[:, 2 * n, :], TH[:, n, :], TRIG[:, 2 * n, :], ALU.mult))
                dve.wait_ge(sem["emb_cos"], 2)
                dve.wait_ge(sem["emb_sin"], 2)
                go("hi", dve.tensor_copy(EH.bitcast(F32R), EF))
                dve.wait_ge(sem["hi"], 1)
                go("lo", dve.tensor_tensor(EF, EF, EH, ALU.subtract))
                routing(i, 2, False, 1.0)
                for what, n in plan1():
                    if what == "chunk":
                        chunk(i, n)
                    elif what == "max":
                        row_max(i, n // 2, n % 2)
                dve.wait_ge(sem["mt"], 1)
                go("m2", dve.tensor_scalar(M2[:, 0, :].bitcast(F32R), PS[0:H1, 7, :], -1.0, None, ALU.mult))
                dve.wait_ge(sem["m2"], 1)
                go("m2", dve.scalar_tensor_tensor(M2[:, 1, :].bitcast(F32R), PS[0:H1, 7, :], -1.0, M2[:, 0, :],
                                                  ALU.mult, ALU.subtract))
                for g in range(4):
                    dve.wait_ge(sem["pv"], NT * (g + 1))
                    if g == 0:
                        dve.wait_ge(sem["y1"], E)
                    if g >= 2:
                        dve.wait_ge(sem["oq"], g - 1)
                    go("oe", dve.tensor_copy(A4[:, g % 2, :], PS[:, 7 - g % 2, :]))
                    dve.wait_ge(sem["oq"], g + 1)
                    o = PS[:, 4 + g % 2, :].rearrange("p (t a r) -> p t a r", t=NT, a=4)
                    den = DEN[:, g, :].rearrange("p (t a) -> p t a", t=NT)
                    step(i, dve.reciprocal(den, o[:, :, :, HD1]))
                    dst = H[:].rearrange("p t (h d) -> p t h d", h=H1)[:, :, 4 * g:4 * g + 4]
                    go("ot", dve.tensor_tensor(dst, o[:, :, :, 0:HD1], bc(den, [128, NT, 4, HD1], 3), ALU.mult))
                dve.wait_ge(sem["silu"], 2)
                step(i, dve.scalar_tensor_tensor(ACC[:], ntok(TH[:, 0, :]), 1.0, ACC[:], ALU.add, ALU.mult))
                dve.wait_ge(sem["wo"], 1)
                step(i, dve.scalar_tensor_tensor(ACC[:], ACC[:], 0.5, ntok(PS[:, 1, :]), ALU.mult, ALU.mult))
                go("out", dve.tensor_tensor(S0[:], ACC[:], XA[:], ALU.add))

            with dve.Fori(0, B) as i:
                layer0(i)
                layer1(i)
                end_pass(dve, i)


def kernel(**inputs):
    import concourse.bacc as bacc
    from concourse.bass_utils import run_bass_kernel_spmd

    g = {n: np.asarray(v) for n, v in inputs.items()}
    dense = np.ascontiguousarray
    w1 = np.concatenate([g["L0_ffn_w1"], g["L0_ffn_sw1"][None]])
    w3 = np.concatenate([g["L0_ffn_w3"], g["L0_ffn_sw3"][None]])
    b1 = np.concatenate([g["L0_ffn_b1"], g["L0_ffn_sb1"][None]])
    b3 = np.concatenate([g["L0_ffn_b3"], g["L0_ffn_sb3"][None]])
    w0 = np.stack([w1[:, ::2], w3[:, ::2], w1[:, 1::2], w3[:, 1::2]], 1).transpose(3, 0, 1, 2)
    b0 = np.stack([b1[:, ::2], b3[:, ::2], b1[:, 1::2], b3[:, 1::2]], 1).transpose(2, 0, 1)
    w0d = np.concatenate([g["L0_ffn_w2"], g["L0_ffn_sw2"][None]]).transpose(2, 0, 1)
    order = np.array([(2 * j + par) * HD1 + d for par in range(2) for d in range(HD1) for j in range(8)])
    watt = np.stack([g["L1_attn_wq"].T[:, order], g["L1_attn_wk"].T[:, order],
                     g["L1_attn_wv"].T, g["L1_attn_wo"].T], 1)
    inv = np.float32(10000.0) ** (-(np.arange(HD1, dtype=np.float32) / np.float32(HD1)))
    freq = np.arange(T, dtype=np.float32)[None, :] * inv.astype(np.float32)[:, None]
    freq = freq[order % HD1].astype(np.float64)
    trig = np.stack([np.cos(freq), np.sin(freq)], 1).astype(np.float32)
    arrays = {
        "x": g["L0_attn_x"].reshape(B * T, D),
        "ident": np.eye(128, dtype=np.float32),
        "headsum": np.kron(np.eye(32, dtype=np.float32), np.ones((4, 4), np.float32)),
        "rev": np.tile(np.arange(E, 0, -1, dtype=np.float32), (128, 1)),
        "trig": trig, "w0": w0, "b0": b0, "w0d": w0d, "watt": watt,
        "rpb1": np.repeat(g["L0_attn_rpb1"][::-1].T, 4, 0), "rpb2": np.repeat(g["L0_attn_rpb2"][::-1].T, 4, 0),
        "gate_w": g["L0_ffn_gate_w"].T, "gate_b": g["L0_ffn_gate_b"], "b2": g["L0_ffn_b2"], "sb2": g["L0_ffn_sb2"],
        "pope_bias": g["L1_attn_pope_bias"].reshape(-1)[order],
        "ln_weight": g["L1_ffn_ln_weight"], "router_w": g["L1_ffn_router_w"],
        "w1": g["L1_ffn_w1"], "w3": g["L1_ffn_w3"], "w2": g["L1_ffn_w2"],
    }
    for n in ("down_w", "down_b", "up_w", "up_b", "norm1_w", "norm2_w", "qkv1_w", "qkv1_b", "proj1_w", "proj1_b",
              "qkv2_w", "qkv2_b", "proj2_w", "proj2_b", "ffn_w1", "ffn_b1", "ffn_w2", "ffn_b2"):
        arrays[n] = g[f"L0_attn_{n}"]
    for n, width in (("qkv1_b", 3), ("qkv2_b", 3), ("ffn_b1", 2), ("norm1_w", 1), ("norm2_w", 1), ("proj1_b", 1),
                     ("proj2_b", 1), ("pope_bias", 1), ("ln_weight", 1)):
        arrays[n] = arrays[n].reshape(width, -1).T
    nc = bacc.Bacc("TRN2", target_bir_lowering=False, num_devices=1)
    ins, aps = {}, {}
    for n, a in arrays.items():
        ins[f"in_{n}"] = dense(a)
        aps[n] = nc.dram_tensor(f"in_{n}", a.shape, mybir.dt.from_np(a.dtype), kind="ExternalInput").ap()
    aps["y"] = nc.dram_tensor("out_y", (B * T, D), F32, kind="ExternalOutput").ap()
    build(nc, aps)
    r = run_bass_kernel_spmd(nc, [ins], core_ids=[0])
    return r.results[0]["out_y"].reshape(B, T, D)
```

```python
from contextlib import ExitStack

import numpy as np
import concourse.bass as bass
from concourse import mybir

F32 = mybir.dt.float32
F32R = mybir.dt.float32r
ALU = mybir.AluOpType
ACT = mybir.ActivationFunctionType
AX = mybir.AxisListType

B, T, D = 8, 512, 128
FIRST = -1
NT = T // 128
E = 8
WIN = (10, 20)
SHIFT = (5, 10)
NWIN = (13, 7)
GRP = (WIN[0] * NWIN[0], WIN[1] * NWIN[1])
PADT = 520
XIT_W = SHIFT[1] + 4 * GRP[1]
CHUNKS = [(1, w, 1) for w in range(NWIN[1])] + [(0, 0, 5), (0, 5, 5), (0, 10, 3)]
CHUNK_AT = {5: (0, 2), 6: (2, 4), 7: (4, 6), 8: (6, 8), 9: (8, 10)}
WEXP_AT = (12, 13)
FRONT = 19
AHEAD = 2
OUT_AT = {4: 0, 8: 1, 12: 2, 16: 3}
TURN_AT = {6: 0, 10: 1, 14: 2, 17: 3}
S_AT = (0, NWIN[0] * WIN[0] ** 2)
S_W = S_AT[1] + NWIN[1] * WIN[1] ** 2
H1, HD1 = 16, 8
FF = 352
FCH = [(0, 128), (128, 128), (256, 96)]
NCH = len(FCH)
V_W = H1 * (HD1 + 1) + 32 - (HD1 + 1)
SMALL = 29
SETUP_H, SETUP_V, SETUP_P, SETUP_A = 4, 13, 41, 2
SETUP_W = SETUP_V + 2
ITEMS = {"c": "chunk", "d": "down", "m": "max"}
TURN_AT_MAX = 22
FRONT_AFTER = 5
LEAD = "cccdcdcdcdcdcdc"
PATTERN = "mdcmmdcm"
SROWS = 48
LIMIT, ALPHA = 7.0, 1.702

COUNTED = {
    "TensorE":
        "tp tp0 logits gpair lpair y cwt proj up ffn1 ffn2 qk v fh1 fh3 mpair y1 oq mt st pv wo "
        "f_tp down f_logits qkv S",
    "ScalarE":
        "evac evac0 lexp h3g h3l th ys ys1 cwT ppT sqs0 gelu qabs qexp qln v_sb fth ex silu silu0 "
        "f_evac f_lexp qkv_sb wexp0 wexp1",
    "GpSimd":
        "rstd rstd0 xb emb_sin acc acc1 pstep f_rstd f_xb wsub1 wpv1",
    "VectorE":
        "stats xn lsub g cw cw0 gused lused gg lc a x1 h h0 layer0 xrh mag "
        "emb_cos hi lo mx m2 fused oe ot out step "
        "f_stats f_xn f_lsub xi_sq xi prod S_sb wmax0 wmax1 wsub0 wsum0 wsum1 wpv0 wout0 wout1",
    "DMA":
        "stacked max_stacked0 max_stacked1",
    "all":
        "arrived",
}


def plan1():
    out, done = [], {"chunk": 0, "down": 0, "max": 0}
    limit = {"chunk": E * NCH, "down": E * NCH, "max": 2 * H1}

    def emit(what):
        if done[what] < limit[what] and (what != "down" or done["chunk"] > done["down"]):
            out.append((what, done[what]))
            done[what] += 1

    for what in LEAD:
        emit(ITEMS[what])
    while done != limit:
        for what in PATTERN:
            emit(ITEMS[what])
    return out


def maxima_first(plan):
    plan = list(plan)
    for n in range(len(plan) - 1):
        if plan[n][0] == "chunk" and plan[n + 1][0] == "max":
            plan[n], plan[n + 1] = plan[n + 1], plan[n]
    return plan


def ff_bank(c, s):
    return (4, 5, 7)[(2 * c + s) % 3]


def build(nc, A):
    ctx = ExitStack()
    with ctx:
        def sb(name, shape, dt=F32):
            return ctx.enter_context(nc.sbuf_tensor(name, shape, dt))

        sem = {n: ctx.enter_context(nc.semaphore(n)) for n in " ".join(COUNTED.values()).split()}
        numbers = sorted(s.num for s in sem.values())
        counted = range(numbers[0], numbers[-1] + 1)
        assert len(counted) == len(numbers)
        released = ctx.enter_context(nc.semaphore("released"))
        seen = ctx.enter_context(nc.semaphore("seen"))
        x_loaded = ctx.enter_context(nc.semaphore("x_loaded"))
        small_loaded = ctx.enter_context(nc.semaphore("small_loaded"))
        w0_loaded = ctx.enter_context(nc.semaphore("w0_loaded"))
        moe_loaded = ctx.enter_context(nc.semaphore("moe_loaded"))
        stage_loaded = ctx.enter_context(nc.semaphore("stage_loaded"))
        setup = ctx.enter_context(nc.semaphore("setup"))
        setup_pool = ctx.enter_context(nc.semaphore("setup_pool"))
        setup_act = ctx.enter_context(nc.semaphore("setup_act"))
        stacked, arrived = sem["stacked"], sem["arrived"]
        stored = ctx.enter_context(nc.semaphore("stored"))

        IDENT = sb("IDENT", [128, 128])
        HEADSUM = sb("HEADSUM", [128, 128])
        REV = sb("REV", [128, E])
        NHALF = sb("NHALF", [128, NT])
        DOWN = sb("DOWN", [128, 64])
        DOWNB = sb("DOWNB", [128, 64])
        N1W = sb("N1W", [64, 1])
        N2W = sb("N2W", [128, 1])
        WQKV = sb("WQKV", [64, 2, 96])
        QKVB = sb("QKVB", [128, 2, 3])
        PROJ = sb("PROJ", [128, 2, 4, 32])
        PROJB = sb("PROJB", [64, 1])
        UPW = sb("UPW", [64, 128])
        UPB = sb("UPB", [128, 128])
        RPB = [sb(f"RPB{r}", [128, 2 * WIN[r] - 1]) for r in range(2)]
        BIAS = [sb(f"BIAS{r}", [128, WIN[r], WIN[r]]) for r in range(2)]
        MASK = [sb(f"MASK{r}", [128, WIN[r], WIN[r]]) for r in range(2)]
        FW1 = sb("FW1", [128, 256])
        FB1 = sb("FB1", [128, 2])
        FW2 = sb("FW2", [128, 2, 128])
        FB2 = sb("FB2", [128, 128])
        GATEW = sb("GATEW", [128, E])
        GATEB = sb("GATEB", [128, E])
        W0 = sb("W0", [128, E + 1, 4, 128])
        B0 = sb("B0", [128, E + 1, 4])
        W0D = sb("W0D", [128, E + 1, 128])
        B0D = sb("B0D", [E, 128])
        SB0D = sb("SB0D", [128, 128])
        WATT = sb("WATT", [128, 4, 128])
        POPEB = sb("POPEB", [128, 1])
        TRIG = sb("TRIG", [128, 4, T])
        PB = sb("PB", [128, 5])
        LNW = sb("LNW", [128, 1])
        ROUTW = sb("ROUTW", [128, E])
        W1H = sb("W1H", [128, E, 2, FF], F32R)
        W1L = sb("W1L", [128, E, 2, FF], F32R)
        W1D = sb("W1D", [128, E, NCH, 128])

        XIN = sb("XIN", [128, NT, 128])
        STAT = sb("STAT", [128, NT, 6])
        MV = sb("MV", [128, NT, 2])
        VAR = sb("VAR", [128, NT])
        RSTD = sb("RSTD", [128, NT])
        VAR2 = sb("VAR2", [128, 2, NT])
        SCALES = sb("SCALES", [128, 2, NT])
        SQ = sb("SQ", [128, NT])
        XA = sb("XA", [128, NT, 128])
        XNT = sb("XNT", [128, T])
        XI = sb("XI", [128, NT, 64])
        XIT = sb("XIT", [64, XIT_W])
        QKV = [sb(f"QKV{r}", [128, 3, GRP[r]]) for r in range(2)]
        SC = sb("SC", [128, 4096])
        WM = [sb(f"WM{r}", [128, GRP[r]]) for r in range(2)]
        WO = [sb(f"WO{r}", [128, GRP[r]]) for r in range(2)]
        X1 = sb("X1", [128, NT, 128])
        H = sb("H", [128, NT, 128])
        HT = sb("HT", [128, T])
        G = sb("G", [128, 2, 512])
        S0 = sb("S0", [128, NT, 128])
        RT = sb("RT", [128, 8, NT, E])
        RS = sb("RS", [128, 6, NT])
        CW = sb("CW", [128, NT, E])
        WORK = sb("WORK", [128, 1024 + S_W])
        ACC = sb("ACC", [128, NT, 128])
        XRH = sb("XRH", [128, T], F32R)
        XRL = sb("XRL", [128, T], F32R)
        QS = sb("QS", [128, 8, T], F32R)
        KS = sb("KS", [128, 8, T], F32R)
        V = sb("V", [128, NT, V_W])
        MX = sb("MX", [128, NT, H1])
        DEN = sb("DEN", [128, 4, 16])
        PS = ctx.enter_context(nc.psum_tensor("PS", [128, 8, 512], F32))

        A4 = WORK[:, 0:2048].rearrange("p (c n) -> p c n", c=4)
        AA, H3 = A4[:, 0:2, :], A4[:, 2:4, :]
        UL = WORK[:, 2048:4096].rearrange("p (c b n) -> p c b n", c=2, b=2)
        TH = WORK[:, 4096:5120].rearrange("p (c n) -> p c n", c=2)
        WS = WORK[:, 1024:1024 + S_W]
        PPT = HT[0:64, :]
        CWT = XA[0:E].rearrange("p t f -> p (t f)")
        XN = X1
        YS = S0
        EH = SC[:, 0:4 * T].rearrange("p (c n) -> p c n", c=4)
        M2 = [G[32 * w:32 * w + 8] for w in range(2)]
        EF = UL.rearrange("p a b n -> p (a b) n")
        P = SC[:, 0:4096].rearrange("p (s a n) -> p s a n", s=2, a=4)
        STAGE = SC[:, 0:4 * 2 * FF].rearrange("p (e b f) -> p e b f", e=4, b=2)
        ntok = lambda ap: ap.rearrange("p (t f) -> p t f", t=NT)

        def bc(ap, shape, axis):
            return ap.unsqueeze(axis).to_broadcast(shape)

        def end_pass(eng, i, last=False):
            all_done(eng, i, last)
            eng.sem_inc(arrived, 1)
            eng.wait_ge(released, i + 2)

        def all_done(eng, i, last):
            if i is not FIRST:
                eng.wait_ge(sem["out"], 1)
            if not last:
                eng.wait_ge(sem["layer0"], 1)

        block = ctx.enter_context(nc.Block())

        @block.sync
        def _(sp):
            x_t = A["x"].rearrange("(b t p) d -> b p t d", b=B, t=NT)
            y_t = A["y"].rearrange("(b t p) d -> b p t d", b=B, t=NT)
            sp.sem_inc(stored, 16)
            sp.dma_start(XIN[:], x_t[0]).then_inc(x_loaded, 16)
            n = [0]

            def small(dst, src):
                sp.dma_start(dst, src).then_inc(small_loaded, 16)
                n[0] += 1

            small(IDENT[:], A["ident"])
            small(HEADSUM[:], A["headsum"])
            small(REV[:], A["rev"])
            small(DOWN[:], A["down_w"])
            small(DOWNB[:], A["down_b"].partition_broadcast(128))
            small(N1W[:], A["norm1_w"])
            small(N2W[:], A["norm2_w"])
            small(UPW[:], A["up_w"])
            small(UPB[:], A["up_b"].partition_broadcast(128))
            small(WQKV[:], A["wqkv"])
            small(QKVB[:], A["qkvb"])
            small(PROJ[:], A["proj"])
            small(PROJB[:], A["projb"])
            for r in range(2):
                small(RPB[r][:], A[f"rpb{r + 1}"])
            small(FW1[:], A["ffn_w1"])
            small(FB1[:], A["ffn_b1"])
            small(FW2[:], A["ffn_w2"].rearrange("(c p) d -> p c d", c=2))
            small(FB2[:], A["ffn_b2"].partition_broadcast(128))
            small(GATEW[:], A["gate_w"])
            small(GATEB[:], A["gate_b"].partition_broadcast(128))
            small(B0[:], A["b0"])
            small(B0D[:], A["b2"])
            small(SB0D[:], A["sb2"].partition_broadcast(128))
            small(WATT[:], A["watt"])
            small(POPEB[:], A["pope_bias"])
            small(TRIG[:, 0:2, :], A["trig"])
            small(LNW[:], A["ln_weight"])
            small(ROUTW[:], A["router_w"])
            assert n[0] == SMALL
            sp.dma_start(W0[:], A["w0"]).then_inc(w0_loaded, 16)
            sp.dma_start(W0D[:], A["w0d"]).then_inc(w0_loaded, 16)
            for half in range(2):
                if half:
                    for c, (f, m) in enumerate(FCH):
                        sp.dma_start(W1D[0:m, :, c, :], A["w2"][:, f:f + m, :].rearrange("e f d -> f e d")
                                     ).then_inc(moe_loaded, 16)
                    sp.wait_ge(setup, SETUP_W - 1)
                es = slice(4 * half, 4 * half + 4)
                sp.dma_start(STAGE[:, :, 0, :], A["w1"][es].rearrange("e d f -> d e f")).then_inc(stage_loaded, 16)
                sp.dma_start(STAGE[:, :, 1, :], A["w3"][es].rearrange("e d f -> d e f")).then_inc(stage_loaded, 16)

            def one_pass(i, last):
                if not last:
                    sp.dma_start(XIN[:], x_t[i + 1]).then_inc(x_loaded, 16)
                for part, src in (("hi", EH), ("lo", EF)):
                    sp.wait_ge(sem[part], 1)
                    for dst, first, blocks in ((QS, 0, (0, 0, 1)), (KS, 2, (0, 1, 0))):
                        for r, low in enumerate(blocks):
                            for c in range(2):
                                for par in range(2):
                                    row = 64 * par + 16 * r + 8 * c
                                    if low == (part == "lo"):
                                        sp.dma_start(dst[row:row + 8, :, :].bitcast(F32),
                                                     src[64 * par:64 * par + 64, first + c, :]).then_inc(stacked, 16)
                for which in range(2):
                    for part in range(2):
                        sp.wait_ge(sem["m2"], 2 * which + part + 1)
                        for par in range(2):
                            row = 64 * par + SROWS + part
                            sp.dma_start(QS[row:row + 1, 4 * which:4 * which + 4, :].bitcast(F32),
                                         M2[which][4 * par:4 * par + 4, part, :]
                                         ).then_inc(sem[f"max_stacked{which}"], 16)
                sp.wait_ge(sem["out"], 1)
                sp.dma_start(y_t[i], S0[:]).then_inc(stored, 16)
                end_pass(sp, i, last)
                sp.sem_inc(seen, 1)

            end_pass(sp, FIRST)
            sp.sem_inc(seen, 1)
            with sp.Fori(0, B - 1) as i:
                one_pass(i, False)
            one_pass(B - 1, True)
            sp.wait_ge(stored, 16 * (B + 1))

        @block.tensor
        def _(pe):
            def signal(ins, name):
                ins.then_inc(sem[name], 1)

            def transposes(i, src, rows, bank, name="tp"):
                for t in range(NT):
                    ins = pe.transpose(PS[0:rows, bank, 128 * t:128 * t + 128], src[:, t, :], IDENT[:])
                signal(ins, name)

            def tok_matmul(bank, width, lhs, rhs, name):
                out = PS[:, bank, 0:NT * width].rearrange("p (t f) -> p t f", t=NT)
                for t in range(NT):
                    ins = pe.matmul(out[:, t, :], lhs[:, 128 * t:128 * t + 128], rhs, start=True, stop=True)
                signal(ins, name)

            def expert_pair(k, pair):
                if k:
                    pe.wait_ge(sem[("gused", "lused")[pair]], k)
                for m in range(2):
                    ins = pe.matmul(PS[:, 2 * pair + m, :], W0[:, k, 2 * pair + m, :], XNT[:],
                                    start=True, stop=True)
                signal(ins, ("gpair", "lpair")[pair])

            def layer0(i):
                for k in range(E + 3):
                    if k <= E and (k or i is FIRST):
                        expert_pair(k, 0)
                        expert_pair(k, 1)
                    if k >= 2:
                        e = k - 2
                        pe.wait_ge(sem["a"], e + 1)
                        if e == 1:
                            pe.wait_ge(sem["cwT"], 1)
                        if e >= 2:
                            pe.wait_ge(sem["ys"], e - 1)
                        shared = e == E
                        for t in range(NT):
                            out = PS[:, 6 + e % 2, 128 * t:128 * t + 128]
                            if shared:
                                pe.matmul(out, CWT[:, 128 * t:128 * t + 128], B0D[:], start=True, stop=False)
                            ins = pe.matmul(out, AA[:, e % 2, 128 * t:128 * t + 128], W0D[:, e, :],
                                            start=not shared, stop=True)
                        signal(ins, "y")
                    tail0(i, k)
                pe.wait_ge(sem["gelu"], 2)
                for t in range(NT):
                    for c in range(2):
                        ins = pe.matmul(PS[:, 4, 128 * t:128 * t + 128], G[:, c, 128 * t:128 * t + 128],
                                        FW2[:, c, :], start=c == 0, stop=c == 1)
                signal(ins, "ffn2")

            def front(i, n):
                if n == 0:
                    pe.wait_ge(sem["f_xn"], 1)
                    transposes(i, XN, 128, 4, "f_tp")
                if n == 1:
                    pe.wait_ge(sem["f_evac"], 1)
                    for t in range(NT):
                        ins = pe.matmul(PS[:, 5, 256 + E * t:256 + E * t + E], XNT[:, 128 * t:128 * t + 128], GATEW[:],
                                        start=True, stop=True)
                    signal(ins, "f_logits")
                    tok_matmul(5, 64, XNT, DOWN[:], "down")
                if n == 3:
                    pe.wait_ge(sem["xi"], 1)
                    transposes(i, XI, 64, 4, "f_tp")
                if n == 4:
                    pe.wait_ge(sem["f_evac"], 2)
                    pe.wait_ge(sem["f_lsub"], 1)
                    for r in range(2):
                        for g in range(4):
                            for c in range(3):
                                a = SHIFT[r] + g * GRP[r]
                                ins = pe.matmul(PS[32 * g:32 * g + 32, 5 - r, c * GRP[r]:(c + 1) * GRP[r]],
                                                WQKV[:, r, 32 * c:32 * c + 32], XIT[:, a:a + GRP[r]],
                                                start=True, stop=True)
                        signal(ins, "qkv")
                if n - 1 in CHUNK_AT:
                    for c in range(*CHUNK_AT[n - 1]):
                        r, w, m = CHUNKS[c]
                        width = m * WIN[r] ** 2
                        pe.wait_ge(sem["prod"], c + 1)
                        if c >= 2:
                            pe.wait_ge(sem["S_sb"], c - 1)
                        else:
                            pe.wait_ge(sem["qkv_sb"], 2)
                        signal(pe.matmul(PS[:, 4 + c % 2, 0:width], HEADSUM[:], G[:, c % 2, 0:width],
                                         start=True, stop=True), "S")

            def front_beside(i, n):
                if n == 0:
                    front(i, 1)
                front(i, n + AHEAD)

            def tail0(i, k):
                if k == 1:
                    pe.wait_ge(sem["wout0"], 1)
                    pe.wait_ge(sem["wout1"], 1)
                    for r in range(2):
                        for g in range(4):
                            a = SHIFT[r] + g * GRP[r]
                            n = min(GRP[r], T - a)
                            out = PS[32 * r:32 * r + 32, 4, :]
                            ins = pe.matmul(out[:, a:a + n], PROJ[:, r, g, :], WO[r][:, 0:n], start=True, stop=True)
                        ins = pe.matmul(out[:, 0:SHIFT[r]], PROJ[:, r, 3, :],
                                        WO[r][:, PADT - a:PADT - a + SHIFT[r]], start=True, stop=True)
                    signal(ins, "proj")
                if k == 2:
                    pe.wait_ge(sem["ppT"], 1)
                    if i is not FIRST:
                        pe.wait_ge(sem["out"], 1)
                    tok_matmul(5, 128, PPT, UPW[:], "up")
                    pe.wait_ge(sem["cw0"], 1)
                    for t in range(NT):
                        ins = pe.transpose(PS[0:E, 7, 128 * t:128 * t + 128], CW[:, t, :], IDENT[:])
                    signal(ins, "cwt")
                if k == 5:
                    pe.wait_ge(sem["h0"], 1)
                    transposes(i, H, 128, 4, "tp0")
                if k == 6:
                    pe.wait_ge(sem["evac0"], 1)
                    for c in range(2):
                        signal(pe.matmul(PS[:, 5 - c, :], FW1[:, 128 * c:128 * c + 128], HT[:],
                                         start=True, stop=True), "ffn1")

            def scores_for_max(i, h, half):
                n = 2 * h + half
                if n >= 2:
                    pe.wait_ge(sem["mx"], n - 1)
                rows = slice(64 * (h % 2), 64 * (h % 2) + SROWS)
                for s in range(2):
                    t = 2 * half + s
                    ins = pe.matmul(PS[:, 2 * half + s, :], QS[rows, h // 2, 128 * t:128 * t + 128],
                                    KS[rows, h // 2, :], start=True, stop=True)
                signal(ins, "mpair")

            def turn_maxima(i, which, bank):
                for t in range(NT):
                    ins = pe.transpose(PS[0:8, bank, 128 * t:128 * t + 128],
                                       MX[:, t, 8 * which:8 * which + 8], IDENT[:])
                signal(ins, "mt")

            def ff_pair(i, c):
                e, (f, m) = c // NCH, FCH[c % NCH]
                for s in range(2):
                    if s == 0 and c >= 2:
                        pe.wait_ge(sem["fused"], c - 1)
                    if s == 1 and c:
                        pe.wait_ge(sem["fth"], c)
                    for n, (w, x) in enumerate(((W1H, XRH), (W1H, XRL), (W1L, XRH))):
                        ins = pe.matmul(PS[0:m, ff_bank(c, s), :], w[:, e, s, f:f + m], x[:], start=n == 0, stop=n == 2)
                    signal(ins, ("fh1", "fh3")[s])

            def ff_down(i, part):
                e, c = divmod(part, NCH)
                m = FCH[c][1]
                pe.wait_ge(sem["fused"], part + 1)
                if e and c == 0:
                    pe.wait_ge(sem["ys1"], e)
                for t in range(NT):
                    ins = pe.matmul(PS[:, 6, 128 * t:128 * t + 128],
                                    A4[0:m, part % 4, 128 * t:128 * t + 128], W1D[0:m, e, c, :],
                                    start=c == 0 and t == 0, stop=c == NCH - 1 and t == NT - 1,
                                    skip_group_check=True)
                signal(ins, "y1")

            def layer1(i, last):
                pe.wait_ge(sem["xn"], 1)
                transposes(i, X1, 128, 0)
                pe.wait_ge(sem["h"], 1)
                transposes(i, H, 128, 1)
                pe.wait_ge(sem["evac"], 1)
                for n in range(2):
                    signal(pe.matmul(PS[:, 2 + n, :], WATT[:, n, :], XNT[:], start=True, stop=True), "qk")
                pe.wait_ge(sem["evac"], 2)
                tok_matmul(6, E, HT, ROUTW[:], "logits")
                pe.wait_ge(sem["xrh"], 2)
                for what, n in plan1():
                    if what == "chunk":
                        ff_pair(i, n)
                        if n == 0:
                            tok_matmul(0, 128, XNT, WATT[:, 2, :], "v")
                    elif what == "down":
                        if n == 0:
                            pe.wait_ge(sem["lsub"], 1)
                        ff_down(i, n)
                    else:
                        if n == 0:
                            pe.wait_ge(stacked, 16 * 24)
                            pe.wait_ge(sem["v_sb"], 1)
                        if n == TURN_AT_MAX:
                            pe.wait_ge(sem["mx"], n - 1)
                            turn_maxima(i, 0, 0)
                            pe.wait_ge(sem["m2"], 2)
                        scores_for_max(i, n // 2, n % 2)
                pe.wait_ge(sem["mx"], 32)
                pe.wait_ge(sem["fused"], E * NCH)
                turn_maxima(i, 1, 7)
                if not last:
                    front(i, 0)
                pe.wait_ge(sem["max_stacked0"], 16 * 4)
                for n in range(4 * NT + 2):
                    if n == 2 * NT:
                        pe.wait_ge(sem["max_stacked1"], 16 * 4)
                    if n < 4 * NT:
                        k = n % NT
                        for half in range(2):
                            if n:
                                pe.wait_ge(sem["ex"], 2 * n - 1 + half)
                            for a in range(2 * half, 2 * half + 2):
                                h = n // NT * 4 + a
                                rows = slice(64 * (h % 2), 64 * (h % 2) + SROWS + 2)
                                ins = pe.matmul(PS[:, a, :], KS[rows, h // 2, 128 * k:128 * k + 128],
                                                QS[rows, h // 2, :], start=True, stop=True)
                            signal(ins, "st")
                    if 1 <= n <= 4 * NT:
                        g, k = divmod(n - 1, NT)
                        pe.wait_ge(sem["ex"], 2 * n)
                        if n == 1:
                            pe.wait_ge(sem["m2"], 4)
                        if n == 5:
                            pe.wait_ge(sem["ys1"], E)
                        if g >= 2 and k == 0:
                            pe.wait_ge(sem["ot"], g - 1)
                        for a in range(4):
                            at = (4 * g + a) * (HD1 + 1)
                            ins = pe.matmul(PS[32 * a:32 * a + 32, 7 - g % 2, :], V[:, k, at:at + 32],
                                            P[:, (n - 1) % 2, a, :], start=k == 0, stop=k == NT - 1)
                        signal(ins, "pv")
                    if n in TURN_AT:
                        g = TURN_AT[n]
                        pe.wait_ge(sem["oe"], g + 1)
                        for t in range(NT):
                            ins = pe.transpose(PS[:, 7 - g % 2, 128 * t:128 * t + 128],
                                               A4[:, g % 2, 128 * t:128 * t + 128], IDENT[:])
                        signal(ins, "oq")
                    if not last:
                        front_beside(i, n)
                if not last:
                    expert_pair(0, 0)
                pe.wait_ge(sem["ot"], 4)
                transposes(i, H, 128, 7)
                if not last:
                    expert_pair(0, 1)
                pe.wait_ge(sem["evac"], 3)
                tok_matmul(5, 128, HT, WATT[:, 3, :], "wo")

            pe.wait_ge(small_loaded, 16 * SMALL)
            pe.wait_ge(setup, SETUP_V)
            pe.wait_ge(setup_pool, SETUP_P)
            for n in range(FRONT):
                front(FIRST, n)
            pe.wait_ge(w0_loaded, 16 * 2)
            layer0(FIRST)
            end_pass(pe, FIRST)
            pe.wait_ge(moe_loaded, 16 * NCH)
            pe.wait_ge(setup, SETUP_W)
            with pe.Fori(0, B - 1) as i:
                layer1(i, False)
                layer0(i)
                end_pass(pe, i)
            layer1(B - 1, True)
            end_pass(pe, B - 1, True)

        @block.scalar
        def _(act):
            def go(name, *a, **k):
                act.activation(*a, **k).then_inc(sem[name], 1)

            act.wait_ge(small_loaded, 16 * SMALL)
            act.wait_ge(setup_pool, SETUP_P)
            act.wait_ge(setup, SETUP_H)
            act.activation(PB[:, 3:4], PB[:, 1:2], ACT.Sin).then_inc(setup_act, 1)
            act.activation(PB[:, 4:5], PB[:, 2:3], ACT.Sin).then_inc(setup_act, 1)

            def layer0(i):
                act.wait_ge(sem["wout0"], 1)
                act.wait_ge(sem["wout1"], 1)
                for k in range(E + 3):
                    if k <= E:
                        for s, (ready, used, done) in enumerate((("gpair", "gused", "h3g"), ("lpair", "lused", "h3l"))):
                            act.wait_ge(sem[ready], k + 1)
                            if k:
                                act.wait_ge(sem[used], k)
                            go(done, H3[:, s, :], PS[:, 2 * s + 1, :], ACT.Identity, bias=B0[:, k, 2 * s + 1:2 * s + 2])
                        act.wait_ge(sem["gg"], k + 1)
                        if k >= 2:
                            act.wait_ge(sem["a"], k - 1)
                        go("th", TH[:, k % 2, :], UL[:, k % 2, 0, :], ACT.Silu, scale=ALPHA)
                    if k >= 2:
                        e = k - 2
                        if e >= E - 1:
                            continue
                        act.wait_ge(sem["y"], e + 1)
                        if e == 0:
                            act.wait_ge(sem["cw0"], 1)
                            act.wait_ge(stored, 16 * (i + 2))
                        if e:
                            act.wait_ge(sem["acc"], e)
                        weighted(6 + e % 2, "ys", CW[:, :, e:e + 1])
                    tail0(i, k)
                act.wait_ge(sem["g"], 1)
                go("silu0", TH[:, 0, :], ACC[:].rearrange("p t f -> p (t f)"), ACT.Tanh, scale=0.5)

            def weighted(bank, name, gate):
                for t in range(NT):
                    ins = act.activation(YS[:, t, :], PS[:, bank, 128 * t:128 * t + 128], ACT.Copy,
                                         scale=gate[:, t, :])
                ins.then_inc(sem[name], 1)

            def front(i, n):
                if n == 0:
                    act.wait_ge(sem["f_tp"], 1)
                    go("f_evac", XNT[:], PS[:, 4, :], ACT.Copy)
                if n == 2:
                    act.wait_ge(sem["f_lsub"], 1)
                    go("f_lexp", RT[:, 1], RT[:, 0], ACT.Exp)
                if n == 3:
                    act.wait_ge(sem["f_tp"], 2)
                    act.activation(XIT[:, 0:T], PS[0:64, 4, :], ACT.Copy, scale=N1W[:, 0:1])
                    go("f_evac", XIT[:, PADT:PADT + SHIFT[1]], PS[0:64, 4, 0:SHIFT[1]], ACT.Copy, scale=N1W[:, 0:1])
                if n == 4:
                    for r in range(2):
                        act.wait_ge(sem["qkv"], r + 1)
                        for c in range(3):
                            ins = act.activation(QKV[r][:, c, :], PS[:, 5 - r, c * GRP[r]:(c + 1) * GRP[r]],
                                                 ACT.Identity, bias=QKVB[:, r, c:c + 1], scale=0.5 if c == 0 else 1.0)
                        ins.then_inc(sem["qkv_sb"], 1)
                if n in WEXP_AT:
                    r = WEXP_AT.index(n)
                    act.wait_ge(sem[f"wsub{r}"], 1)
                    s = WS[:, S_AT[r]:S_AT[r] + GRP[r] * WIN[r]]
                    go(f"wexp{r}", s, s, ACT.Exp)

            def front_beside(i, n):
                if n == 0:
                    front(i, 1)
                front(i, n + AHEAD)

            def tail0(i, k):
                if k == 1:
                    act.wait_ge(sem["proj"], 1)
                    if i is not FIRST:
                        act.wait_ge(sem["wo"], 1)
                    go("ppT", PPT, PS[0:64, 4, :], ACT.Identity, bias=PROJB[:, 0:1])
                if k == 2:
                    act.wait_ge(sem["cwt"], 1)
                    if i is not FIRST:
                        act.wait_ge(sem["out"], 1)
                    go("cwT", CWT, PS[0:E, 7, :], ACT.Copy, scale=ALPHA ** 2)
                if k == 3:
                    act.wait_ge(sem["x1"], 1)
                    square_sums("sqs0")
                if k == 5:
                    act.wait_ge(sem["tp0"], 1)
                    go("evac0", HT[:], PS[:, 4, :], ACT.Copy, scale=N2W[:, 0:1])
                if k == 8:
                    for c in range(2):
                        act.wait_ge(sem["ffn1"], c + 1)
                        go("gelu", G[:, c, :], PS[:, 5 - c, :], ACT.Gelu, bias=FB1[:, c:c + 1])

            def square_sums(name):
                for t in range(NT):
                    ins = act.activation(H[:, t, :], X1[:, t, :], ACT.Square, accum_out=SQ[:, t:t + 1])
                ins.then_inc(sem[name], 1)

            def layer1(i, last):
                act.wait_ge(sem["tp"], 1)
                go("evac", XNT[:], PS[:, 0, :], ACT.Copy)
                act.wait_ge(sem["tp"], 2)
                go("evac", HT[:], PS[:, 1, :], ACT.Copy, scale=LNW[:, 0:1])
                for n in range(2):
                    act.wait_ge(sem["qk"], n + 1)
                    go("qabs", AA[:, n, :], PS[:, 2 + n, :], ACT.Abs)
                for n in range(2):
                    act.wait_ge(sem["qabs"], n + 1)
                    go("qexp", AA[:, n, :], AA[:, n, :], ACT.Exp, scale=-1.0)
                act.wait_ge(sem["lsub"], 1)
                go("lexp", RT[:, 1], RT[:, 0], ACT.Exp)
                for n in range(2):
                    act.wait_ge(sem["qexp"], n + 1)
                    go("qln", AA[:, n, :], AA[:, n, :], ACT.Ln, bias=1.0)
                act.wait_ge(sem["v"], 1)
                heads = V[:, :, 0:H1 * (HD1 + 1)].rearrange("p t (h d) -> p t h d", h=H1)
                go("v_sb", heads[:, :, :, 0:HD1], PS[:, 0, :].rearrange("p (t h d) -> p t h d", t=NT, h=H1), ACT.Copy)
                for what, n in plan1():
                    if what == "chunk":
                        m = FCH[n % NCH][1]
                        act.wait_ge(sem["fh1"], n + 1)
                        if n >= 2:
                            act.wait_ge(sem["fused"], n - 1)
                        go("fth", TH[0:m, n % 2, :], PS[0:m, ff_bank(n, 0), :], ACT.Silu)
                    elif what == "down" and n % NCH == NCH - 1:
                        e = n // NCH
                        act.wait_ge(sem["y1"], n + 1)
                        if e == 0:
                            act.wait_ge(sem["cw"], 1)
                        if e:
                            act.wait_ge(sem["acc1"], e)
                        weighted(6, "ys1", CW[:, :, e:e + 1])
                if not last:
                    front(i, 0)
                for n in range(4 * NT):
                    for half in range(2):
                        act.wait_ge(sem["st"], 2 * n + half + 1)
                        if n >= 2:
                            act.wait_ge(sem["pv"], n - 1)
                        go("ex", P[:, n % 2, 2 * half:2 * half + 2, :], PS[:, 2 * half:2 * half + 2, :], ACT.Exp,
                           scale=HD1 ** -0.5)
                    if not last:
                        front_beside(i, n)
                act.wait_ge(sem["tp"], 3)
                go("evac", HT[:], PS[:, 7, :], ACT.Copy)
                act.wait_ge(sem["acc1"], E)
                go("silu", G[:, 0, :], ACC[:].rearrange("p t f -> p (t f)"), ACT.Tanh, scale=0.5)

            for n in range(FRONT):
                front(FIRST, n)
            for n in range(2):
                if n:
                    layer0(FIRST)
                act.wait_ge(stage_loaded, 32 * (n + 1))
                act.activation(W1H[:, 4 * n:4 * n + 4], STAGE, ACT.Copy).then_inc(setup_act, 1)
            end_pass(act, FIRST)
            act.wait_ge(setup, SETUP_W)
            with act.Fori(0, B - 1) as i:
                layer1(i, False)
                layer0(i)
                end_pass(act, i)
            layer1(B - 1, True)
            end_pass(act, B - 1, True)

        @block.gpsimd
        def _(pool):
            n = [0]

            def init(ins):
                n[0] += 1
                ins.then_inc(setup_pool, 1)
                pool.wait_ge(setup_pool, n[0])

            init(pool.memset(NHALF[:], -0.5))
            for r in range(2):
                init(pool.memset(MASK[r][96:128], 0.0))
            init(pool.memset(XIT[:, T:XIT_W], 0.0))
            init(pool.memset(V[:], 1.0))
            for row in (32, 96):
                init(pool.memset(KS[row:row + SROWS - 32 + 2].bitcast(F32), 1.0))
            for r in range(2):
                w, s = WIN[r], SHIFT[r]
                init(pool.memset(MASK[r][96:128, 0:w - s, w - s:w], -100.0))
                init(pool.memset(MASK[r][96:128, w - s:w, 0:w - s], -100.0))
            pool.wait_ge(small_loaded, 16 * SMALL)
            for r in range(2):
                w = WIN[r]
                for q in range(w):
                    init(pool.tensor_copy(BIAS[r][:, q, :], RPB[r][:, w - 1 - q:2 * w - 1 - q]))
            assert n[0] == SETUP_P, n[0]
            pool.wait_ge(setup, SETUP_V)
            done = {}

            def go(name, ins):
                done[name] = done.get(name, 0) + 1
                ins.then_inc(sem[name], 1)
                pool.wait_ge(sem[name], done[name])

            def rsqrt(i, src, scale, eps, name):
                go("pstep", pool.tensor_scalar(VAR[:], src, scale, eps, ALU.mult, ALU.add))
                go(name, pool.tensor_tensor(RSTD[:], VAR[:], NHALF[:], ALU.pow))

            def layernorm_front(i):
                pool.wait_ge(sem["f_stats"], 1)
                rsqrt(i, MV[:, :, 1], 1.0, 1e-5, "f_rstd")

            def front(i):
                pool.wait_ge(sem["f_tp"], 1)
                go("f_xb", pool.tensor_tensor(X1[:], XN[:], bc(UPB[:], [128, NT, 128], 1), ALU.add))
                pool.wait_ge(sem["xi_sq"], 1)
                rsqrt(i, SQ[:], 1.0 / 64, 1e-6, "f_rstd")
                w = WIN[1]
                s = WS[:, S_AT[1]:S_AT[1] + GRP[1] * w].rearrange("p (n k) -> p n k", k=w)
                pool.wait_ge(sem["wmax1"], 1)
                go("wsub1", pool.tensor_tensor(s, s, bc(WM[1][:], [128, GRP[1], w], 2), ALU.subtract))
                pool.wait_ge(sem["wexp1"], 1)
                pool.wait_ge(sem["wsum1"], 1)
                s = s.rearrange("p (w q) k -> p w q k", q=w)
                v = QKV[1][:, 2, :].rearrange("p (w k) -> p w k", k=w)
                go("wpv1", pool.tensor_tensor(s, s, bc(v, [128, NWIN[1], w, w], 2), ALU.mult))

            def layer0(i):
                for k in range(E + 3):
                    if k >= 2:
                        e = k - 2
                        if e >= E - 1:
                            continue
                        pool.wait_ge(sem["ys"], e + 1)
                        if e:
                            go("acc", pool.tensor_tensor(ACC[:], YS[:], ACC[:], ALU.add))
                        else:
                            if i is not FIRST:
                                pool.wait_ge(sem["out"], 1)
                            go("acc", pool.tensor_tensor(ACC[:], YS[:], bc(SB0D[:], [128, NT, 128], 1), ALU.add))
                    if k == 3:
                        pool.wait_ge(sem["sqs0"], 1)
                        rsqrt(i, SQ[:], 1.0 / 128, 1e-6, "rstd0")
                    if k == 5:
                        pool.wait_ge(sem["h0"], 1)
                        go("xb", pool.tensor_tensor(X1[:], X1[:], bc(FB2[:], [128, NT, 128], 1), ALU.add))

            def layer1(i, last):
                pool.wait_ge(sem["stats"], 1)
                eps = 1e-5
                go("pstep", pool.tensor_scalar(VAR2[:, 0], MV[:, :, 1], 1.0, eps, ALU.mult, ALU.add))
                go("rstd", pool.tensor_tensor(SCALES[:, 0], VAR2[:, 0], NHALF[:], ALU.pow))
                go("pstep", pool.tensor_scalar(VAR2[:, 1], MV[:, :, 1], 1.0 + eps, eps * eps, ALU.mult, ALU.add))
                go("rstd", pool.tensor_tensor(SCALES[:, 1], VAR2[:, 1], NHALF[:], ALU.pow))
                for n in range(2):
                    pool.wait_ge(sem["mag"], n + 1)
                    go("emb_sin", pool.tensor_tensor(EF[:, 2 * n + 1, :], H3[:, n, :], TRIG[:, 2 * n + 1, :], ALU.mult))
                for e in range(E):
                    pool.wait_ge(sem["ys1"], e + 1)
                    if e:
                        go("acc1", pool.tensor_tensor(ACC[:], YS[:], ACC[:], ALU.add))
                    else:
                        go("acc1", pool.tensor_copy(ACC[:], YS[:]))

                    if e == FRONT_AFTER and not last:
                        layernorm_front(i)
                if not last:
                    front(i)

            def close(i, last=False):
                all_done(pool, i, last)
                pool.wait_ge(arrived, 4)
                pool.sem_clear(counted)
                pool.sem_inc(released, 1)
                done.clear()

            layernorm_front(FIRST)
            front(FIRST)
            layer0(FIRST)
            close(FIRST)
            with pool.Fori(0, B - 1) as i:
                layer1(i, False)
                layer0(i)
                close(i)
            layer1(B - 1, True)
            close(B - 1, True)

        @block.vector
        def _(dve):
            count = [0]

            def go(name, ins):
                ins.then_inc(sem[name], 1)

            def step(i, ins):
                count[0] += 1
                ins.then_inc(sem["step"], 1)
                dve.wait_ge(sem["step"], count[0])

            n = [0]

            def init(ins):
                n[0] += 1
                ins.then_inc(setup, 1)
                dve.wait_ge(setup, n[0])

            dve.wait_ge(small_loaded, 16 * SMALL)
            pi = float(np.pi)
            init(dve.tensor_scalar(PB[:, 0:1], POPEB[:], 0.0, -2.0 * pi, ALU.min, ALU.max))
            init(dve.tensor_scalar(PB[:, 1:2], PB[:, 0:1], pi, 0.5, ALU.add, ALU.mult))
            init(dve.scalar_tensor_tensor(PB[:, 2:3], PB[:, 1:2], -1.0, PB[:, 1:2], ALU.mult, ALU.min))
            init(dve.tensor_scalar(PB[:, 2:3], PB[:, 2:3], pi / 2, None, ALU.add))
            assert n[0] == SETUP_H
            dve.wait_ge(setup_act, SETUP_A)
            init(dve.scalar_tensor_tensor(PB[:, 0:1], PB[:, 3:4], 2.0, PB[:, 4:5], ALU.mult, ALU.mult))
            init(dve.scalar_tensor_tensor(PB[:, 1:2], PB[:, 3:4], 2.0, PB[:, 3:4], ALU.mult, ALU.mult))
            init(dve.tensor_scalar(PB[:, 1:2], PB[:, 1:2], 1.0, None, ALU.subtract))
            init(dve.tensor_scalar(PB[:, 2:3], PB[:, 0:1], -1.0, None, ALU.mult))
            for m, (first, second) in enumerate(((0, 0), (1, 2))):
                init(dve.tensor_scalar(TRIG[:, 2 + m, :], TRIG[:, m, :], PB[:, 1:2], None, ALU.mult))
                init(dve.scalar_tensor_tensor(TRIG[:, 2 + m, :], TRIG[:, 1 - m, :], PB[:, second:second + 1],
                                              TRIG[:, 2 + m, :], ALU.mult, ALU.add))
            init(dve.tensor_scalar(QKVB[:, :, 0:1], QKVB[:, :, 0:1], 0.5, None, ALU.mult))
            assert n[0] == SETUP_V, n[0]
            dve.wait_ge(setup_pool, SETUP_P)

            def statistics(i, src, name):
                for t in range(NT):
                    ins = dve.bn_stats(STAT[:, t, :], src[:, t, :])
                step(i, ins)
                for t in range(NT):
                    ins = dve.bn_aggr(MV[:, t, :], STAT[:, t, :])
                go(name, ins)
                dve.wait_ge(sem[name], 1)

            def normalise(dst, src, scale, name):
                for t in range(NT):
                    ins = dve.tensor_scalar(dst[:, t, :], src[:, t, :], MV[:, t, 0:1], scale[:, t:t + 1],
                                            ALU.subtract, ALU.mult)
                go(name, ins)

            def routing_logits(i, pre, logits):
                dve.wait_ge(sem[pre + "logits"], 1)
                step(i, dve.tensor_reduce(RS[:, 0], logits, AX.X, ALU.max))
                go(pre + "lsub", dve.tensor_tensor(RT[:, 0], logits, bc(RS[:, 0], [128, NT, E], 2), ALU.subtract))

            def routing_scores(i, biased):
                s4 = [128, NT, E]
                step(i, dve.tensor_reduce(RS[:, 1], RT[:, 1], AX.X, ALU.add))
                step(i, dve.reciprocal(RS[:, 2], RS[:, 1]))
                step(i, dve.tensor_tensor(RT[:, 1], RT[:, 1], bc(RS[:, 2], s4, 2), ALU.mult))
                if biased:
                    step(i, dve.tensor_tensor(RT[:, 2], RT[:, 1], bc(GATEB[:], s4, 1), ALU.add))

            def routing_pick(i, biased, pick):
                s4 = [128, NT, E]
                key = 5 if pick else 2 if biased else 1
                hot = RT[:, 3 + pick]
                step(i, dve.tensor_reduce(RS[:, 3], RT[:, key], AX.X, ALU.max))
                step(i, dve.tensor_tensor(hot, RT[:, key], bc(RS[:, 3], s4, 2), ALU.is_equal))
                step(i, dve.tensor_tensor(hot, hot, bc(REV[:], s4, 1), ALU.mult))
                step(i, dve.tensor_reduce(RS[:, 3], hot, AX.X, ALU.max))
                step(i, dve.tensor_tensor(hot, hot, bc(RS[:, 3], s4, 2), ALU.is_equal))
                if pick == 0:
                    step(i, dve.scalar_tensor_tensor(RT[:, 5], hot, -1e30, RT[:, key], ALU.mult, ALU.add))

            def routing_weights(i, name, scale):
                step(i, dve.tensor_tensor(RT[:, 6], RT[:, 3], RT[:, 4], ALU.add))
                go(name, dve.scalar_tensor_tensor(CW[:], RT[:, 6], scale, RT[:, 1], ALU.mult, ALU.mult))
                dve.wait_ge(sem[name], 1)

            def layer0(i):
                for k in range(E + 3):
                    if k <= E:
                        for s, (pair, h3, used) in enumerate((("gpair", "h3g", "gused"), ("lpair", "h3l", "lused"))):
                            dve.wait_ge(sem[pair], k + 1)
                            dve.wait_ge(sem[h3], k + 1)
                            if k >= 2:
                                dve.wait_ge(sem["a"], k - 1)
                            go(used, dve.scalar_tensor_tensor(UL[:, k % 2, s, :], PS[:, 2 * s, :],
                                                              B0[:, k, 2 * s:2 * s + 1], H3[:, s, :], ALU.add, ALU.mult))
                        dve.wait_ge(sem["gused"], k + 1)
                        u = UL[:, k % 2, 0, :]
                        go("gg", dve.tensor_scalar(u, u, LIMIT, None, ALU.min))
                        dve.wait_ge(sem["lused"], k + 1)
                        v = UL[:, k % 2, 1, :]
                        go("lc", dve.tensor_scalar(v, v, LIMIT, -LIMIT, ALU.min, ALU.max))
                    if 1 <= k <= E + 1:
                        e = k - 1
                        th = TH[:, e % 2, :]
                        dve.wait_ge(sem["th"], e + 1)
                        dve.wait_ge(sem["lc"], e + 1)
                        if e >= 2:
                            dve.wait_ge(sem["y"], e - 1)
                        go("a", dve.scalar_tensor_tensor(AA[:, e % 2, :], UL[:, e % 2, 1, :], 1.0, th, ALU.add, ALU.mult))
                    tail0(i, k)
                dve.wait_ge(sem["acc"], E - 1)
                dve.wait_ge(sem["y"], E)
                for t in range(NT):
                    ins = dve.scalar_tensor_tensor(ACC[:, t, :], PS[:, 6 + (E - 1) % 2, 128 * t:128 * t + 128],
                                                   CW[:, t, E - 1:E], ACC[:, t, :], ALU.mult, ALU.add)
                step(i, ins)
                dve.wait_ge(sem["y"], E + 1)
                go("g", dve.scalar_tensor_tensor(ACC[:], ntok(PS[:, 6 + E % 2, :]), 1.0 / ALPHA, ACC[:],
                                                 ALU.mult, ALU.add))
                dve.wait_ge(sem["silu0"], 1)
                step(i, dve.scalar_tensor_tensor(ACC[:], ntok(TH[:, 0, :]), 1.0, ACC[:], ALU.add, ALU.mult))
                dve.wait_ge(sem["xb"], 1)
                step(i, dve.scalar_tensor_tensor(H[:], X1[:], 0.5, ACC[:], ALU.mult, ALU.mult))
                step(i, dve.tensor_tensor(H[:], H[:], XIN[:], ALU.add))
                dve.wait_ge(sem["ffn2"], 1)
                step(i, dve.scalar_tensor_tensor(ACC[:], ntok(PS[:, 4, :]), 0.5, ACC[:], ALU.mult, ALU.mult))
                go("layer0", dve.tensor_tensor(XA[:], ACC[:], H[:], ALU.add))
                dve.wait_ge(sem["layer0"], 1)

            def statistics_front(i):
                dve.wait_ge(x_loaded, 16 * (i + 2))
                statistics(i, XIN, "f_stats")

            def normalise_front(i):
                dve.wait_ge(sem["f_rstd"], 1)
                normalise(XN, XIN, RSTD, "f_xn")


            def window_scores(r):
                return WS[:, S_AT[r]:S_AT[r] + GRP[r] * WIN[r]].rearrange("p (n k) -> p n k", k=WIN[r])

            def window_max(i, r):
                w, lastw = WIN[r], (PADT // WIN[r] - 1) % NWIN[r]
                s = WS[96:128, S_AT[r] + lastw * w * w:S_AT[r] + (lastw + 1) * w * w]
                step(i, dve.tensor_tensor(s, s, MASK[r][96:128].rearrange("p q k -> p (q k)"), ALU.add))
                go(f"wmax{r}", dve.tensor_reduce(WM[r][:], window_scores(r), AX.X, ALU.max))

            def window_sum(i, r):
                dve.wait_ge(sem[f"wexp{r}"], 1)
                go(f"wsum{r}", dve.tensor_reduce(WM[r][:], window_scores(r), AX.X, ALU.add))
                dve.wait_ge(sem[f"wsum{r}"], 1)
                step(i, dve.reciprocal(WM[r][:], WM[r][:]))

            def window_out(i, r):
                dve.wait_ge(sem[f"wpv{r}"], 1)
                step(i, dve.tensor_reduce(WO[r][:], window_scores(r), AX.X, ALU.add))
                go(f"wout{r}", dve.tensor_tensor(WO[r][:], WO[r][:], WM[r][:], ALU.mult))

            def front(i, n):
                if n == 1:
                    dve.wait_ge(sem["down"], 1)
                    square = HT[:, 0:NT * 64].rearrange("p (t f) -> p t f", t=NT)
                    step(i, dve.tensor_tensor(XI[:], ntok(PS[:, 5, 0:256]), bc(DOWNB[:], [128, NT, 64], 1), ALU.add))
                    step(i, dve.tensor_tensor(square, XI[:], XI[:], ALU.mult))
                    go("xi_sq", dve.tensor_reduce(SQ[:], square, AX.X, ALU.add))
                    routing_logits(i, "f_", ntok(PS[:, 5, 256:256 + NT * E]))
                if n == 2:
                    dve.wait_ge(sem["f_rstd"], 2)
                    go("xi", dve.tensor_tensor(XI[:], XI[:], bc(RSTD[:], [128, NT, 64], 2), ALU.mult))
                if n == 3:
                    dve.wait_ge(sem["f_lexp"], 1)
                    routing_scores(i, True)
                    routing_pick(i, True, 0)
                if n == 4:
                    if i is not FIRST:
                        dve.wait_ge(sem["ys1"], E)
                    routing_pick(i, True, 1)
                    routing_weights(i, "cw0", 1.0 / ALPHA)
                if n in CHUNK_AT or n - 2 in CHUNK_AT:
                    if n == min(CHUNK_AT):
                        dve.wait_ge(sem["qkv_sb"], 2)
                        if i is not FIRST:
                            dve.wait_ge(sem["max_stacked0"], 16 * 4)
                            dve.wait_ge(sem["max_stacked1"], 16 * 4)
                    for c in range(*CHUNK_AT.get(n - 2, (0, 0))):
                        r, w, m = CHUNKS[c]
                        a = WIN[r] ** 2
                        dve.wait_ge(sem["S"], c + 1)
                        dst = WS[:, S_AT[r] + w * a:S_AT[r] + (w + m) * a].rearrange("p (w a) -> p w a", w=m)
                        src = PS[:, 4 + c % 2, 0:m * a].rearrange("p (w a) -> p w a", w=m)
                        bias = BIAS[r][:].rearrange("p q k -> p (q k)")
                        go("S_sb", dve.tensor_tensor(dst, src, bc(bias, [128, m, a], 1), ALU.add))
                        dve.wait_ge(sem["S_sb"], c + 1)
                    for c in range(*CHUNK_AT.get(n, (0, 0))):
                        r, w, m = CHUNKS[c]
                        q, kk = (QKV[r][:, j, :].rearrange("p (w q) -> p w q", q=WIN[r])[:, w:w + m] for j in range(2))
                        full = [128, m, WIN[r], WIN[r]]
                        if c >= 2:
                            dve.wait_ge(sem["S"], c - 1)
                        dst = G[:, c % 2, 0:m * WIN[r] ** 2].rearrange("p (w q k) -> p w q k", w=m, q=WIN[r])
                        go("prod", dve.tensor_tensor(dst, bc(q, full, 3), bc(kk, full, 2), ALU.mult))
                if n == 10:
                    window_max(i, 1)
                if n == 11:
                    window_max(i, 0)
                    dve.wait_ge(sem["wmax0"], 1)
                    s = window_scores(0)
                    go("wsub0", dve.tensor_tensor(s, s, bc(WM[0][:], [128, GRP[0], WIN[0]], 2), ALU.subtract))
                if n == WEXP_AT[0] + 1:
                    window_sum(i, 0)
                    s = window_scores(0).rearrange("p (w q) k -> p w q k", q=WIN[0])
                    v = QKV[0][:, 2, :].rearrange("p (w k) -> p w k", k=WIN[0])
                    go("wpv0", dve.tensor_tensor(s, s, bc(v, [128, NWIN[0], WIN[0], WIN[0]], 2), ALU.mult))
                    window_out(i, 0)
                if n == WEXP_AT[1] + 1:
                    window_sum(i, 1)
                if n == 18:
                    window_out(i, 1)

            def front_beside(i, n):
                if n == 0:
                    front(i, 1)
                front(i, n + AHEAD)

            def tail0(i, k):
                if k == 2:
                    dve.wait_ge(sem["up"], 1)
                    go("x1", dve.tensor_tensor(X1[:], ntok(PS[:, 5, :]), X1[:], ALU.add))
                if k == 4:
                    dve.wait_ge(sem["x1"], 1)
                    dve.wait_ge(sem["rstd0"], 1)
                    go("h0", dve.tensor_tensor(H[:], X1[:], bc(RSTD[:], [128, NT, 128], 2), ALU.mult))

            def chunk(i, c):
                m = FCH[c % NCH][1]
                th = TH[0:m, c % 2, :]
                dve.wait_ge(sem["fh3"], c + 1)
                dve.wait_ge(sem["fth"], c + 1)
                if c >= 4:
                    dve.wait_ge(sem["y1"], c - 3)
                go("fused", dve.tensor_tensor(A4[0:m, c % 4, :], PS[0:m, ff_bank(c, 1), :], th, ALU.mult))

            def row_max(i, h, half):
                dve.wait_ge(sem["mpair"], 2 * h + half + 1)
                go("mx", dve.tensor_reduce(MX[:, 2 * half:2 * half + 2, 8 * (h // 8) + 4 * (h % 2) + h // 2 % 4], PS[:, 2 * half:2 * half + 2, :], AX.X, ALU.max))

            def minus_maxima(i, which, bank):
                src = PS[0:8, bank, :]
                m2 = M2[which]
                dve.wait_ge(sem["mt"], which + 1)
                go("m2", dve.tensor_scalar(m2[:, 0, :].bitcast(F32R), src, -1.0, None, ALU.mult))
                dve.wait_ge(sem["m2"], 2 * which + 1)
                go("m2", dve.scalar_tensor_tensor(m2[:, 1, :].bitcast(F32R), src, -1.0, m2[:, 0, :],
                                                  ALU.mult, ALU.subtract))

            def layer1(i, last):
                statistics(i, XA, "stats")
                dve.wait_ge(sem["rstd"], 1)
                normalise(X1, XA, SCALES[:, 0], "xn")
                dve.wait_ge(sem["rstd"], 2)
                normalise(H, XA, SCALES[:, 1], "h")
                dve.wait_ge(sem["evac"], 2)
                go("xrh", dve.tensor_copy(XRH[:], HT[:]))
                dve.wait_ge(sem["xrh"], 1)
                go("xrh", dve.tensor_tensor(XRL[:], HT[:], XRH[:].bitcast(F32), ALU.subtract))
                routing_logits(i, "", ntok(PS[:, 6, 0:NT * E]))
                for n in range(2):
                    dve.wait_ge(sem["qln"], n + 1)
                    go("mag", dve.scalar_tensor_tensor(H3[:, n, :], PS[:, 2 + n, :], 0.0, AA[:, n, :], ALU.max, ALU.add))
                for n in range(2):
                    dve.wait_ge(sem["mag"], n + 1)
                    go("emb_cos", dve.tensor_tensor(EF[:, 2 * n, :], H3[:, n, :], TRIG[:, 2 * n, :], ALU.mult))
                for what, n in maxima_first(plan1()):
                    if what == "chunk":
                        chunk(i, n)
                        if n == 0:
                            dve.wait_ge(sem["emb_cos"], 2)
                            dve.wait_ge(sem["emb_sin"], 2)
                            go("hi", dve.tensor_copy(EH.bitcast(F32R), EF))
                        if n == 1:
                            dve.wait_ge(sem["hi"], 1)
                            go("lo", dve.tensor_tensor(EF, EF, EH, ALU.subtract))
                        if n == 2:
                            dve.wait_ge(sem["lexp"], 1)
                            routing_scores(i, False)
                            routing_pick(i, False, 0)
                        if n == 3:
                            routing_pick(i, False, 1)
                            routing_weights(i, "cw", 1.0)
                    elif what == "max":
                        if n == TURN_AT_MAX:
                            minus_maxima(i, 0, 0)
                        row_max(i, n // 2, n % 2)
                    elif n == NCH * FRONT_AFTER + NCH - 1 and not last:
                        statistics_front(i)
                    elif n == NCH * FRONT_AFTER + NCH + 1 and not last:
                        normalise_front(i)
                minus_maxima(i, 1, 7)
                if not last:
                    front(i, 0)
                for n in range(4 * NT + 2):
                    if not last:
                        front_beside(i, n)
                    if n in OUT_AT:
                        g = OUT_AT[n]
                        dve.wait_ge(sem["pv"], NT * (g + 1))
                        if g == 0:
                            dve.wait_ge(sem["y1"], E * NCH)
                        if g >= 2:
                            dve.wait_ge(sem["oq"], g - 1)
                        go("oe", dve.tensor_copy(A4[:, g % 2, :], PS[:, 7 - g % 2, :]))
                    if n in TURN_AT:
                        g = TURN_AT[n]
                        dve.wait_ge(sem["oq"], g + 1)
                        o = PS[:, 7 - g % 2, :].rearrange("p (t a r) -> p t a r", t=NT, a=4)
                        den = DEN[:, g, :].rearrange("p (t a) -> p t a", t=NT)
                        step(i, dve.reciprocal(den, o[:, :, :, HD1]))
                        dst = H[:].rearrange("p t (h d) -> p t h d", h=H1)[:, :, 4 * g:4 * g + 4]
                        go("ot", dve.tensor_tensor(dst, o[:, :, :, 0:HD1], bc(den, [128, NT, 4, HD1], 3), ALU.mult))
                dve.wait_ge(sem["silu"], 1)
                step(i, dve.scalar_tensor_tensor(ACC[:], ntok(G[:, 0, :]), 1.0, ACC[:], ALU.add, ALU.mult))
                dve.wait_ge(sem["wo"], 1)
                step(i, dve.scalar_tensor_tensor(ACC[:], ACC[:], 0.5, ntok(PS[:, 5, :]), ALU.mult, ALU.mult))
                go("out", dve.tensor_tensor(S0[:], ACC[:], XA[:], ALU.add))

            statistics_front(FIRST)
            normalise_front(FIRST)
            for n_front in range(FRONT):
                front(FIRST, n_front)
            for half in range(2):
                if half:
                    layer0(FIRST)
                dve.wait_ge(setup_act, 2 + half + 1)
                hi = W1H[:, 4 * half:4 * half + 4]
                init(dve.tensor_tensor(W1L[:, 4 * half:4 * half + 4], STAGE, hi.bitcast(F32), ALU.subtract))
            assert n[0] == SETUP_W
            end_pass(dve, FIRST)
            count[0] = 0
            with dve.Fori(0, B - 1) as i:
                layer1(i, False)
                layer0(i)
                end_pass(dve, i)
            count[0] = 0
            layer1(B - 1, True)
            end_pass(dve, B - 1, True)


def kernel(**inputs):
    import concourse.bacc as bacc
    from concourse.bass_utils import run_bass_kernel_spmd

    g = {n: np.asarray(v) for n, v in inputs.items()}
    dense = np.ascontiguousarray
    w1 = np.concatenate([g["L0_ffn_w1"], g["L0_ffn_sw1"][None]])
    w3 = np.concatenate([g["L0_ffn_w3"], g["L0_ffn_sw3"][None]])
    b1 = np.concatenate([g["L0_ffn_b1"], g["L0_ffn_sb1"][None]])
    b3 = np.concatenate([g["L0_ffn_b3"], g["L0_ffn_sb3"][None]])
    w0 = np.stack([w1[:, ::2], w3[:, ::2], w1[:, 1::2], w3[:, 1::2]], 1).transpose(3, 0, 1, 2)
    b0 = np.stack([b1[:, ::2], b3[:, ::2], b1[:, 1::2], b3[:, 1::2]], 1).transpose(2, 0, 1)
    w0d = np.concatenate([g["L0_ffn_w2"], g["L0_ffn_sw2"][None]]).transpose(2, 0, 1)
    order = np.array([(2 * j + par) * HD1 + d for par in range(2) for d in range(HD1) for j in range(8)])
    watt = np.stack([g["L1_attn_wq"].T[:, order], g["L1_attn_wk"].T[:, order],
                     g["L1_attn_wv"].T, g["L1_attn_wo"].T], 1)
    inv = np.float32(10000.0) ** (-(np.arange(HD1, dtype=np.float32) / np.float32(HD1)))
    freq = np.arange(T, dtype=np.float32)[None, :] * inv.astype(np.float32)[:, None]
    freq = freq[order % HD1].astype(np.float64)
    trig = np.stack([np.cos(freq), np.sin(freq)], 1).astype(np.float32)
    wqkv = np.zeros((64, 2, 96), np.float32)
    proj = np.zeros((128, 2, 4, 32), np.float32)
    for r in range(2):
        wqkv[32 * r:32 * r + 32, r] = g[f"L0_attn_qkv{r + 1}_w"]
        for n in range(4):
            proj[32 * n:32 * n + 32, r, n] = g[f"L0_attn_proj{r + 1}_w"]
    qkvb = np.tile(np.stack([g[f"L0_attn_qkv{r + 1}_b"].reshape(3, 32).T for r in range(2)], 1), (4, 1, 1))
    arrays = {
        "x": g["L0_attn_x"].reshape(B * T, D),
        "ident": np.eye(128, dtype=np.float32),
        "headsum": np.kron(np.eye(32, dtype=np.float32), np.ones((4, 4), np.float32)),
        "rev": np.tile(np.arange(E, 0, -1, dtype=np.float32), (128, 1)),
        "trig": trig, "w0": w0, "b0": b0, "w0d": w0d, "watt": watt,
        "rpb1": np.tile(np.repeat(g["L0_attn_rpb1"][::-1].T, 4, 0), (4, 1)),
        "rpb2": np.tile(np.repeat(g["L0_attn_rpb2"][::-1].T, 4, 0), (4, 1)),
        "wqkv": wqkv, "proj": proj, "qkvb": qkvb,
        "projb": np.concatenate([g["L0_attn_proj1_b"], g["L0_attn_proj2_b"]])[:, None],
        "gate_w": g["L0_ffn_gate_w"].T, "gate_b": g["L0_ffn_gate_b"], "b2": g["L0_ffn_b2"], "sb2": g["L0_ffn_sb2"],
        "pope_bias": g["L1_attn_pope_bias"].reshape(FIRST)[order],
        "ln_weight": g["L1_ffn_ln_weight"], "router_w": g["L1_ffn_router_w"],
        "w1": g["L1_ffn_w1"], "w3": g["L1_ffn_w3"], "w2": g["L1_ffn_w2"],
    }
    for n in ("down_w", "down_b", "up_w", "up_b", "norm1_w", "norm2_w", "ffn_w1", "ffn_b1", "ffn_w2", "ffn_b2"):
        arrays[n] = g[f"L0_attn_{n}"]
    for n, width in (("ffn_b1", 2), ("norm1_w", 1), ("norm2_w", 1), ("pope_bias", 1), ("ln_weight", 1)):
        arrays[n] = arrays[n].reshape(width, FIRST).T
    nc = bacc.Bacc("TRN2", target_bir_lowering=False, num_devices=1)
    ins, aps = {}, {}
    for n, a in arrays.items():
        ins[f"in_{n}"] = dense(a)
        aps[n] = nc.dram_tensor(f"in_{n}", a.shape, mybir.dt.from_np(a.dtype), kind="ExternalInput").ap()
    aps["y"] = nc.dram_tensor("out_y", (B * T, D), F32, kind="ExternalOutput").ap()
    build(nc, aps)
    r = run_bass_kernel_spmd(nc, [ins], core_ids=[0])
    return r.results[0]["out_y"].reshape(B, T, D)
```
